# Optimizing a Trainium2 kernel written in Bass

```python
import numpy as np
import jax
import jax.numpy as jnp

def _softmax(x, axis=-1):
    return jax.nn.softmax(x, axis=axis)

def _gelu(x):
    return jax.nn.gelu(x, approximate=True)

def _silu(x):
    return jax.nn.silu(x)

def _sigmoid(x):
    return jax.nn.sigmoid(x)

def _layernorm(x, axis=-1, eps=1e-05):
    m = jnp.mean(x, axis=axis, keepdims=True)
    v = jnp.var(x, axis=axis, keepdims=True)
    return (x - m) / jnp.sqrt(v + eps)

def _scatter_add(tgt, idx, src, axis=0):
    return tgt.at[idx].add(src)

def _segment_sum(src, seg, n):
    return jax.ops.segment_sum(src, seg, n)
kernel_name = 'mk_decoder_preln_d2_seqx_r4_68d6b5'

def setup_inputs(seed: int=0):
    np.random.seed(seed)
    _w = jnp.asarray

    def _rec_inputs():
        import jax
        import jax.numpy as jnp
        _rk = jax.random.key(seed)
        x = 7.22e-05 + 1 * jax.random.normal(jax.random.fold_in(_rk, 1), (16, 256, 256), jnp.float32)
        _lenS = 256 - jax.random.randint(jax.random.fold_in(_rk, 7), (16,), 0, max(1, 256 // 4) + 1, jnp.int32)
        _lenS2 = 77 - jax.random.randint(jax.random.fold_in(_rk, 8), (16,), 0, max(1, 77 // 4) + 1, jnp.int32)
        _ctx_1024P = jax.random.normal(jax.random.fold_in(_rk, 11), (16, 16, 256), jnp.float32)
        _ctx_1024c = jax.random.dirichlet(jax.random.fold_in(_rk, 511), 0.3 * jnp.ones((16,), jnp.float32), (16, 77))
        _ctx_1024t = jnp.einsum('bsk,bkd->bsd', _ctx_1024c, _ctx_1024P)
        _ctx_1024t = _ctx_1024t * jax.lax.rsqrt(jnp.mean(jnp.square(_ctx_1024t)) + 1e-12) * 0.953939
        ctx_1024 = 4.13588e-05 + 0.999923 * (_ctx_1024t + 0.3 * jax.random.normal(jax.random.fold_in(_rk, 611), (16, 77, 256), jnp.float32))
        _validS = jnp.arange(256)[None, :] < _lenS[:, None]
        _validS2 = jnp.arange(77)[None, :] < _lenS2[:, None]
        _causal = jnp.tril(jnp.ones((256, 256), dtype=bool))
        mask_1x1xSxS2_if1 = jnp.where(jnp.ones((1, 1, 256, 77), dtype=bool), 1, 0).astype(jnp.int32)
        return (x, ctx_1024, mask_1x1xSxS2_if1)
    x, ctx_1024, mask_1x1xSxS2_if1 = _rec_inputs()

    def _L0_attn_setup():
        import jax, jax.numpy as jnp
        import numpy as np
        import math
        T = 0.28
        EPS = 1e-06
        D_MODEL = 256
        N_HEADS = 16
        D_K = D_MODEL // N_HEADS

        def compute_radius(t, epsilon):
            raw = math.sqrt(4.0 * t * math.log(1.0 / epsilon))
            return max(int(math.ceil(raw * 2.0)), 1)
        RADIUS = compute_radius(T, EPS)
        WIN = RADIUS + 1
        key = jax.random.key(seed)
        ks = jax.random.split(key, 5)
        B, S = (2, 1024)
        x = jax.random.normal(ks[0], (B, S, D_MODEL), dtype=jnp.float32)
        scale = 1.0 / math.sqrt(D_MODEL)
        Wq = jax.random.normal(ks[1], (D_MODEL, D_MODEL), dtype=jnp.float32) * scale
        Wk = jax.random.normal(ks[2], (D_MODEL, D_MODEL), dtype=jnp.float32) * scale
        Wv = jax.random.normal(ks[3], (D_MODEL, D_MODEL), dtype=jnp.float32) * scale
        Wo = jax.random.normal(ks[4], (D_MODEL, D_MODEL), dtype=jnp.float32) * scale
        return {'x': x, 'Wq': Wq, 'Wk': Wk, 'Wv': Wv, 'Wo': Wo}
    _L0_attn_all = _L0_attn_setup()
    _L0_attn_in = {k: v for k, v in _L0_attn_all.items() if k in ('Wq', 'Wk', 'Wv', 'Wo')}
    del _L0_attn_all

    def _L0_xattn_setup():
        import math
        import jax, jax.numpy as jnp
        import numpy as np
        EMBED_DIM = 256
        N_HEADS = 16
        B = 4
        L = 512
        key = jax.random.key(seed)
        ks = jax.random.split(key, 12)
        s = 1.0 / math.sqrt(EMBED_DIM)
        inp = {'q': jax.random.normal(ks[0], (B, L, EMBED_DIM), jnp.float32), 'k': jax.random.normal(ks[1], (B, L, EMBED_DIM), jnp.float32), 'v': jax.random.normal(ks[2], (B, L, EMBED_DIM), jnp.float32), 'mask': jnp.ones((1, 1, L, L), jnp.int32), 'Wq': jax.random.normal(ks[3], (EMBED_DIM, EMBED_DIM), jnp.float32) * s, 'bq': jnp.zeros((EMBED_DIM,), jnp.float32), 'Wk': jax.random.normal(ks[4], (EMBED_DIM, EMBED_DIM), jnp.float32) * s, 'bk': jnp.zeros((EMBED_DIM,), jnp.float32), 'Wv': jax.random.normal(ks[5], (EMBED_DIM, EMBED_DIM), jnp.float32) * s, 'bv': jnp.zeros((EMBED_DIM,), jnp.float32), 'Wo': jax.random.normal(ks[6], (EMBED_DIM, EMBED_DIM), jnp.float32) * s, 'bo': jnp.zeros((EMBED_DIM,), jnp.float32)}
        return inp
    _L0_xattn_all = _L0_xattn_setup()
    _L0_xattn_in = {k: v for k, v in _L0_xattn_all.items() if k in ('Wq', 'bq', 'Wk', 'bk', 'Wv', 'bv', 'Wo', 'bo')}
    del _L0_xattn_all

    def _L0_ffn_setup():
        import jax, jax.numpy as jnp
        import numpy as np
        IN_F = 256
        OUT_F = 256
        B, S = (8, 1024)

        def _pack_ternary(tern):
            enc = (tern + 1.0).astype(jnp.int32).reshape(-1)
            return (enc[0::4] | enc[1::4] << 2 | enc[2::4] << 4 | enc[3::4] << 6).astype(jnp.int32)
        key = jax.random.key(seed)
        kx, kw = jax.random.split(key)
        x = jax.random.normal(kx, (B, S, IN_F), dtype=jnp.float32)
        w = jax.random.normal(kw, (OUT_F, IN_F), dtype=jnp.float32) * 0.02
        scale = jnp.maximum(jnp.mean(jnp.abs(w)), 1e-05)
        wn = w / scale
        tern = jnp.sign(wn) * (jnp.abs(wn) > 0.5).astype(jnp.float32)
        packed = _pack_ternary(tern)
        bias = jnp.zeros((OUT_F,), dtype=jnp.float32)
        return {'x': x, 'packed_weight': packed, 'weight_scale': scale.reshape(1), 'bias': bias}
    _L0_ffn_all = _L0_ffn_setup()
    _L0_ffn_in = {k: v for k, v in _L0_ffn_all.items() if k in ('packed_weight', 'weight_scale', 'bias')}
    del _L0_ffn_all

    def _L1_attn_setup():
        import jax, jax.numpy as jnp
        import numpy as np
        D_MODEL = 256
        N_HEADS = 16
        DH = D_MODEL // N_HEADS
        B, T = (4, 512)
        ROPE_BASE = 10000.0
        EPS = 1e-06

        def _rope(q, k, base=ROPE_BASE):
            half = q.shape[-1] // 2
            freqs = jnp.arange(half, dtype=q.dtype)
            inv_freq = base ** (-freqs / half)
            pos = jnp.arange(q.shape[2], dtype=q.dtype)
            ang = pos[:, None] * inv_freq[None, :]
            c = jnp.cos(ang)[None, None]
            s = jnp.sin(ang)[None, None]

            def rot(x):
                x1 = x[..., :half]
                x2 = x[..., half:2 * half]
                return jnp.concatenate([x1 * c - x2 * s, x1 * s + x2 * c], axis=-1)
            return (rot(q), rot(k))

        def _phi(x):
            return jax.nn.elu(x) + 1.0

        def _forward(x, Wq, Wk, Wv, Wo):
            Bx, Tx, D = x.shape
            H, dh = (N_HEADS, D // N_HEADS)
            q = (x @ Wq.T).reshape(Bx, Tx, H, dh).transpose(0, 2, 1, 3)
            k = (x @ Wk.T).reshape(Bx, Tx, H, dh).transpose(0, 2, 1, 3)
            v = (x @ Wv.T).reshape(Bx, Tx, H, dh).transpose(0, 2, 1, 3)
            q, k = _rope(q, k)
            q = _phi(q)
            k = _phi(k)
            qT = q.transpose(2, 0, 1, 3)
            kT = k.transpose(2, 0, 1, 3)
            vT = v.transpose(2, 0, 1, 3)

            def step(carry, qkv):
                K_sum, KV = carry
                q_t, k_t, v_t = qkv
                K_sum = K_sum + k_t
                KV = KV + k_t[..., :, None] * v_t[..., None, :]
                num = jnp.einsum('bhd,bhde->bhe', q_t, KV)
                den = jnp.maximum(jnp.einsum('bhd,bhd->bh', q_t, K_sum), EPS)
                return ((K_sum, KV), num / den[..., None])
            init = (jnp.zeros((Bx, H, dh), x.dtype), jnp.zeros((Bx, H, dh, dh), x.dtype))
            _, Y = jax.lax.scan(step, init, (qT, kT, vT))
            Y = Y.transpose(1, 0, 2, 3).reshape(Bx, Tx, D)
            return Y @ Wo.T
        key = jax.random.key(seed)
        kx, kq, kk, kv, ko = jax.random.split(key, 5)
        scale = 0.02
        return {'x': jax.random.normal(kx, (B, T, D_MODEL), jnp.float32), 'Wq': jax.random.normal(kq, (D_MODEL, D_MODEL), jnp.float32) * scale, 'Wk': jax.random.normal(kk, (D_MODEL, D_MODEL), jnp.float32) * scale, 'Wv': jax.random.normal(kv, (D_MODEL, D_MODEL), jnp.float32) * scale, 'Wo': jax.random.normal(ko, (D_MODEL, D_MODEL), jnp.float32) * scale}
    _L1_attn_all = _L1_attn_setup()
    _L1_attn_in = {k: v for k, v in _L1_attn_all.items() if k in ('Wq', 'Wk', 'Wv', 'Wo')}
    del _L1_attn_all

    def _L1_xattn_setup():
        import jax, jax.numpy as jnp
        import numpy as np
        EMBED_DIM = 256
        NUM_HEADS = 16
        HEAD_DIM = EMBED_DIM // NUM_HEADS
        key = jax.random.key(seed)
        ks = jax.random.split(key, 11)
        s = 1.0 / np.sqrt(EMBED_DIM)
        inp = {'query': jax.random.normal(ks[0], (4, 512, EMBED_DIM), jnp.float32), 'key': jax.random.normal(ks[1], (4, 512, EMBED_DIM), jnp.float32), 'value': jax.random.normal(ks[2], (4, 512, EMBED_DIM), jnp.float32), 'Wq': jax.random.uniform(ks[3], (EMBED_DIM, EMBED_DIM), jnp.float32, -s, s), 'bq': jax.random.uniform(ks[4], (EMBED_DIM,), jnp.float32, -s, s), 'Wk': jax.random.uniform(ks[5], (EMBED_DIM, EMBED_DIM), jnp.float32, -s, s), 'bk': jax.random.uniform(ks[6], (EMBED_DIM,), jnp.float32, -s, s), 'Wv': jax.random.uniform(ks[7], (EMBED_DIM, EMBED_DIM), jnp.float32, -s, s), 'bv': jax.random.uniform(ks[8], (EMBED_DIM,), jnp.float32, -s, s), 'Wo': jax.random.uniform(ks[9], (EMBED_DIM, EMBED_DIM), jnp.float32, -s, s), 'bo': jax.random.uniform(ks[10], (EMBED_DIM,), jnp.float32, -s, s)}
        return inp
    _L1_xattn_all = _L1_xattn_setup()
    _L1_xattn_in = {k: v for k, v in _L1_xattn_all.items() if k in ('Wq', 'bq', 'Wk', 'bk', 'Wv', 'bv', 'Wo', 'bo')}
    del _L1_xattn_all

    def _L1_ffn_setup():
        import jax, jax.numpy as jnp
        import numpy as np
        E, H, I, K = (8, 256, 512, 2)
        B, S = (4, 512)
        key = jax.random.key(seed)
        k1, k2, k3, k4 = jax.random.split(key, 4)
        x = jax.random.normal(k1, (B, S, H), dtype=jnp.float32)
        router_w = jax.random.uniform(k2, (E, H), dtype=jnp.float32, minval=-1.0, maxval=1.0) / np.sqrt(H).astype(np.float32)
        w13 = jax.random.normal(k3, (E, H, 2 * I), dtype=jnp.float32) * 0.02
        w2 = jax.random.normal(k4, (E, I, H), dtype=jnp.float32) * 0.02
        return {'x': x, 'router_w': router_w, 'w13': w13, 'w2': w2}
    _L1_ffn_all = _L1_ffn_setup()
    _L1_ffn_in = {k: v for k, v in _L1_ffn_all.items() if k in ('router_w', 'w13', 'w2')}
    del _L1_ffn_all
    return {'x': x, 'ctx_1024': ctx_1024, 'mask_1x1xSxS2_if1': mask_1x1xSxS2_if1, 'L0_attn_Wq': _L0_attn_in['Wq'], 'L0_attn_Wk': _L0_attn_in['Wk'], 'L0_attn_Wv': _L0_attn_in['Wv'], 'L0_attn_Wo': _L0_attn_in['Wo'], 'L0_xattn_Wq': _L0_xattn_in['Wq'], 'L0_xattn_bq': _L0_xattn_in['bq'], 'L0_xattn_Wk': _L0_xattn_in['Wk'], 'L0_xattn_bk': _L0_xattn_in['bk'], 'L0_xattn_Wv': _L0_xattn_in['Wv'], 'L0_xattn_bv': _L0_xattn_in['bv'], 'L0_xattn_Wo': _L0_xattn_in['Wo'], 'L0_xattn_bo': _L0_xattn_in['bo'], 'L0_ffn_packed_weight': _L0_ffn_in['packed_weight'], 'L0_ffn_weight_scale': _L0_ffn_in['weight_scale'], 'L0_ffn_bias': _L0_ffn_in['bias'], 'L1_attn_Wq': _L1_attn_in['Wq'], 'L1_attn_Wk': _L1_attn_in['Wk'], 'L1_attn_Wv': _L1_attn_in['Wv'], 'L1_attn_Wo': _L1_attn_in['Wo'], 'L1_xattn_Wq': _L1_xattn_in['Wq'], 'L1_xattn_bq': _L1_xattn_in['bq'], 'L1_xattn_Wk': _L1_xattn_in['Wk'], 'L1_xattn_bk': _L1_xattn_in['bk'], 'L1_xattn_Wv': _L1_xattn_in['Wv'], 'L1_xattn_bv': _L1_xattn_in['bv'], 'L1_xattn_Wo': _L1_xattn_in['Wo'], 'L1_xattn_bo': _L1_xattn_in['bo'], 'L1_ffn_router_w': _L1_ffn_in['router_w'], 'L1_ffn_w13': _L1_ffn_in['w13'], 'L1_ffn_w2': _L1_ffn_in['w2']}

def reference(x, ctx_1024, mask_1x1xSxS2_if1, L0_attn_Wq, L0_attn_Wk, L0_attn_Wv, L0_attn_Wo, L0_xattn_Wq, L0_xattn_bq, L0_xattn_Wk, L0_xattn_bk, L0_xattn_Wv, L0_xattn_bv, L0_xattn_Wo, L0_xattn_bo, L0_ffn_packed_weight, L0_ffn_weight_scale, L0_ffn_bias, L1_attn_Wq, L1_attn_Wk, L1_attn_Wv, L1_attn_Wo, L1_xattn_Wq, L1_xattn_bq, L1_xattn_Wk, L1_xattn_bk, L1_xattn_Wv, L1_xattn_bv, L1_xattn_Wo, L1_xattn_bo, L1_ffn_router_w, L1_ffn_w13, L1_ffn_w2):
    import jax
    import jax.numpy as jnp

    def _L0_attn_ref(x, Wq, Wk, Wv, Wo):
        import jax, jax.numpy as jnp
        import numpy as np
        import math
        T = 0.28
        EPS = 1e-06
        D_MODEL = 256
        N_HEADS = 16
        D_K = D_MODEL // N_HEADS

        def compute_radius(t, epsilon):
            raw = math.sqrt(4.0 * t * math.log(1.0 / epsilon))
            return max(int(math.ceil(raw * 2.0)), 1)
        RADIUS = compute_radius(T, EPS)
        WIN = RADIUS + 1
        B, S, _ = x.shape

        def split_heads(h):
            return h.reshape(B, S, N_HEADS, D_K).transpose(0, 2, 1, 3)
        q = split_heads(x @ Wq)
        k = split_heads(x @ Wk)
        v = split_heads(x @ Wv)
        pos = jnp.arange(S)
        idx = pos[:, None] + jnp.arange(-RADIUS, 1)[None, :]
        valid = idx >= 0
        idx_c = jnp.clip(idx, 0, S - 1)
        k_win = k[:, :, idx_c, :]
        v_win = v[:, :, idx_c, :]
        scores = jnp.einsum('bhsd,bhswd->bhsw', q, k_win) / (2.0 * T)
        scores = jnp.where(valid[None, None, :, :], scores, -jnp.inf)
        wts = jax.nn.softmax(scores, axis=-1)
        wts = jnp.nan_to_num(wts, nan=0.0)
        attn = jnp.einsum('bhsw,bhswd->bhsd', wts, v_win)
        attn = attn.transpose(0, 2, 1, 3).reshape(B, S, D_MODEL)
        return attn @ Wo

    def _L0_xattn_ref(q, k, v, mask, Wq, bq, Wk, bk, Wv, bv, Wo, bo):
        import math
        import jax, jax.numpy as jnp
        import numpy as np
        EMBED_DIM = 256
        N_HEADS = 16
        B = 4
        L = 512
        Bq, Lq, C = q.shape
        Bk, Lk, _ = k.shape
        H = N_HEADS
        hd = C // H
        qp = q @ Wq + bq
        kp = k @ Wk + bk
        vp = v @ Wv + bv
        qh = qp.reshape(Bq, Lq, H, hd).transpose(0, 2, 1, 3)
        kh = kp.reshape(Bk, Lk, H, hd).transpose(0, 2, 1, 3)
        vh = vp.reshape(Bk, Lk, H, hd).transpose(0, 2, 1, 3)
        scores = jnp.einsum('bhqd,bhkd->bhqk', qh, kh) / math.sqrt(hd)
        scores = jnp.where(mask == 0, jnp.float32(-10000000000.0), scores)
        attn = jax.nn.softmax(scores, axis=-1)
        x = jnp.einsum('bhqk,bhkd->bhqd', attn, vh)
        x = x.transpose(0, 2, 1, 3).reshape(Bq, Lq, C)
        return x @ Wo + bo

    def _L0_ffn_ref(x, packed_weight, weight_scale, bias):
        import jax, jax.numpy as jnp
        import numpy as np
        IN_F = 256
        OUT_F = 256
        B, S = (8, 1024)

        def _pack_ternary(tern):
            enc = (tern + 1.0).astype(jnp.int32).reshape(-1)
            return (enc[0::4] | enc[1::4] << 2 | enc[2::4] << 4 | enc[3::4] << 6).astype(jnp.int32)
        n = OUT_F * IN_F
        shifts = jnp.array([0, 2, 4, 6], dtype=jnp.int32)
        enc = (packed_weight[None, :] >> shifts[:, None] & 3).reshape(-1)[:n]
        w = (enc.astype(jnp.float32) - 1.0).reshape(OUT_F, IN_F) * weight_scale
        act_scale = 127.0 / jnp.maximum(jnp.max(jnp.abs(x), axis=-1, keepdims=True), 1e-05)
        x_dq = jnp.clip(jnp.round(x * act_scale), -128.0, 127.0) / act_scale
        return jnp.einsum('bsi,oi->bso', x_dq, w) + bias

    def _L1_attn_ref(x, Wq, Wk, Wv, Wo):
        import jax, jax.numpy as jnp
        import numpy as np
        D_MODEL = 256
        N_HEADS = 16
        DH = D_MODEL // N_HEADS
        B, T = (4, 512)
        ROPE_BASE = 10000.0
        EPS = 1e-06

        def _rope(q, k, base=ROPE_BASE):
            half = q.shape[-1] // 2
            freqs = jnp.arange(half, dtype=q.dtype)
            inv_freq = base ** (-freqs / half)
            pos = jnp.arange(q.shape[2], dtype=q.dtype)
            ang = pos[:, None] * inv_freq[None, :]
            c = jnp.cos(ang)[None, None]
            s = jnp.sin(ang)[None, None]

            def rot(x):
                x1 = x[..., :half]
                x2 = x[..., half:2 * half]
                return jnp.concatenate([x1 * c - x2 * s, x1 * s + x2 * c], axis=-1)
            return (rot(q), rot(k))

        def _phi(x):
            return jax.nn.elu(x) + 1.0

        def _forward(x, Wq, Wk, Wv, Wo):
            Bx, Tx, D = x.shape
            H, dh = (N_HEADS, D // N_HEADS)
            q = (x @ Wq.T).reshape(Bx, Tx, H, dh).transpose(0, 2, 1, 3)
            k = (x @ Wk.T).reshape(Bx, Tx, H, dh).transpose(0, 2, 1, 3)
            v = (x @ Wv.T).reshape(Bx, Tx, H, dh).transpose(0, 2, 1, 3)
            q, k = _rope(q, k)
            q = _phi(q)
            k = _phi(k)
            qT = q.transpose(2, 0, 1, 3)
            kT = k.transpose(2, 0, 1, 3)
            vT = v.transpose(2, 0, 1, 3)

            def step(carry, qkv):
                K_sum, KV = carry
                q_t, k_t, v_t = qkv
                K_sum = K_sum + k_t
                KV = KV + k_t[..., :, None] * v_t[..., None, :]
                num = jnp.einsum('bhd,bhde->bhe', q_t, KV)
                den = jnp.maximum(jnp.einsum('bhd,bhd->bh', q_t, K_sum), EPS)
                return ((K_sum, KV), num / den[..., None])
            init = (jnp.zeros((Bx, H, dh), x.dtype), jnp.zeros((Bx, H, dh, dh), x.dtype))
            _, Y = jax.lax.scan(step, init, (qT, kT, vT))
            Y = Y.transpose(1, 0, 2, 3).reshape(Bx, Tx, D)
            return Y @ Wo.T
        return _forward(x, Wq, Wk, Wv, Wo)

    def _L1_xattn_ref(query, key, value, Wq, bq, Wk, bk, Wv, bv, Wo, bo):
        import jax, jax.numpy as jnp
        import numpy as np
        EMBED_DIM = 256
        NUM_HEADS = 16
        HEAD_DIM = EMBED_DIM // NUM_HEADS
        B, T, E = query.shape
        S = key.shape[1]
        H, D = (NUM_HEADS, HEAD_DIM)
        q = (query @ Wq.T + bq).reshape(B, T, H, D).transpose(0, 2, 1, 3)
        k = (key @ Wk.T + bk).reshape(B, S, H, D).transpose(0, 2, 1, 3)
        v = (value @ Wv.T + bv).reshape(B, S, H, D).transpose(0, 2, 1, 3)
        scores = jnp.einsum('bhtd,bhsd->bhts', q, k) / np.sqrt(D)
        causal = jnp.triu(jnp.full((T, S), -jnp.inf, jnp.float32), k=1)
        scores = scores + causal[None, None]
        attn = jax.nn.softmax(scores, axis=-1)
        out = jnp.einsum('bhts,bhsd->bhtd', attn, v)
        out = out.transpose(0, 2, 1, 3).reshape(B, T, E)
        out = out @ Wo.T + bo
        return out

    def _L1_ffn_ref(x, router_w, w13, w2):
        import jax, jax.numpy as jnp
        import numpy as np
        E, H, I, K = (8, 256, 512, 2)
        B, S = (4, 512)
        logits = jnp.einsum('bsh,eh->bse', x, router_w)
        probs = jax.nn.softmax(logits, axis=-1)
        weights, indices = jax.lax.top_k(probs, K)
        weights = weights / (weights.sum(axis=-1, keepdims=True) + 1e-06)
        h13 = jnp.einsum('bsh,ehi->bsei', x, w13)
        gate, up = jnp.split(h13, 2, axis=-1)
        h = jax.nn.silu(gate) * up
        y = jnp.einsum('bsei,eih->bseh', h, w2)
        y_sel = jnp.take_along_axis(y, indices[..., None], axis=2)
        return (y_sel * weights[..., None]).sum(axis=2)
    x = x + _L0_attn_ref(_layernorm(x, axis=-1), L0_attn_Wq, L0_attn_Wk, L0_attn_Wv, L0_attn_Wo)
    x = x + _L0_xattn_ref(_layernorm(x, axis=-1), ctx_1024, ctx_1024, mask_1x1xSxS2_if1, L0_xattn_Wq, L0_xattn_bq, L0_xattn_Wk, L0_xattn_bk, L0_xattn_Wv, L0_xattn_bv, L0_xattn_Wo, L0_xattn_bo)
    x = x + _L0_ffn_ref(_layernorm(x, axis=-1), L0_ffn_packed_weight, L0_ffn_weight_scale, L0_ffn_bias)
    x = x + _L1_attn_ref(_layernorm(x, axis=-1), L1_attn_Wq, L1_attn_Wk, L1_attn_Wv, L1_attn_Wo)
    x = x + _L1_xattn_ref(_layernorm(x, axis=-1), ctx_1024, ctx_1024, L1_xattn_Wq, L1_xattn_bq, L1_xattn_Wk, L1_xattn_bk, L1_xattn_Wv, L1_xattn_bv, L1_xattn_Wo, L1_xattn_bo)
    x = x + _L1_ffn_ref(_layernorm(x, axis=-1), L1_ffn_router_w, L1_ffn_w13, L1_ffn_w2)
    return x

_drawn_inputs = setup_inputs


def setup_inputs(seed=0):
    import zlib

    import numpy as np

    out = dict(_drawn_inputs(seed))
    spreads = {'L0_xattn_bq': (0.0, 0.476),
     'L0_xattn_bk': (0.0, 2.0),
     'L0_xattn_bv': (0.0, 0.1),
     'L0_xattn_bo': (0.0, 0.1),
     'L0_ffn_bias': (0.0, 0.1)}
    factors = {'L1_attn_Wq': 30.401,
     'L1_attn_Wk': 8.0,
     'L1_xattn_Wq': 3.554,
     'L1_xattn_bq': 8.0,
     'L1_xattn_Wk': 3.543,
     'L1_xattn_bk': 64.0,
     'L1_xattn_bv': 4.204,
     'L1_ffn_router_w': 5.6,
     'L1_ffn_w13': 4.852,
     'L1_ffn_w2': 4.841}
    for name, (base, spread) in spreads.items():
        noise = np.random.default_rng([zlib.crc32(name.encode()), seed]).standard_normal(out[name].shape)
        drawn = base * np.exp(spread * noise) if base else spread * noise
        out[name] = jnp.asarray(drawn.astype(out[name].dtype))
    for name, factor in factors.items():
        out[name] = (out[name] * factor).astype(out[name].dtype)
    return out
```

```python
from contextlib import ExitStack

import numpy as np

import concourse.bass as bass
from concourse import mybir

F32 = mybir.dt.float32
BF16 = mybir.dt.bfloat16
I32 = mybir.dt.int32
ALU = mybir.AluOpType
ACT = mybir.ActivationFunctionType
AX_X = mybir.AxisListType.X

P = 128
B, S, D = 16, 256, 256
SC = 77
H, DH = 16, 16
KD = D // P
TB = S // P
NT = B * TB
HS = H * SC
LANES = 2
ITERS = B // LANES
EPS_LN = 1e-5

RADIUS = 8
WIN = 32
WQ = WIN - RADIUS
NW = -(-S // WQ)
SPAD = RADIUS + NW * WQ
L0_SCALE = 1.0 / (2.0 * 0.28)
HG = 4
NG = H // HG
NU = NW * NG

NC_CH = -(-HS // P)
CREP = SC + P
VH = 3
DV = DH + 1

CK = 64
NCK = S // CK
NPAIR = H // 2

E, FF = 8, 512
NJ = (2 * B * S) // P + E
CAP = B * S + P
NEG = -1.0e38
BIG = 3.0e38
MAGIC = 12582912.0

(W0Q, W0K, W0V, W0O, X0Q, X0K, X0V, X0O, W1Q, W1K, W1V, W1O, X1Q, X1K, X1V, X1O) = range(16)
NM = 16


def chunk_heads(c):
    return P * c // SC, min(P, HS - P * c)


def shape_tables():
    p = np.arange(P)
    t = {}
    t["ident"] = np.eye(P, dtype=np.float32)
    t["hm4"] = (p[:, None] // DH % HG == np.arange(HG)).astype(np.float32)
    t["hm8"] = (p[:, None] // DH == np.arange(8)).astype(np.float32)
    t["hm2"] = (p[:, None] // DH % 2 == np.arange(2)).astype(np.float32)
    t["rm4"] = (p[:, None] // WIN == np.arange(HG)).astype(np.float32)
    t["rm2"] = (p[:, None] // CK == np.arange(2)).astype(np.float32)
    q, k = (p % WIN)[:, None], np.arange(WIN)[None, :]
    seen = (k <= q) & (k >= q - RADIUS)
    t["band"] = np.where(seen, BIG, NEG).astype(np.float32)
    t["band0"] = np.where(seen & (k >= RADIUS), BIG, NEG).astype(np.float32)
    tok = p[:, None] + P * np.arange(TB)[None, :]
    t["caus"] = np.where(np.arange(SC) <= tok[:, :, None], BIG, NEG).astype(np.float32).reshape(P, -1)
    t["tri"] = ((p % CK)[:, None] <= np.arange(CK)).astype(np.float32)
    vm = np.zeros((P, NC_CH, VH), np.float32)
    for c in range(NC_CH):
        h0, rows = chunk_heads(c)
        head = (P * c + p) // SC
        vm[:, c] = (head[:, None] == h0 + np.arange(VH)) & (p < rows)[:, None]
    t["vmask"] = vm.reshape(P, -1)
    half = DH // 2
    inv = (np.float32(10000.0) ** (-np.arange(half, dtype=np.float32) / np.float32(half))).astype(np.float32)
    ang = (tok.astype(np.float32)[:, :, None] * inv).astype(np.float32)
    c, s = np.cos(ang).astype(np.float32), np.sin(ang).astype(np.float32)
    t["rope"] = np.concatenate([c, -s, s], axis=-1).reshape(P, -1)
    t["power"] = np.full((P, TB), -0.5, np.float32)
    t["ones"] = np.ones((P, P), np.float32)
    t["before"] = (p[:, None] < p[None, :]).astype(np.float32)
    t["desc"] = np.tile(np.arange(E, 0, -1, dtype=np.float32), (P, 1))
    t["row"] = p[:, None].astype(np.float32)
    t["expert"] = np.tile(np.arange(E, dtype=np.float32), (P, 1))
    t["first_row"] = np.tile(CAP * np.arange(E, dtype=np.float32), (P, 1))
    t["tiles"] = np.tile(np.arange(NJ, dtype=np.float32), (P, 1))
    return t


TABLES = {n: a.shape[1] for n, a in shape_tables().items()}
TAB_AT, _n = {}, 0
for _k, _w in TABLES.items():
    TAB_AT[_k] = _n
    _n += _w
TAB_W = _n

SIGNALS = {
    "x_in": 16,
    "ctx_in": 48,
    "ck_ps": 1,
    "ck_sb": 1,
    "kbd": 4,
    "cv_ps": 2,
    "cv_sb": 2,
    "var": 6,
    "var_eps": 6,
    "rstd": 6,
    "norm": 6,
    "hT_ps": 6,
    "hT": 6,
    "q_ps": 3,
    "q_sb": 3,
    "hrep": 2,
    "qbd": 2,
    "hrep1": 2,
    "k_ps": 1,
    "k_sb": 1,
    "vw_ps": 6,
    "vw_sb": 6,
    "s_ps": 5,
    "s_sb": 5,
    "shift": 5,
    "prob": 5,
    "pT_sb0": 1,
    "pT_ps": 4,
    "pT_sb": 4,
    "o_ps": 6,
    "o_sb": 4 + 2,
    "oT_ps": 4,
    "oT_sb": 4,
    "y_ps": 5,
    "x_first": 1,
    "qk_ps": 2,
    "rot_a": 2,
    "rot": 2,
    "neg": 2,
    "expn": 2,
    "phi": 2,
    "phiT_ps": 1,
    "phiT_sb": 1,
    "v1_ps": 2,
    "v1_bd": 2,
    "v1_sb": 1,
    "a_ps": 1,
    "a_sb": 4,
    "st_ps": NCK - 1,
    "st_sb": NCK - 1,
    "r_ps": 1,
    "r_shift": 1,
    "r_exp": 1,
    "x_done": 1,
    "rank_ps": 1,
    "pos": 1,
    "sorted": 2 * TB * 16,
    "stored": 16,
    "dve_step": 62,
}


STARTS = {"pos": SIGNALS["pos"], "stored": SIGNALS["stored"]}


def mega_kernel(nc, a, out, upto=99, iters=ITERS, dump=None):
    ctx = ExitStack()
    with ctx:
        sb = lambda name, shape, dt=F32: ctx.enter_context(nc.sbuf_tensor(name, shape, dt))
        sem = lambda name: ctx.enter_context(nc.semaphore(name))
        x5_dram = nc.dram_tensor("x5_scratch", [B, P, TB * D], F32).ap()
        hs_dram = nc.dram_tensor("sorted_rows", [E * CAP, D], F32).ap()
        tab = sb("tab", [P, TAB_W])
        table = lambda n: tab[:, TAB_AT[n]:TAB_AT[n] + TABLES[n]]
        gates = sb("gates", [P, NT, 2])
        pos = sb("pos", [P, NT, 2])
        next_row = sb("next_row", [P, E])
        build_layers(nc, a, x5_dram, hs_dram, tab, table, gates, pos, next_row, iters, upto, dump)
        if dump is None:
            build_experts(nc, a, x5_dram, hs_dram, tab, table, gates, pos, next_row, out)


def build_layers(nc, a, x5_dram, hs_dram, tab, table, gates, pos, next_row, iters, upto, dump):
    with ExitStack() as ctx:
        sb = lambda name, shape, dt=F32: ctx.enter_context(nc.sbuf_tensor(name, shape, dt))
        sem = lambda name: ctx.enter_context(nc.semaphore(name))
        w = sb("w", [P, NM, KD, D])
        wr = sb("wr", [P, KD, E])
        ternT = sb("ternT", [P, KD, D], BF16)
        rows = sb("rows", [1, 4, D])
        cols = sb("cols", [P, 4, KD])
        fbias = sb("fbias", [P, D])
        wscale = sb("wscale", [P, 1])
        wscale127 = sb("wscale127", [P, 1])
        bound0 = sb("bound0", [P, TB, SC])
        identb = sb("identb", [P, P], BF16)
        packed = sb("packed", [64, D], I32)
        maski = sb("maski", [P, TB, SC], I32)

        L = []
        for n in range(LANES):
            t = {}
            for name, shape in (("xin", [P, TB, D]), ("x", [P, TB, D]), ("h", [P, TB, D]), ("h6", [P, TB, D]),
                                ("hT", [P, KD, SPAD]), ("kT", [P, KD, SPAD]),
                                ("qT", [P, KD, SPAD]), ("qbd", [P, KD, NW, HG, WIN]),
                                ("crep", [P, KD, CREP]), ("ck", [P, 2, KD, SC]), ("kbd", [P, 2, KD, 8, SC]),
                                ("vbd", [P, 2, NC_CH, VH, DV]), ("o", [P, TB, D]), ("oT", [P, KD, S]),
                                ("v1bd", [P, NCK, NPAIR, 2, DV]), ("v1", [P, TB, H, DV]), ("work", [P, 5632]),
                                ("small", [P, 512])):
                t[name] = sb(f"{name}{n}", shape)
            t["posi"] = sb(f"posi{n}", [P, 2, TB], I32)
            t["hTb"] = sb(f"hTb{n}", [P, KD, S], BF16)
            t["hq"] = sb(f"hq{n}", [P, TB, D], BF16)
            wk = t["work"]
            cut = lambda lo, n_, pat, wk=wk, **k: wk[:, lo:lo + n_].rearrange(pat, **k)
            t["vw"] = cut(0, NW * D, "p (j c) -> p j c", j=NW)
            t["hrep"] = cut(2816, KD * NW * P, "p (k j m) -> p k j m", k=KD, j=NW)
            t["hrep1"] = t["qbd"][:, :, :, :, :].rearrange("p k j h q -> p (k j h q)")[:, 0:KD * NCK * P] \
                .rearrange("p (k c m) -> p k c m", k=KD, c=NCK)
            t["s0"] = cut(2816, NU * WIN, "p (u k) -> p u k", u=NU)
            t["pT0"] = cut(2816 + 1408, NU * WIN, "p (u k) -> p u k", u=NU)
            t["s"] = cut(0, TB * HS, "p (t h s) -> p t h s", t=TB, h=H)
            t["sflat"] = cut(0, TB * HS, "p (t n) -> p t n", t=TB)
            t["pT"] = cut(2464, TB * NC_CH * P, "p (t c q) -> p t c q", t=TB, c=NC_CH)
            t["rotA"] = cut(0, 1024, "p (t c) -> p t c", t=TB)
            t["rotB"] = cut(1024, 1024, "p (t c) -> p t c", t=TB)
            t["at"] = cut(0, 2048, "p (u q) -> p u q", q=CK)
            t["phi"] = cut(2048, 1024, "p (t c) -> p t c", t=TB)
            t["k2"] = cut(3072, 1024, "p (k c h q) -> p k c h q", k=KD, c=NCK, h=2)
            t["st"] = cut(4096, 816, "p (c n) -> p c n", c=NCK - 1)
            t["ps"] = ctx.enter_context(nc.psum_tensor(f"ps{n}", [P, 4, 512], F32))
            t["sem"] = {k: sem(f"{k}_{n}") for k in SIGNALS}
            L.append(t)

        consts_in = sem("consts_in")
        init_pool = sem("init_pool")
        init_dve = sem("init_dve")
        init_pe = sem("init_pe")
        N_CONST = 12

        def after(eng, t, name, it, k):
            eng.wait_ge(t["sem"][name], it * SIGNALS[name] + k + STARTS.get(name, 0))

        def carry(eng, t, col):
            eng.tensor_tensor(t["small"][:, col:col + 1], table("row"), table("row"), ALU.add)

        def lane_psum(t, bank, lo, hi):
            return t["ps"][:, bank, lo:hi]

        def interleave(programs):
            live = list(programs)
            n = 0
            while live:
                live = [g for g in live if next(g, "end") != "end"]
                n += 1
                if n >= upto:
                    break

        programs = ctx.enter_context(ExitStack())
        block = programs.enter_context(nc.Block())

        @block.sync
        def _(sp):
            for dst, src in (
                (tab[:, :], a["tables"]), (w[:, :, :, :], a["proj"]), (wr[:, :, :], a["router"]),
                (rows[:, :, :], a["rows"]), (cols[:, :, :], a["cols"]),
                (fbias[:, :], a["fbias"].partition_broadcast(P)),
                (wscale[:, :], a["wscale"].partition_broadcast(P)), (packed[:, :], a["packed"]),
                (maski[:, 0, :], a["mask"][0:P, :]), (maski[:, 1, :], a["mask"][P:2 * P, :]),
            ):
                sp.dma_start(dst, src).then_inc(consts_in, 16)

            def load(n, batch, it, first):
                t = L[n]
                if not first:
                    after(sp, t, "x_first", it, 1)
                    after(sp, t, "cv_sb", it, 2)
                    after(sp, t, "ck_ps", it, 1)
                for r, (lo, n_c) in enumerate(((0, SC), (SC, SC), (2 * SC, CREP - 2 * SC))):
                    sp.dma_start(t["crep"][:, :, lo:lo + n_c], a["ctxT"][bass.ds(batch, 1), :, :, 0:n_c]
                                 .rearrange("o p k s -> (o p) k s")).then_inc(t["sem"]["ctx_in"], 16)
                sp.dma_start(t["xin"][:, :, :], a["x"][bass.ds(batch, 1)].rearrange("o (t p) c -> p (o t) c", p=P)) \
                  .then_inc(t["sem"]["x_in"], 16)

            def store(n, batch, it):
                t = L[n]
                after(sp, t, "x_done", it, 1)
                sp.dma_start(x5_dram[bass.ds(batch, 1)].rearrange("o p c -> (o p) c"),
                             t["x"][:, :, :].rearrange("p t c -> p (t c)")).then_inc(t["sem"]["stored"], 16)

            for n in range(LANES):
                load(n, n, 0, True)
            if iters > 1:
                with sp.Fori(0, iters - 1) as it:
                    for n in range(LANES):
                        load(n, it * LANES + LANES + n, it, False)
                    for n in range(LANES):
                        store(n, it * LANES + n, it)
            if upto > 90:
                for n in range(LANES):
                    store(n, (iters - 1) * LANES + n, iters - 1)
                for n in range(LANES):
                    sp.wait_ge(L[n]["sem"]["stored"], SIGNALS["stored"] * iters + STARTS["stored"])

        @block.gpsimd
        def _(pool):
            for t in L:
                for k, (name, start) in enumerate(STARTS.items()):
                    pool.memset(t["small"][:, 505 + k:506 + k], 0.0).then_inc(t["sem"][name], start)
                pool.memset(t["qT"][:, :, :], 0.0).then_inc(init_pool, 1)
                pool.memset(t["kT"][:, :, :], 0.0).then_inc(init_pool, 1)
                pool.memset(t["hT"][:, :, :], 0.0).then_inc(init_pool, 1)
                pool.memset(t["v1"][:, :, :, :], 1.0).then_inc(init_pool, 1)
            pool.wait_ge(consts_in, 16 * 10)
            for t in L:
                for layer in range(2):
                    pool.tensor_copy(t["vbd"][:, layer, :, :, DH:DV],
                                     table("vmask").rearrange("p (c h) -> p c h", h=VH).unsqueeze(3)).then_inc(init_pool, 1)
                for c in range(NCK):
                    pool.tensor_copy(t["v1bd"][:, c, :, :, DH:DV],
                                     table("rm2").unsqueeze(1).broadcast_to([P, NPAIR, 2]).unsqueeze(3)).then_inc(init_pool, 1)

            def lane(n, it):
                t = L[n]
                after(pool, t, "ck_sb", it, 1)
                for layer in range(2):
                    for half in range(KD):
                        pool.tensor_tensor(
                            t["kbd"][:, layer, half], t["ck"][:, layer, half].unsqueeze(1).broadcast_to([P, 8, SC]),
                            table("hm8").unsqueeze(2).broadcast_to([P, 8, SC]), ALU.mult) \
                            .then_inc(t["sem"]["kbd"], 1)
                for phase in range(N_PHASES):
                    if phase in NORM_PHASES:
                        k = NORM_PHASES.index(phase) + 1
                        after(pool, t, "var", it, k)
                        carry(pool, t, 480 + phase)
                        rstd = t["small"][:, 20:22]
                        pool.tensor_scalar(rstd.unsqueeze(2),
                                           t["small"][:, 16:20].rearrange("p (t m) -> p t m", m=2)[:, :, 1:2],
                                           EPS_LN, None, ALU.add).then_inc(t["sem"]["var_eps"], 1)
                        after(pool, t, "var_eps", it, k)
                        pool.tensor_tensor(rstd, rstd, table("power"), ALU.pow).then_inc(t["sem"]["rstd"], 1)
                    if phase == 2:
                        windows = lambda x, half: bass.AP(
                            x[:, :, :].tensor, x[:, half, 0:1].offset, [x[:, :, :].ap[0], [WQ, NW], [0, HG], [1, WIN]])
                        after(pool, t, "hT", it, 1)
                        carry(pool, t, 480 + phase)
                        for half in range(KD):
                            pool.tensor_copy(t["hrep"][:, half].rearrange("p j (h q) -> p j h q", h=HG), windows(t["hT"], half)) \
                                .then_inc(t["sem"]["hrep"], 1)
                        after(pool, t, "q_sb", it, 1)
                        for half in range(KD):
                            pool.tensor_tensor(t["qbd"][:, half], windows(t["qT"], half),
                                               table("hm4").unsqueeze(1).unsqueeze(3).broadcast_to([P, NW, HG, WIN]), ALU.mult) \
                                .then_inc(t["sem"]["qbd"], 1)
                    if phase == ROT_PHASE:
                        after(pool, t, "hT", it, 4)
                        carry(pool, t, 480 + phase)
                        for half in range(KD):
                            pool.tensor_copy(t["hrep1"][:, half].rearrange("p c (h q) -> p c h q", h=2),
                                             t["hT"][:, half, RADIUS:RADIUS + S].rearrange("p (c q) -> p c q", c=NCK)
                                             .unsqueeze(2).broadcast_to([P, NCK, 2, CK])).then_inc(t["sem"]["hrep1"], 1)
                        for tile in range(TB):
                            after(pool, t, "rot_a", it, tile + 1)
                            pool.tensor_tensor(t["rotA"][:, tile], t["rotA"][:, tile], t["rotB"][:, tile], ALU.add) \
                                .then_inc(t["sem"]["rot"], 1)
                    if phase == N_PHASES - 1:
                        after(pool, t, "pos", it, 1)
                        carry(pool, t, 480 + phase)
                        for i in range(2):
                            for tile in range(TB):
                                pool.indirect_dma_start(
                                    hs_dram[:, :], bass.IndirectOffsetOnAxis(ap=t["posi"][:, i, tile:tile + 1], axis=0),
                                    t["h6"][:, tile, :], None).then_inc(t["sem"]["sorted"], 16)
                    yield

            with pool.Fori(0, iters) as it:
                interleave([lane(n, it) for n in range(LANES)])
                if upto > 90:
                    for t in L:
                        after(pool, t, "sorted", it, SIGNALS["sorted"])

        @block.scalar
        def _(act):
            act.wait_ge(consts_in, 16 * 10)
            act.wait_ge(init_pool, N_POOL)

            def norm_T(t, it, k, dst, lo):
                after(act, t, "hT_ps", it, k)
                act.activation(dst[:, :, lo:lo + S], t["ps"][:, 0, :].rearrange("p (k c) -> p k c", k=KD), ACT.Copy) \
                    .then_inc(t["sem"]["hT"], 1)

            def out_T(t, it, k):
                after(act, t, "oT_ps", it, k)
                act.activation(t["oT"][:, :, :], t["ps"][:, 0, :].rearrange("p (k c) -> p k c", k=KD), ACT.Copy) \
                    .then_inc(t["sem"]["oT_sb"], 1)

            def lane(n, it):
                t = L[n]
                s = t["sem"]
                after(act, t, "ck_ps", it, 1)
                for layer in range(2):
                    for half in range(KD):
                        i = (layer * KD + half) * SC
                        last = act.activation(t["ck"][:, layer, half], lane_psum(t, 2, i, i + SC), ACT.Identity,
                                              bias=cols[:, 2 * layer + 1, half:half + 1])
                last.then_inc(s["ck_sb"], 1)
                yield
                norm_T(t, it, 1, t["hT"], RADIUS)
                yield
                after(act, t, "q_ps", it, 1)
                act.activation(t["qT"][:, :, RADIUS:RADIUS + S], lane_psum(t, 1, 0, 512).rearrange("p (k c) -> p k c", k=KD),
                               ACT.Copy).then_inc(s["q_sb"], 1)
                after(act, t, "k_ps", it, 1)
                act.activation(t["kT"][:, :, RADIUS:RADIUS + S], lane_psum(t, 2, 0, 512).rearrange("p (k c) -> p k c", k=KD),
                               ACT.Copy).then_inc(s["k_sb"], 1)
                yield
                after(act, t, "shift", it, 1)
                act.activation(t["s0"], t["s0"], ACT.Exp, scale=L0_SCALE).then_inc(s["prob"], 1)
                yield
                after(act, t, "oT_ps", it, 1)
                act.activation(t["oT"][:, :, :], t["ps"][:, 0:2, 0:S], ACT.Copy).then_inc(s["oT_sb"], 1)
                yield

                def cross(i, sub):
                    norm_T(t, it, sub + 1, t["hT"], RADIUS)
                    yield
                    after(act, t, "q_ps", it, 2 + i)
                    for half in range(KD):
                        last = act.activation(t["kT"][:, half, RADIUS:RADIUS + S], lane_psum(t, 1, half * S, half * S + S),
                                              ACT.Identity, bias=cols[:, 2 * i, half:half + 1])
                    last.then_inc(s["q_sb"], 1)
                    yield
                    for tile in range(TB):
                        after(act, t, "shift", it, 2 + TB * i + tile)
                        act.activation(t["sflat"][:, tile], t["sflat"][:, tile], ACT.Exp, scale=DH ** -0.5) \
                            .then_inc(s["prob"], 1)
                    yield
                    for tile in range(TB):
                        after(act, t, "pT_ps", it, TB * i + tile + 1)
                        rest = HS - (NC_CH - 1) * P
                        flat = t["pT"][:, tile].rearrange("p c q -> p (c q)")
                        act.activation(flat[:, 0:4 * P], lane_psum(t, 0, 0, 512), ACT.Copy)
                        act.activation(flat[:, 4 * P:8 * P], lane_psum(t, 1, 0, 512), ACT.Copy)
                        act.activation(flat[:, 8 * P:9 * P], lane_psum(t, 2, 0, P), ACT.Copy)
                        act.activation(flat[0:rest, 9 * P:10 * P], t["ps"][0:rest, 2, P:2 * P], ACT.Copy) \
                            .then_inc(s["pT_sb"], 1)
                    yield
                    out_T(t, it, 2 if i == 0 else 4)
                    yield

                yield from cross(0, 1)
                yield
                yield
                norm_T(t, it, 4, t["hT"], RADIUS)
                yield
                for tile in range(TB):
                    after(act, t, "neg", it, tile + 1)
                    act.activation(t["rotB"][:, tile], t["rotB"][:, tile], ACT.Exp).then_inc(s["expn"], 1)
                yield
                for j in range(TB):
                    after(act, t, "v1_bd", it, j + 1)
                    for r in range(2):
                        src = t["ps"][r * CK:(r + 1) * CK, 1 + j, r * D:(r + 1) * D]
                        last = act.activation(t["v1"][r * CK:(r + 1) * CK, j, :, 0:DH],
                                              src.rearrange("p (h d) -> p h d", h=H), ACT.Copy)
                last.then_inc(s["v1_sb"], 1)
                after(act, t, "phiT_ps", it, 1)
                act.activation(t["kT"][:, :, RADIUS:RADIUS + S], lane_psum(t, 0, 0, 512).rearrange("p (k c) -> p k c", k=KD),
                               ACT.Copy)
                for h in range(2):
                    last = act.activation(t["k2"][:, :, :, h, :],
                                          lane_psum(t, 3, 0, 512).rearrange("p (k c q) -> p k c q", k=KD, c=NCK), ACT.Copy, scale=table("hm2")[:, h:h + 1])
                last.then_inc(s["phiT_sb"], 1)
                yield
                yield
                out_T(t, it, 3)
                yield
                yield from cross(1, 4)
                norm_T(t, it, 6, t["hT"], RADIUS)
                yield
                after(act, t, "r_shift", it, 1)
                act.activation(t["small"][:, 320:336], t["small"][:, 320:336], ACT.Exp).then_inc(s["r_exp"], 1)
                yield
                yield

            with act.Fori(0, iters) as it:
                interleave([lane(n, it) for n in range(LANES)])

        @block.tensor
        def _(pe):
            pe.wait_ge(consts_in, 16 * 10)
            pe.wait_ge(init_pool, N_POOL)
            pe.wait_ge(init_dve, N_DVE_INIT)
            ident = table("ident")
            ones_row = table("ones")[0:1, :]

            t0 = L[0]
            tern = t0["work"][0:64, 0:512].bitcast(BF16)
            psb = t0["ps"][:, 0, :].bitcast(BF16)
            for shift in range(4):
                for k in range(KD):
                    last = pe.transpose(psb[:, k * D + shift * 64:k * D + shift * 64 + 64],
                                        tern[:, shift * D + k * P:shift * D + k * P + P], identb[0:64, 0:64])
            last.then_inc(init_pe, 1)
            pe.wait_ge(init_dve, N_DVE_INIT + 1)

            def norm_T(t, it, k, src):
                after(pe, t, "norm", it, k)
                for kk in range(KD):
                    for tile in range(TB):
                        last = pe.transpose(lane_psum(t, 0, kk * S + tile * P, kk * S + tile * P + P),
                                            src[:, tile, kk * P:(kk + 1) * P], ident)
                last.then_inc(t["sem"]["hT_ps"], 1)

            def out_T(t, it, k):
                for kk in range(KD):
                    for tile in range(TB):
                        last = pe.transpose(lane_psum(t, 0, kk * S + tile * P, kk * S + tile * P + P),
                                            t["o"][:, tile, kk * P:(kk + 1) * P], ident)
                last.then_inc(t["sem"]["oT_ps"], 1)

            def out_proj(t, it, k, bank, mat, bias_row):
                after(pe, t, "oT_sb", it, k)
                for tile in range(TB):
                    dst = lane_psum(t, bank, tile * D, tile * D + D)
                    for half in range(KD):
                        last = pe.matmul(dst, t["oT"][:, half, tile * P:(tile + 1) * P], w[:, mat, half, :],
                                         start=(half == 0), stop=(half == KD - 1 and bias_row is None))
                    if bias_row is not None:
                        last = pe.matmul(dst, ones_row, rows[0:1, bias_row, :], start=False, stop=True)
                last.then_inc(t["sem"]["y_ps"], 1)

            def feature_proj(t, bank, mat, hT):
                for half in range(KD):
                    for k in range(KD):
                        last = pe.matmul(lane_psum(t, bank, half * S, half * S + S), w[:, mat, k, half * P:(half + 1) * P],
                                         hT[:, k, RADIUS:RADIUS + S], start=(k == 0), stop=(k == KD - 1))
                return last

            def lane(n, it):
                t = L[n]
                s = t["sem"]
                hT = t["hT"]
                after(pe, t, "pos", it, 0)
                after(pe, t, "ctx_in", it, 48)
                for layer in range(2):
                    for half in range(KD):
                        i = (layer * KD + half) * SC
                        for k in range(KD):
                            last = pe.matmul(lane_psum(t, 2, i, i + SC), w[:, (X0K, X1K)[layer], k, half * P:(half + 1) * P],
                                             t["crep"][:, k, 0:SC], start=(k == 0), stop=(k == KD - 1))
                last.then_inc(s["ck_ps"], 1)
                for layer in range(2):
                    for c in range(NC_CH):
                        h0, n_rows = chunk_heads(c)
                        nh = min(VH, H - h0)
                        off = P * c % SC
                        dst = t["ps"][0:n_rows, (3, 1)[layer], c * VH * DH:(c * VH + nh) * DH]
                        for k in range(KD):
                            pe.matmul(dst, t["crep"][:, k, off:off + n_rows],
                                      w[:, (X0V, X1V)[layer], k, h0 * DH:(h0 + nh) * DH], start=(k == 0), stop=False)
                        last = pe.matmul(dst, ones_row[:, 0:n_rows], rows[0:1, 2 * layer, h0 * DH:(h0 + nh) * DH],
                                         start=False, stop=True)
                    last.then_inc(s["cv_ps"], 1)
                yield
                norm_T(t, it, 1, t["h"])
                yield
                after(pe, t, "hT", it, 1)
                after(pe, t, "cv_sb", it, 2)
                feature_proj(t, 1, W0Q, hT).then_inc(s["q_ps"], 1)
                after(pe, t, "ck_sb", it, 1)
                feature_proj(t, 2, W0K, hT).then_inc(s["k_ps"], 1)
                after(pe, t, "hrep", it, 2)
                for j in range(NW):
                    bank = (3, 0)[j // 2 % 2]
                    if j >= 4 and j % 2 == 0:
                        after(pe, t, "vw_sb", it, j // 2 - 1)
                    for k in range(KD):
                        last = pe.matmul(lane_psum(t, bank, (j % 2) * D, (j % 2) * D + D), t["hrep"][:, k, j], w[:, W0V, k, :],
                                         start=(k == 0), stop=(k == KD - 1))
                    if j % 2 == 1 or j == NW - 1:
                        last.then_inc(s["vw_ps"], 1)
                yield
                after(pe, t, "qbd", it, 2)
                after(pe, t, "k_sb", it, 1)
                after(pe, t, "vw_sb", it, 6)
                for j in range(NW):
                    for g in range(NG):
                        u, half, r = j * KD + g // 2, g // 2, 64 * (g % 2)
                        win = slice(j * WQ, j * WQ + WIN)
                        last = pe.matmul(lane_psum(t, 2 * (g % 2) + u // 16, u % 16 * WIN, u % 16 * WIN + WIN),
                                         t["qbd"][r:r + 64, half, j].rearrange("p h q -> p (h q)"), t["kT"][r:r + 64, half, win],
                                         start=True, stop=True)
                last.then_inc(s["s_ps"], 1)
                yield
                after(pe, t, "pT_sb0", it, 1)
                after(pe, t, "vw_sb", it, 6)
                for j in range(NW):
                    for g in range(NG):
                        r = 64 * (g % 2)
                        last = pe.matmul(t["ps"][r:r + 64, g // 2, j * WQ:(j + 1) * WQ], t["vw"][:, j, g * 64:(g + 1) * 64],
                                         t["pT0"][:, g % 2 * NW * KD + j * KD + g // 2, RADIUS:WIN], start=True, stop=True)
                last.then_inc(s["oT_ps"], 1)
                out_proj(t, it, 1, 2, W0O, None)
                yield

                def cross(i, sub):
                    norm_T(t, it, sub + 1, t["h"])
                    yield
                    after(pe, t, "hT", it, sub + 1)
                    feature_proj(t, 1, (X0Q, X1Q)[i], hT).then_inc(s["q_ps"], 1)
                    yield
                    after(pe, t, "q_sb", it, 2 + i)
                    after(pe, t, "kbd", it, 4)
                    for tile in range(TB):
                        if tile:
                            after(pe, t, "s_sb", it, 1 + TB * i + tile)
                        for g in range(4):
                            last = pe.matmul(lane_psum(t, g, 0, 4 * SC),
                                             t["kT"][:, g // 2, RADIUS + tile * P:RADIUS + (tile + 1) * P],
                                             t["kbd"][:, i, g // 2, g % 2 * 4:g % 2 * 4 + 4, :], start=True, stop=True)
                        last.then_inc(s["s_ps"], 1)
                    yield
                    for tile in range(TB):
                        after(pe, t, "prob", it, 2 + TB * i + tile)
                        if tile == 0:
                            after(pe, t, "s_sb", it, 1 + TB * (i + 1))
                        else:
                            after(pe, t, "pT_sb", it, TB * i + tile)
                        for c in range(NC_CH):
                            n_rows = chunk_heads(c)[1]
                            last = pe.transpose(t["ps"][0:n_rows, c // 4, c % 4 * P:c % 4 * P + P],
                                                t["sflat"][:, tile, c * P:c * P + n_rows], ident)
                        last.then_inc(s["pT_ps"], 1)
                        after(pe, t, "pT_sb", it, TB * i + tile + 1)
                        if tile:
                            after(pe, t, "o_sb", it, (0 if i == 0 else 4) + tile)
                        for c in range(NC_CH):
                            h0, n_rows = chunk_heads(c)
                            nh = min(VH, H - h0)
                            last = pe.matmul(lane_psum(t, 3, h0 * DV, (h0 + nh) * DV), t["pT"][0:n_rows, tile, c, :],
                                             t["vbd"][0:n_rows, i, c, 0:nh, :], start=(c == 0), stop=(c == NC_CH - 1),
                                             skip_group_check=True)
                        last.then_inc(s["o_ps"], 1)
                    yield
                    after(pe, t, "o_sb", it, (2 if i == 0 else 6))
                    out_T(t, it, 0)
                    out_proj(t, it, (2 if i == 0 else 4), 1, (X0O, X1O)[i], 1 + 2 * i)
                    yield

                after(pe, t, "cv_sb", it, 2)
                yield from cross(0, 1)
                after(pe, t, "norm", it, 3)
                psb = t["ps"][:, 0, :].bitcast(BF16)
                for kk in range(KD):
                    for tile in range(TB):
                        last = pe.transpose(psb[:, kk * S + tile * P:kk * S + tile * P + P],
                                            t["hq"][:, tile, kk * P:(kk + 1) * P], identb[:, :])
                last.then_inc(s["hT_ps"], 1)
                yield
                after(pe, t, "hT", it, 3)
                for tile in range(TB):
                    for k in range(KD):
                        last = pe.matmul(lane_psum(t, 1, tile * D, tile * D + D), t["hTb"][:, k, tile * P:(tile + 1) * P],
                                         ternT[:, k, :], start=(k == 0), stop=(k == KD - 1))
                last.then_inc(s["y_ps"], 1)
                yield
                norm_T(t, it, 4, t["h"])
                yield
                after(pe, t, "hT", it, 4)
                for tile in range(TB):
                    for k in range(KD):
                        last = pe.matmul(lane_psum(t, 1 + tile, 0, 512), hT[:, k, RADIUS + tile * P:RADIUS + (tile + 1) * P],
                                         w[:, W1Q:W1K + 1, k, :], start=(k == 0), stop=(k == KD - 1))
                    last.then_inc(s["qk_ps"], 1)
                yield
                after(pe, t, "rot_a", it, 2)
                after(pe, t, "hrep1", it, 2)
                for c in range(NCK):
                    for k in range(KD):
                        last = pe.matmul(lane_psum(t, 1 + c // 2, c % 2 * D, c % 2 * D + D), t["hrep1"][:, k, c], w[:, W1V, k, :],
                                         start=(k == 0), stop=(k == KD - 1))
                    if c % 2:
                        last.then_inc(s["v1_ps"], 1)
                after(pe, t, "phi", it, 2)
                for part, bank in ((0, 0), (1, 3)):
                    for kk in range(KD):
                        for tile in range(TB):
                            last = pe.transpose(lane_psum(t, bank, kk * S + tile * P, kk * S + tile * P + P),
                                                t["phi"][:, tile, part * D + kk * P:part * D + (kk + 1) * P], ident)
                last.then_inc(s["phiT_ps"], 1)
                yield
                after(pe, t, "phiT_sb", it, 1)
                after(pe, t, "v1_sb", it, 1)
                after(pe, t, "v1_bd", it, 2)
                for c in range(NCK):
                    for pr in range(NPAIR):
                        r = 32 * (pr % 4)
                        u = c * 2 + pr // 4
                        last = pe.matmul(lane_psum(t, pr % 4, u * CK, (u + 1) * CK),
                                         t["k2"][r:r + 32, pr // 4, c].rearrange("p h q -> p (h q)"),
                                         t["kT"][r:r + 32, pr // 4, RADIUS + c * CK:RADIUS + (c + 1) * CK],
                                         start=True, stop=True)
                last.then_inc(s["a_ps"], 1)
                for c in range(1, NCK):
                    after(pe, t, "a_sb", it, c)
                    for half in range(KD):
                        dst = lane_psum(t, c - 1, half * 8 * DV, (half + 1) * 8 * DV)
                        col = slice(D + half * P, D + (half + 1) * P)
                        hh = slice(half * 8, half * 8 + 8)
                        full = c // 2
                        if full:
                            last = pe.matmul(dst, t["phi"][:, 0, col], t["v1"][:, 0, hh, :], start=True, stop=(c % 2 == 0))
                        if c % 2:
                            last = pe.matmul(dst, t["phi"][0:CK, full, col], t["v1"][0:CK, full, hh, :],
                                             start=(full == 0), stop=True)
                    last.then_inc(s["st_ps"], 1)
                after(pe, t, "a_sb", it, 4)
                for c in range(NCK):
                    bank, r = (3, 0)[c // 2], CK * (c % 2)
                    if c:
                        after(pe, t, "st_sb", it, c)
                    for pr in range(NPAIR):
                        last = pe.matmul(t["ps"][r:r + CK, bank, pr * 2 * DV:(pr + 1) * 2 * DV],
                                         t["at"][:, pr % 4 * 2 * NCK + c * 2 + pr // 4, :], t["v1bd"][:, c, pr], start=(pr == 0),
                                         stop=(pr == NPAIR - 1 and c == 0), skip_group_check=True)
                    if c:
                        for half in range(KD):
                            last = pe.matmul(t["ps"][r:r + CK, bank, half * 8 * DV:(half + 1) * 8 * DV],
                                             t["kT"][:, half, RADIUS + c * CK:RADIUS + (c + 1) * CK],
                                             t["st"][:, c - 1, half * 8 * DV:(half + 1) * 8 * DV], start=False,
                                             stop=(half == KD - 1), skip_group_check=True)
                    if c % 2:
                        last.then_inc(s["o_ps"], 1)
                yield
                after(pe, t, "o_sb", it, 4)
                out_T(t, it, 0)
                out_proj(t, it, 3, 1, W1O, None)
                yield
                yield from cross(1, 4)
                norm_T(t, it, 6, t["h6"])
                yield
                after(pe, t, "hT", it, 6)
                for tile in range(TB):
                    for k in range(KD):
                        last = pe.matmul(lane_psum(t, 1, tile * E, (tile + 1) * E),
                                         hT[:, k, RADIUS + tile * P:RADIUS + (tile + 1) * P], wr[:, k, :],
                                         start=(k == 0), stop=(k == KD - 1))
                last.then_inc(s["r_ps"], 1)
                yield
                after(pe, t, "x_done", it, 1)
                pe.matmul(lane_psum(t, 2, 0, TB * E), table("before"), t["small"][:, 402:402 + TB * E], start=True, stop=True)
                pe.matmul(lane_psum(t, 2, TB * E, 2 * TB * E), table("ones"), t["small"][:, 402:402 + TB * E],
                          start=True, stop=True).then_inc(s["rank_ps"], 1)
                yield

            with pe.Fori(0, iters) as it:
                interleave([lane(n, it) for n in range(LANES)])

        @block.vector
        def _(dve):
            dve.wait_ge(consts_in, 16 * 10)
            steps = [0]

            def init(ins):
                steps[0] += 1
                ins.then_inc(init_dve, 1)
                dve.wait_ge(init_dve, steps[0])

            init(dve.tensor_copy(identb[:, :], table("ident")))
            init(dve.tensor_copy(next_row[:, :], table("first_row")))
            maskf = L[0]["work"][:, 1024:1024 + TB * SC].rearrange("p (t s) -> p t s", t=TB)
            init(dve.tensor_copy(maskf, maski[:, :, :]))
            init(dve.tensor_scalar(maskf, maskf, 0.0, None, ALU.is_equal))
            init(dve.tensor_scalar(bound0[:, :, :], maskf, -BIG, BIG, ALU.mult, ALU.add))
            init(dve.tensor_scalar(maskf, maskf, -1e10 * DH ** 0.5, None, ALU.mult))
            init(dve.tensor_tensor(bound0[:, :, :], bound0[:, :, :], maskf, ALU.add))
            init(dve.tensor_scalar(wscale127[:, :], wscale[:, :], 1.0 / 127.0, None, ALU.mult))
            codes = L[0]["work"][0:64, 2048:3072].bitcast(I32)
            for shift in range(4):
                init(dve.tensor_scalar(codes[:, shift * D:(shift + 1) * D], packed[:, :], 2 * shift, 3,
                                       ALU.logical_shift_right, ALU.bitwise_and))
            tern = L[0]["work"][0:64, 0:512].bitcast(BF16)
            init(dve.tensor_scalar(tern, codes, -1.0, None, ALU.add))
            assert steps[0] == N_DVE_INIT, steps
            dve.wait_ge(init_pe, 1)
            init(dve.tensor_copy(ternT[:, :, :], L[0]["ps"][:, 0, :].bitcast(BF16)[:, 0:KD * D]
                                 .rearrange("p (k c) -> p k c", k=KD)))
            counts = [[0] for _ in L]
            norms = [0] * LANES

            def lane(n, it):
                t = L[n]
                s = t["sem"]
                count = counts[n]
                small = t["small"]

                def link(ins):
                    count[0] += 1
                    ins.then_inc(s["dve_step"], 1)
                    after(dve, t, "dve_step", it, count[0])

                def layernorm(x, dst, signal):
                    for tile in range(TB):
                        dve.bn_stats(small[:, tile * 6:tile * 6 + 6], x[:, tile]) if tile < TB - 1 else \
                            link(dve.bn_stats(small[:, tile * 6:tile * 6 + 6], x[:, tile]))
                    carry(dve, t, 440 + norms[n])
                    for tile in range(TB):
                        ins = dve.bn_aggr(small[:, 16 + tile * 2:18 + tile * 2], small[:, tile * 6:tile * 6 + 6])
                    ins.then_inc(s["var"], 1)
                    norms[n] += 1
                    after(dve, t, "rstd", it, norms[n])
                    for tile in range(TB):
                        ins = dve.tensor_scalar(dst[:, tile], x[:, tile], small[:, 16 + 2 * tile:17 + 2 * tile],
                                                small[:, 20 + tile:21 + tile], ALU.subtract, ALU.mult)
                    if signal:
                        ins.then_inc(s["norm"], 1)
                    else:
                        link(ins)

                def residual(it_k, bank, x_old):
                    after(dve, t, "y_ps", it, it_k)
                    count[0] += 1
                    dve.tensor_tensor(t["x"][:, :, :].rearrange("p t c -> p (t c)"), lane_psum(t, bank, 0, 512),
                                      x_old[:, :, :].rearrange("p t c -> p (t c)"), ALU.add) \
                       .then_inc(s["dve_step"], 1)
                    after(dve, t, "dve_step", it, count[0])

                for layer in range(2):
                    after(dve, t, "cv_ps", it, layer + 1)
                    bank = (3, 1)[layer]
                    n9 = NC_CH - 1
                    vm = table("vmask").unsqueeze(2).broadcast_to([P, NC_CH * VH, DH])
                    ps = t["ps"][:, bank, 0:NC_CH * VH * DH].rearrange("p (c d) -> p c d", d=DH)
                    dst = t["vbd"][:, layer].rearrange("p c h d -> p (c h) d")
                    dve.tensor_tensor(dst[:, 0:n9 * VH, 0:DH], ps[:, 0:n9 * VH], vm[:, 0:n9 * VH], ALU.mult)
                    h0, nr = chunk_heads(n9)
                    dve.tensor_tensor(dst[0:nr, n9 * VH:n9 * VH + H - h0, 0:DH], ps[0:nr, n9 * VH:n9 * VH + H - h0],
                                      vm[0:nr, n9 * VH:n9 * VH + H - h0], ALU.mult).then_inc(s["cv_sb"], 1)
                yield
                after(dve, t, "x_in", it, 16)
                layernorm(t["xin"], t["h"], True)
                yield
                for j in range(0, NW, 2):
                    nj = min(2, NW - j)
                    after(dve, t, "vw_ps", it, j // 2 + 1)
                    src = lane_psum(t, (3, 0)[j // 2 % 2], 0, nj * D).rearrange("p (g h d) -> p g h d", h=HG, d=DH)
                    dst = t["vw"][:, j:j + nj, :].rearrange("p j (g h d) -> p (j g) h d", h=HG, d=DH)
                    dve.tensor_tensor(dst, src, table("rm4").unsqueeze(1).unsqueeze(3).broadcast_to([P, nj * NG, HG, DH]),
                                      ALU.mult).then_inc(s["vw_sb"], 1)
                yield
                after(dve, t, "s_ps", it, 1)
                for r in range(2):
                    ps = t["ps"][:, 2 * r:2 * r + 2, :].rearrange("p b (u k) -> p (b u) k", k=WIN)
                    u = r * NW * KD
                    dve.tensor_tensor(t["s0"][:, u:u + KD], ps[:, 0:KD],
                                      table("band0").unsqueeze(1).broadcast_to([P, KD, WIN]), ALU.min)
                    last = dve.tensor_tensor(t["s0"][:, u + KD:u + NW * KD], ps[:, KD:NW * KD],
                                             table("band").unsqueeze(1).broadcast_to([P, (NW - 1) * KD, WIN]), ALU.min)
                last.then_inc(s["s_sb"], 1)
                after(dve, t, "s_sb", it, 1)
                link(dve.tensor_reduce(small[:, 64:64 + NU], t["s0"], AX_X, ALU.max))
                dve.tensor_tensor(t["s0"], t["s0"], small[:, 64:64 + NU].unsqueeze(2).broadcast_to([P, NU, WIN]),
                                  ALU.subtract).then_inc(s["shift"], 1)
                after(dve, t, "prob", it, 1)
                link(dve.tensor_reduce(small[:, 64:64 + NU], t["s0"], AX_X, ALU.add))
                link(dve.reciprocal(small[:, 64:64 + NU], small[:, 64:64 + NU]))
                link(dve.tensor_tensor(t["s0"], t["s0"], small[:, 64:64 + NU].unsqueeze(2).broadcast_to([P, NU, WIN]),
                                       ALU.mult))
                dve.transpose(t["pT0"].rearrange("p u k -> p (u k)"), t["s0"].rearrange("p u k -> p (u k)")) \
                   .then_inc(s["pT_sb0"], 1)
                yield
                after(dve, t, "y_ps", it, 1)
                after(dve, t, "stored", it, 0)
                dve.tensor_tensor(t["x"][:, :, :].rearrange("p t c -> p (t c)"), lane_psum(t, 2, 0, 512),
                                  t["xin"][:, :, :].rearrange("p t c -> p (t c)"), ALU.add).then_inc(s["x_first"], 1)
                after(dve, t, "x_first", it, 1)
                yield

                def normalise(it_k, o_k, bank, tile, floor):
                    after(dve, t, "o_ps", it, o_k)
                    o = lane_psum(t, bank, 0, H * DV).rearrange("p (h d) -> p h d", d=DV)
                    rec = small[:, 160 + 16 * tile:176 + 16 * tile].unsqueeze(2)
                    if floor is None:
                        link(dve.reciprocal(rec, o[:, :, DH:DV]))
                    else:
                        link(dve.tensor_scalar(rec, o[:, :, DH:DV], floor, None, ALU.max))
                        link(dve.reciprocal(rec, rec))
                    dve.tensor_tensor(t["o"][:, tile].rearrange("p (h d) -> p h d", d=DH), o[:, :, 0:DH],
                                      rec.broadcast_to([P, H, DH]), ALU.mult).then_inc(s["o_sb"], 1)

                def cross(i, sub):
                    layernorm(t["x"], t["h"], True)
                    yield
                    yield
                    bounds = bound0[:, :, :] if i == 0 else table("caus").rearrange("p (t s) -> p t s", t=TB)
                    for tile in range(TB):
                        after(dve, t, "s_ps", it, 2 + TB * i + tile)
                        ps = t["ps"][:, :, 0:4 * SC].rearrange("p g (h s) -> p g h s", s=SC)
                        bd = bounds[:, tile].unsqueeze(1).unsqueeze(1).broadcast_to([P, 4, 4, SC])
                        dst = t["s"][:, tile].rearrange("p (g h) s -> p g h s", g=4)
                        dve.tensor_tensor(dst, ps, bd, ALU.min).then_inc(s["s_sb"], 1)
                    for tile in range(TB):
                        after(dve, t, "s_sb", it, 2 + TB * i + tile)
                        mx = small[:, 128 + 16 * tile:144 + 16 * tile]
                        link(dve.tensor_reduce(mx, t["s"][:, tile], AX_X, ALU.max))
                        dve.tensor_tensor(t["s"][:, tile], t["s"][:, tile], mx.unsqueeze(2).broadcast_to([P, H, SC]),
                                          ALU.subtract).then_inc(s["shift"], 1)
                    yield
                    for tile in range(TB):
                        normalise(it, (1 if i == 0 else 5) + tile, 3, tile, None)
                    yield
                    residual(2 if i == 0 else 5, 1, t["x"])
                    yield

                yield from cross(0, 1)
                layernorm(t["x"], t["h"], False)
                amax = small[:, 200:202]
                link(dve.tensor_reduce(amax, t["h"][:, :, :], AX_X, ALU.max, apply_absolute_value=True))
                link(dve.tensor_scalar(amax, amax, 1e-5, None, ALU.max))
                dve.tensor_scalar(small[:, 204:206], amax, wscale127[:, 0:1], None, ALU.mult)
                link(dve.reciprocal(small[:, 202:204], amax))
                link(dve.tensor_scalar(small[:, 202:204], small[:, 202:204], 127.0, None, ALU.mult))
                for tile in range(TB):
                    ins = dve.tensor_scalar(t["h"][:, tile], t["h"][:, tile], small[:, 202 + tile:203 + tile], MAGIC,
                                            ALU.mult, ALU.add)
                link(ins)
                dve.tensor_scalar(t["hq"][:, :, :], t["h"][:, :, :], -MAGIC, 127.0, ALU.add, ALU.min) \
                   .then_inc(s["norm"], 1)
                yield
                after(dve, t, "hT_ps", it, 3)
                dve.tensor_scalar(t["hTb"][:, :, :], t["ps"][:, 0, :].bitcast(BF16)[:, 0:KD * S]
                                  .rearrange("p (k c) -> p k c", k=KD), -128.0, None, ALU.max).then_inc(s["hT"], 1)
                after(dve, t, "y_ps", it, 3)
                for tile in range(TB):
                    ins = dve.scalar_tensor_tensor(t["h"][:, tile], lane_psum(t, 1, tile * D, tile * D + D),
                                                   small[:, 204 + tile:205 + tile], fbias[:, :], ALU.mult, ALU.add)
                link(ins)
                link(dve.tensor_tensor(t["x"][:, :, :], t["x"][:, :, :], t["h"][:, :, :], ALU.add))
                yield
                layernorm(t["x"], t["h"], True)
                yield
                rope = table("rope").rearrange("p (t c) -> p t c", t=TB)
                for tile in range(TB):
                    after(dve, t, "qk_ps", it, tile + 1)
                    qk = lane_psum(t, 1 + tile, 0, 512).rearrange("p (h d) -> p h d", d=DH)
                    rb = t["rotB"][:, tile].rearrange("p (h d) -> p h d", d=DH)
                    ra = t["rotA"][:, tile].rearrange("p (h r d) -> p h r d", r=2, d=8)
                    dve.tensor_tensor(rb[:, :, 0:8], qk[:, :, 8:16],
                                      rope[:, tile, 8:16].unsqueeze(1).broadcast_to([P, 32, 8]), ALU.mult)
                    dve.tensor_tensor(rb[:, :, 8:16], qk[:, :, 0:8],
                                      rope[:, tile, 16:24].unsqueeze(1).broadcast_to([P, 32, 8]), ALU.mult)
                    dve.tensor_tensor(ra, qk.rearrange("p h (r d) -> p h r d", r=2),
                                      rope[:, tile, 0:8].unsqueeze(1).unsqueeze(1).broadcast_to([P, 32, 2, 8]), ALU.mult) \
                       .then_inc(s["rot_a"], 1)
                for tile in range(TB):
                    after(dve, t, "rot", it, tile + 1)
                    dve.tensor_scalar(t["rotB"][:, tile], t["rotA"][:, tile], 0.0, None, ALU.min).then_inc(s["neg"], 1)
                for tile in range(TB):
                    after(dve, t, "expn", it, tile + 1)
                    dve.scalar_tensor_tensor(t["phi"][:, tile], t["rotA"][:, tile], 0.0, t["rotB"][:, tile],
                                             ALU.max, ALU.add).then_inc(s["phi"], 1)
                yield
                for j in range(2):
                    after(dve, t, "v1_ps", it, j + 1)
                    dve.tensor_tensor(t["v1bd"][:, 2 * j:2 * j + 2, :, :, 0:DH].rearrange("p c q h d -> p (c q) h d"),
                                      lane_psum(t, 1 + j, 0, 512).rearrange("p (q h d) -> p q h d", h=2, d=DH),
                                      table("rm2").unsqueeze(1).unsqueeze(3).broadcast_to([P, 2 * NPAIR, 2, DH]), ALU.mult) \
                       .then_inc(s["v1_bd"], 1)
                yield
                after(dve, t, "a_ps", it, 1)
                for c in range(NCK):
                    dve.tensor_tensor(t["at"][:, c * NPAIR:(c + 1) * NPAIR],
                                      lane_psum(t, c, 0, 512).rearrange("p (u q) -> p u q", q=CK),
                                      table("tri").unsqueeze(1).broadcast_to([P, NPAIR, CK]), ALU.mult) \
                       .then_inc(s["a_sb"], 1)
                for c in range(1, NCK):
                    after(dve, t, "st_ps", it, c)
                    dve.tensor_tensor(t["st"][:, c - 1].rearrange("p (k h d) -> p k h d", k=KD, h=8),
                                      lane_psum(t, c - 1, 0, H * DV).rearrange("p (k h d) -> p k h d", k=KD, h=8),
                                      table("hm8").unsqueeze(1).unsqueeze(3).broadcast_to([P, KD, 8, DV]), ALU.mult) \
                       .then_inc(s["st_sb"], 1)
                for tile in range(TB):
                    normalise(it, 3 + tile, (3, 0)[tile], tile, 1e-6)
                yield
                residual(4, 1, t["x"])
                yield
                yield from cross(1, 4)
                layernorm(t["x"], t["h6"], True)
                yield
                after(dve, t, "r_ps", it, 1)
                lg = small[:, 300:316].rearrange("p (t e) -> p t e", e=E)
                m1, m2 = small[:, 340:342], small[:, 342:344]
                r1 = small[:, 344:346]
                pr = small[:, 320:336].rearrange("p (t e) -> p t e", e=E)
                rk = small[:, 350:366].rearrange("p (t e) -> p t e", e=E)
                desc = table("desc").unsqueeze(1).broadcast_to([P, TB, E])
                wide = lambda v: v.unsqueeze(2).broadcast_to([P, TB, E])
                link(dve.tensor_copy(lg, lane_psum(t, 1, 0, TB * E).rearrange("p (t e) -> p t e", e=E)))
                link(dve.tensor_reduce(m1, lg, AX_X, ALU.max))
                dve.tensor_tensor(pr, lg, wide(m1), ALU.subtract).then_inc(s["r_shift"], 1)
                after(dve, t, "r_exp", it, 1)
                link(dve.tensor_reduce(m1, pr, AX_X, ALU.add))
                link(dve.reciprocal(m1, m1))
                link(dve.tensor_tensor(pr, pr, wide(m1), ALU.mult))
                hot = [small[:, 370 + 16 * i:386 + 16 * i].rearrange("p (t e) -> p t e", e=E) for i in range(2)]
                for i, m in enumerate((m1, m2)):
                    link(dve.tensor_reduce(m, pr, AX_X, ALU.max))
                    link(dve.tensor_tensor(rk, pr, wide(m), ALU.is_equal))
                    link(dve.tensor_tensor(rk, rk, desc, ALU.mult))
                    link(dve.tensor_reduce(r1, rk, AX_X, ALU.max))
                    link(dve.tensor_tensor(hot[i], rk, wide(r1), ALU.is_equal))
                    if i == 0:
                        link(dve.tensor_scalar(rk, hot[i], 4.0, None, ALU.mult))
                        link(dve.tensor_tensor(pr, pr, rk, ALU.subtract))
                link(dve.tensor_tensor(r1, m1, m2, ALU.add))
                link(dve.tensor_scalar(r1, r1, 1e-6, None, ALU.add))
                link(dve.reciprocal(r1, r1))
                first = it * LANES * TB + n * TB
                chosen = small[:, 402:418].rearrange("p (t e) -> p t e", e=E)
                dve.tensor_tensor(chosen, hot[0], hot[1], ALU.add)
                for i, m in enumerate((m1, m2)):
                    ins = dve.tensor_tensor(gates[:, bass.ds(first, TB), i], m, r1, ALU.mult)
                ins.then_inc(s["x_done"], 1)
                yield
                after(dve, t, "rank_ps", it, 1)
                place = small[:, 420:436].rearrange("p (t e) -> p t e", e=E)
                ranks = lane_psum(t, 2, 0, TB * E).rearrange("p (t e) -> p t e", e=E)
                totals = lane_psum(t, 2, TB * E, 2 * TB * E).rearrange("p (t e) -> p t e", e=E)
                for tile in range(TB):
                    link(dve.tensor_tensor(place[:, tile], ranks[:, tile], next_row[:, :], ALU.add))
                    link(dve.tensor_tensor(next_row[:, :], totals[:, tile], next_row[:, :], ALU.add))
                for i in range(2):
                    link(dve.tensor_tensor(rk, hot[i], place, ALU.mult))
                    link(dve.tensor_reduce(r1, rk, AX_X, ALU.add))
                    dve.tensor_copy(pos[:, bass.ds(first, TB), i], r1)
                    ins = dve.tensor_copy(t["posi"][:, i], r1) if i else link(dve.tensor_copy(t["posi"][:, i], r1))
                ins.then_inc(s["pos"], 1)
                yield
                assert count[0] == SIGNALS["dve_step"], count

            with dve.Fori(0, iters) as it:
                interleave([lane(n, it) for n in range(LANES)])

        programs.close()
        if dump is not None:
            dump(nc, L, dict(ternT=ternT, bound0=bound0, pos=pos, next_row=next_row, gates=gates))


def build_experts(nc, a, x5_dram, hs_dram, tab, table, gates, pos, next_row, out):
    with ExitStack() as ctx:
        sb = lambda name, shape, dt=F32: ctx.enter_context(nc.sbuf_tensor(name, shape, dt))
        sem = lambda name: ctx.enter_context(nc.semaphore(name))
        ys_dram = nc.dram_tensor("sorted_outputs", [NJ * P, D], F32).ap()
        NC = FF // P
        w13 = sb("w13", [P, E, KD, 2 * FF])
        w2 = sb("w2", [P, E, NC, D])
        hin = sb("hin", [P, 2, D])
        hT = sb("hT", [P, 2, KD, P])
        th = sb("th", [P, 2, FF])
        gated = sb("gated", [P, 2, FF])
        inner = sb("inner", [P, 2, FF])
        innerT = sb("innerT", [P, 2, NC, P])
        y = sb("y", [P, 2, D])
        zeros = sb("zeros", [P, D])
        pad_at = sb("pad_at", [P, E], I32)
        plan = sb("plan", [1, 2, NJ], I32)
        f = sb("plan_f", [1, 2, NJ])
        out_at = sb("out_at", [P, NT, 2])
        past = sb("past", [P, NT * 2, E])
        now, upto_e, inside, val = (sb(n, [1, NJ, E]) for n in ("now", "upto_e", "inside", "val"))
        e8 = sb("e8", [P, 7, E])
        padf = sb("padf", [P, E])
        back = sb("back", [P, 2, TB, D])
        yback = sb("yback", [P, 2, 2, TB, D])
        at = sb("at", [P, 2, 2, TB], I32)
        gate = sb("gate", [P, 2, 2, TB])
        gu = ctx.enter_context(nc.psum_tensor("gu", [P, 2, 2, FF], F32))
        psT = ctx.enter_context(nc.psum_tensor("psT", [P, FF], F32))
        psH = ctx.enter_context(nc.psum_tensor("psH", [P, 512], F32))
        psY = ctx.enter_context(nc.psum_tensor("psY", [P, 2, 512], F32))

        weights_in = sem("weights_in")
        plan_step = sem("plan_step")
        zeroed = sem("zeroed")
        padded = sem("padded")
        h_in = [sem(f"h_in{q}") for q in range(2)]
        hT_ps, hT_sb = sem("e_hT_ps"), sem("e_hT_sb")
        gu_ps = sem("gu_ps")
        tanh = sem("tanh")
        gated_done = sem("gated_done")
        inner_sb = sem("inner_sb")
        innerT_ps, innerT_sb = sem("innerT_ps"), sem("innerT_sb")
        e_y_ps, e_y_sb = sem("e_y_ps"), sem("e_y_sb")
        y_stored = [sem(f"y_stored{q}") for q in range(2)]
        at_ready = sem("at_ready")
        gathered = [sem(f"gathered{q}") for q in range(2)]
        carried = sem("carried")
        x_back = [sem(f"x_back{q}") for q in range(2)]
        sum1 = sem("sum1")
        summed = sem("summed")
        out_stored = [sem(f"out_stored{q}") for q in range(2)]
        N_PLAN = 20

        def landed(eng, sems, j, q, amount=16):
            eng.wait_ge(sems[q], (j - q) * (amount // 2) + amount)

        block = ctx.enter_context(nc.Block())

        @block.sync
        def _(sp):
            for e in range(E):
                sp.dma_start(w13[:, e], a["w13"][e]).then_inc(weights_in, 16)
                sp.dma_start(w2[:, e], a["w2"][e]).then_inc(weights_in, 16)
            sp.wait_ge(plan_step, N_PLAN)
            sp.wait_ge(padded, 16 * E)

            def load(j, q):
                row = sp.value_load(plan[0:1, 1, bass.ds(j, 1)], min_val=0, max_val=E * CAP - P)
                sp.dma_start(hin[:, q], hs_dram[bass.ds(row, P), :]).then_inc(h_in[q], 16)

            def store(j, q):
                sp.wait_ge(e_y_sb, j + 1)
                sp.dma_start(ys_dram[bass.ds(j * P, P), :], y[:, q]).then_inc(y_stored[q], 16)

            def step(j, q):
                sp.wait_ge(hT_ps, j)
                load(j + 1, 1 - q)
                store(j - 2, q)

            load(0, 0)
            load(1, 1)
            sp.wait_ge(hT_ps, 1)
            load(2, 0)
            step(2, 0)
            with sp.Fori(0, (NJ - 4) // 2) as i:
                step(2 * i + 3, 1)
                step(2 * i + 4, 0)
            store(NJ - 3, 1)
            store(NJ - 2, 0)
            store(NJ - 1, 1)

            def load_x(b, q):
                sp.dma_start(back[:, q].rearrange("p t c -> p (t c)"), x5_dram[bass.ds(b, 1)].rearrange("o p c -> (o p) c")) \
                  .then_inc(x_back[q], 16)

            def store_out(b, q):
                sp.wait_ge(summed, b + 1)
                sp.dma_start(out[bass.ds(b, 1)].rearrange("o (t p) c -> p (o t) c", p=P), back[:, q]) \
                  .then_inc(out_stored[q], 16)

            load_x(0, 0)
            load_x(1, 1)
            with sp.Fori(0, (B - 2) // 2) as i:
                for q in range(2):
                    store_out(2 * i + q, q)
                    landed(sp, out_stored, 2 * i + q, q)
                    load_x(2 * i + q + 2, q)
            for q in range(2):
                store_out(B - 2 + q, q)
            for q in range(2):
                landed(sp, out_stored, B - 2 + q, q)
                landed(sp, y_stored, NJ - 2 + q, q)

        @block.gpsimd
        def _(pool):
            pool.memset(zeros[:, :], 0.0).then_inc(zeroed, 1)
            pool.wait_ge(zeroed, 1)
            pool.wait_ge(plan_step, N_PLAN)
            for e in range(E):
                pool.indirect_dma_start(hs_dram[:, :], bass.IndirectOffsetOnAxis(ap=pad_at[:, e:e + 1], axis=0),
                                        zeros[:, :], None).then_inc(padded, 16)

            pool.wait_ge(padded, 16 * E)
            for q in range(2):
                landed(pool, y_stored, NJ - 2 + q, q)

            def gather(b, q):
                pool.wait_ge(at_ready, b + 1)
                if not isinstance(b, int) or b:
                    pool.wait_ge(carried, b)
                pool.tensor_tensor(zeros[:, 0:1], table("row"), table("row"), ALU.add).then_inc(carried, 1)
                for i in range(2):
                    for tile in range(TB):
                        pool.indirect_dma_start(yback[:, q, i, tile], None, ys_dram[:, :],
                                                bass.IndirectOffsetOnAxis(ap=at[:, q, i, tile:tile + 1], axis=0)) \
                            .then_inc(gathered[q], 16)

            gather(0, 0)
            gather(1, 1)
            with pool.Fori(0, (B - 2) // 2) as i:
                for q in range(2):
                    gather(2 * i + q + 2, q)
            for q in range(2):
                landed(pool, gathered, B - 2 + q, q, 2 * TB * 16)

        @block.tensor
        def _(pe):
            ident = table("ident")

            def step(j, q, tile_here=True, tile_before=True):
                m, r = j - 1, 1 - q
                if tile_here:
                    landed(pe, h_in, j, q)
                    for k in range(KD):
                        last = pe.transpose(psH[:, k * P:(k + 1) * P], hin[:, q, k * P:(k + 1) * P], ident)
                    last.then_inc(hT_ps, 1)
                if tile_before:
                    pe.wait_ge(inner_sb, m + 1)
                    for c in range(NC):
                        last = pe.transpose(psT[:, c * P:(c + 1) * P], inner[:, r, c * P:(c + 1) * P], ident)
                    last.then_inc(innerT_ps, 1)
                if tile_here:
                    e = pe.value_load(plan[0:1, 0, bass.ds(j, 1)], min_val=0, max_val=E - 1)
                    pe.wait_ge(hT_sb, j + 1)
                    for g in range(2):
                        for k in range(KD):
                            last = pe.matmul(gu[:, q, g], hT[:, q, k],
                                             w13[:, bass.ds(e, 1), k, g * FF:(g + 1) * FF].rearrange("p o n -> p (o n)"),
                                             start=(k == 0), stop=(k == KD - 1))
                    last.then_inc(gu_ps, 1)
                if tile_before:
                    e = pe.value_load(plan[0:1, 0, bass.ds(m, 1)], min_val=0, max_val=E - 1)
                    pe.wait_ge(innerT_sb, m + 1)
                    if not isinstance(m, int) or m >= 2:
                        pe.wait_ge(e_y_sb, m - 1)
                    for c in range(NC):
                        last = pe.matmul(psY[:, r, 0:D], innerT[:, r, c],
                                         w2[:, bass.ds(e, 1), c, :].rearrange("p o n -> p (o n)"), start=(c == 0), stop=(c == NC - 1))
                    last.then_inc(e_y_ps, 1)

            pe.wait_ge(weights_in, 16 * 2 * E)
            pe.wait_ge(plan_step, N_PLAN)
            step(0, 0, tile_before=False)
            step(1, 1)
            step(2, 0)
            with pe.Fori(0, (NJ - 4) // 2) as i:
                step(2 * i + 3, 1)
                step(2 * i + 4, 0)
            step(NJ - 1, 1)
            step(NJ, 0, tile_here=False)

        @block.scalar
        def _(act):
            def step(j, q, tile_here=True, tile_before=True):
                m, r = j - 1, 1 - q
                if tile_here:
                    act.wait_ge(hT_ps, j + 1)
                    act.activation(hT[:, q], psH[:, 0:D].rearrange("p (k c) -> p k c", k=KD), ACT.Copy).then_inc(hT_sb, 1)
                if tile_before:
                    act.wait_ge(innerT_ps, m + 1)
                    act.activation(innerT[:, r], psT[:, :].rearrange("p (k c) -> p k c", k=NC), ACT.Copy).then_inc(innerT_sb, 1)
                if tile_here:
                    act.wait_ge(gu_ps, j + 1)
                    act.activation(th[:, q], gu[:, q, 0], ACT.Tanh, scale=0.5).then_inc(tanh, 1)
                if tile_before:
                    act.wait_ge(e_y_ps, m + 1)
                    if not isinstance(m, int) or m >= 2:
                        landed(act, y_stored, m - 2, r)
                    act.activation(y[:, r], psY[:, r, 0:D], ACT.Copy).then_inc(e_y_sb, 1)

            step(0, 0, tile_before=False)
            step(1, 1)
            step(2, 0)
            with act.Fori(0, (NJ - 4) // 2) as i:
                step(2 * i + 3, 1)
                step(2 * i + 4, 0)
            step(NJ - 1, 1)
            step(NJ, 0, tile_here=False)

        @block.vector
        def _(dve):
            done = [0]

            def plan_link(ins):
                done[0] += 1
                ins.then_inc(plan_step, 1)
                dve.wait_ge(plan_step, done[0])

            plan_link(dve.tensor_scalar(padf[:, :], next_row[:, :], table("row"), None, ALU.add))
            plan_link(dve.tensor_copy(pad_at[:, :], padf[:, :]))
            cnt, tiles, end, start, base, shift, jump = (e8[:, i] for i in range(7))
            first_row = table("first_row")
            plan_link(dve.tensor_tensor(cnt, next_row[:, :], first_row, ALU.subtract))
            plan_link(dve.tensor_scalar(tiles, cnt, 1.0 / P, (P - 1.0) / P - 0.5 + 0.5 / P, ALU.mult, ALU.add))
            plan_link(dve.tensor_scalar(tiles, tiles, MAGIC, None, ALU.add))
            plan_link(dve.tensor_scalar(tiles, tiles, -MAGIC, None, ALU.add))
            src = tiles
            for i, dst in ((1, end), (2, start), (4, end)):
                dve.tensor_copy(dst[:, 0:i], src[:, 0:i])
                plan_link(dve.tensor_tensor(dst[:, i:E], src[:, i:E], src[:, 0:E - i], ALU.add))
                src = dst
            plan_link(dve.tensor_tensor(start, end, tiles, ALU.subtract))
            plan_link(dve.scalar_tensor_tensor(shift, start, float(P), first_row, ALU.mult, ALU.subtract))
            dve.tensor_copy(jump[:, 0:1], shift[:, 0:1])
            dve.tensor_tensor(jump[:, 1:E], shift[:, 1:E], shift[:, 0:E - 1], ALU.subtract)
            tiles_j = table("tiles")[0:1].unsqueeze(2).broadcast_to([1, NJ, E])
            wide = lambda v: v[0:1].unsqueeze(1).broadcast_to([1, NJ, E])
            dve.tensor_tensor(now[:, :, :], tiles_j, wide(start), ALU.is_ge)
            dve.tensor_tensor(upto_e[:, :, :], tiles_j, wide(end), ALU.is_ge)
            plan_link(dve.scalar_tensor_tensor(val[:, :, :], tiles_j, float(P), wide(shift), ALU.mult, ALU.subtract))
            plan_link(dve.tensor_tensor(inside[:, :, :], now[:, :, :], upto_e[:, :, :], ALU.subtract))
            dve.tensor_tensor(val[:, :, :], val[:, :, :], inside[:, :, :], ALU.mult)
            plan_link(dve.tensor_tensor(now[:, :, :], inside[:, :, :], wide(table("expert")), ALU.mult))
            dve.tensor_reduce(f[:, 0], now[:, :, :], AX_X, ALU.add)
            plan_link(dve.tensor_reduce(f[:, 1], val[:, :, :], AX_X, ALU.add))
            plan_link(dve.tensor_copy(plan[:, :, :], f[:, :, :]))
            flat = pos[:, :, :].rearrange("p t i -> p (t i)")
            pairs = lambda v: v.unsqueeze(1).broadcast_to([P, NT * 2, E])
            plan_link(dve.tensor_tensor(past[:, :, :], flat.unsqueeze(2).broadcast_to([P, NT * 2, E]), pairs(first_row),
                                        ALU.is_ge))
            plan_link(dve.tensor_tensor(past[:, :, :], past[:, :, :], pairs(jump), ALU.mult))
            out_flat = out_at[:, :, :].rearrange("p t i -> p (t i)")
            plan_link(dve.tensor_reduce(out_flat, past[:, :, :], AX_X, ALU.add))
            plan_link(dve.tensor_tensor(out_flat, out_flat, flat, ALU.add))
            assert done[0] == N_PLAN, done

            def tile(j, q):
                dve.wait_ge(tanh, j + 1)
                dve.scalar_tensor_tensor(gated[:, q], th[:, q], 1.0, gu[:, q, 0], ALU.add, ALU.mult).then_inc(gated_done, 1)
                dve.wait_ge(gated_done, j + 1)
                if not isinstance(j, int) or j >= 2:
                    dve.wait_ge(innerT_ps, j - 1)
                dve.scalar_tensor_tensor(inner[:, q], gated[:, q], 0.5, gu[:, q, 1], ALU.mult, ALU.mult).then_inc(inner_sb, 1)

            tile(0, 0)
            tile(1, 1)
            with dve.Fori(0, (NJ - 2) // 2) as i:
                tile(2 * i + 2, 0)
                tile(2 * i + 3, 1)

            def copy_at(b, q):
                if not isinstance(b, int):
                    landed(dve, gathered, b - 2, q, 2 * TB * 16)
                dve.tensor_copy(gate[:, q].rearrange("p i t -> p t i"), gates[:, bass.ds(b * TB, TB), :])
                dve.tensor_copy(at[:, q].rearrange("p i t -> p t i"), out_at[:, bass.ds(b * TB, TB), :]).then_inc(at_ready, 1)

            def combine(b, q):
                landed(dve, gathered, b, q, 2 * TB * 16)
                landed(dve, x_back, b, q)
                dve.wait_ge(at_ready, b + 1)
                for i in range(2):
                    for t in range(TB):
                        ins = dve.scalar_tensor_tensor(back[:, q, t], yback[:, q, i, t], gate[:, q, i, t:t + 1], back[:, q, t],
                                                       ALU.mult, ALU.add)
                    ins.then_inc((sum1, summed)[i], 1)
                    dve.wait_ge((sum1, summed)[i], b + 1)

            copy_at(0, 0)
            copy_at(1, 1)
            with dve.Fori(0, (B - 2) // 2) as i:
                for q in range(2):
                    combine(2 * i + q, q)
                    copy_at(2 * i + q + 2, q)
            for q in range(2):
                combine(B - 2 + q, q)


N_PHASES = 25
NORM_PHASES = (1, 5, 10, 12, 17, 22)
ROT_PHASE = 13
N_POOL = 8 + LANES * (2 + NCK)
N_DVE_INIT = 13


def arrays_of(i):
    i = {k: np.asarray(v) for k, v in i.items()}
    mats = [i["L0_attn_Wq"], i["L0_attn_Wk"], i["L0_attn_Wv"], i["L0_attn_Wo"],
            i["L0_xattn_Wq"], i["L0_xattn_Wk"], i["L0_xattn_Wv"], i["L0_xattn_Wo"],
            i["L1_attn_Wq"].T, i["L1_attn_Wk"].T, i["L1_attn_Wv"].T, i["L1_attn_Wo"].T,
            i["L1_xattn_Wq"].T, i["L1_xattn_Wk"].T, i["L1_xattn_Wv"].T, i["L1_xattn_Wo"].T]
    rows_first = lambda m: m.reshape(-1, P, m.shape[-1]).transpose(1, 0, 2)
    o = {
        "x": i["x"],
        "ctxT": i["ctx_1024"].reshape(B, SC, KD, P).transpose(0, 3, 2, 1),
        "mask": i["mask_1x1xSxS2_if1"].reshape(S, SC),
        "proj": np.stack([rows_first(m) for m in mats], axis=1),
        "router": rows_first(i["L1_ffn_router_w"].T),
        "rows": np.stack([i["L0_xattn_bv"], i["L0_xattn_bo"], i["L1_xattn_bv"], i["L1_xattn_bo"]])[None],
        "cols": np.stack([i[n].reshape(KD, P).T for n in ("L0_xattn_bq", "L0_xattn_bk", "L1_xattn_bq", "L1_xattn_bk")],
                         axis=1),
        "fbias": i["L0_ffn_bias"],
        "wscale": i["L0_ffn_weight_scale"],
        "packed": i["L0_ffn_packed_weight"].reshape(64, D),
        "w13": i["L1_ffn_w13"].reshape(E, KD, P, 2 * FF).transpose(0, 2, 1, 3),
        "w2": i["L1_ffn_w2"].reshape(E, FF // P, P, D).transpose(0, 2, 1, 3),
        "tables": np.concatenate(list(shape_tables().values()), axis=1),
    }
    return {k: np.ascontiguousarray(v) for k, v in o.items()}


def kernel(**inputs):
    import concourse.bacc as _bacc
    from concourse.bass_utils import run_bass_kernel_spmd as _run

    arrays = {f"in_{k}": v for k, v in arrays_of(inputs).items()}
    nc = _bacc.Bacc("TRN2", target_bir_lowering=False, num_devices=1)
    aps = {k[3:]: nc.dram_tensor(k, v.shape, mybir.dt.from_np(v.dtype), kind="ExternalInput").ap() for k, v in arrays.items()}
    out = nc.dram_tensor("out", (B, S, D), F32, kind="ExternalOutput").ap()
    mega_kernel(nc, aps, out)
    r = _run(nc, [arrays], core_ids=[0])
    return r.results[0]["out"]
```

```python
from contextlib import ExitStack

import numpy as np

import concourse.bass as bass
from concourse import mybir

F32 = mybir.dt.float32
BF16 = mybir.dt.bfloat16
I32 = mybir.dt.int32
ALU = mybir.AluOpType
ACT = mybir.ActivationFunctionType
AX_X = mybir.AxisListType.X

P = 128
B, S, D = 16, 256, 256
SC = 77
H, DH = 16, 16
KD = D // P
TB = S // P
NT = B * TB
HS = H * SC
LANES = 2
ITERS = B // LANES
EPS_LN = 1e-5

RADIUS = 8
WIN = 32
WQ = WIN - RADIUS
NW = -(-S // WQ)
SPAD = RADIUS + NW * WQ
L0_SCALE = 1.0 / (2.0 * 0.28)
HG = 4
NG = H // HG
NU = NW * NG

NC_CH = -(-HS // P)
CREP = SC + P
CB = NC_CH // 2
VH = 3
DV = DH + 1

CK = 64
NCK = S // CK
NPAIR = H // 2

E, FF = 8, 512
NJ = (2 * B * S) // P + E
CAP = B * S + P
NEG = -1.0e38
BIG = 3.0e38
MAGIC = 12582912.0

(W0Q, W0K, W0V, W0O, X0Q, X0K, X0V, X0O, W1Q, W1K, W1V, W1O, X1Q, X1K, X1V, X1O) = range(16)
NM = 16


def chunk_heads(c):
    return P * c // SC, min(P, HS - P * c)


def shape_tables():
    p = np.arange(P)
    t = {}
    t["ident"] = np.eye(P, dtype=np.float32)
    t["hm4"] = (p[:, None] // DH % HG == np.arange(HG)).astype(np.float32)
    t["hm8"] = (p[:, None] // DH == np.arange(8)).astype(np.float32)
    t["hp4"] = (p[:, None] // (2 * DH) == np.arange(4)).astype(np.float32)
    t["hg2"] = (p[:, None] // (HG * DH) == np.arange(2)).astype(np.float32)
    t["hm2"] = (p[:, None] // DH % 2 == np.arange(2)).astype(np.float32)
    t["rm4"] = (p[:, None] // WIN == np.arange(HG)).astype(np.float32)
    t["rm2"] = (p[:, None] // CK == np.arange(2)).astype(np.float32)
    q, k = (p % WIN)[:, None], np.arange(WIN)[None, :]
    seen = (k <= q) & (k >= q - RADIUS)
    t["band"] = np.where(seen, BIG, NEG).astype(np.float32)
    t["band0"] = np.where(seen & (k >= RADIUS), BIG, NEG).astype(np.float32)
    tok = p[:, None] + P * np.arange(TB)[None, :]
    t["caus"] = np.where(np.arange(SC) <= tok[:, :, None], BIG, NEG).astype(np.float32).reshape(P, -1)
    t["tri"] = ((p % CK)[:, None] <= np.arange(CK)).astype(np.float32)
    vm = np.zeros((P, NC_CH, VH), np.float32)
    for c in range(NC_CH):
        h0, rows = chunk_heads(c)
        head = (P * c + p) // SC
        vm[:, c] = (head[:, None] == h0 + np.arange(VH)) & (p < rows)[:, None]
    t["vmask"] = vm.reshape(P, -1)
    half = DH // 2
    inv = (np.float32(10000.0) ** (-np.arange(half, dtype=np.float32) / np.float32(half))).astype(np.float32)
    ang = (tok.astype(np.float32)[:, :, None] * inv).astype(np.float32)
    c, s = np.cos(ang).astype(np.float32), np.sin(ang).astype(np.float32)
    t["rope"] = np.concatenate([c, -s, s], axis=-1).reshape(P, -1)
    t["power"] = np.full((P, TB), -0.5, np.float32)
    t["ones"] = np.ones((P, P), np.float32)
    t["before"] = (p[:, None] < p[None, :]).astype(np.float32)
    t["desc"] = np.tile(np.arange(E, 0, -1, dtype=np.float32), (P, 1))
    t["row"] = p[:, None].astype(np.float32)
    t["expert"] = np.tile(np.arange(E, dtype=np.float32), (P, 1))
    t["first_row"] = np.tile(CAP * np.arange(E, dtype=np.float32), (P, 1))
    t["tiles"] = np.tile(np.arange(NJ, dtype=np.float32), (P, 1))
    return t


TABLES = {n: a.shape[1] for n, a in shape_tables().items()}
TAB_AT, _n = {}, 0
for _k, _w in TABLES.items():
    TAB_AT[_k] = _n
    _n += _w
TAB_W = _n

SIGNALS = {
    "x_in": 16,
    "ctx_in": 48,
    "ctx_ps": 3,
    "ck_sb": 1,
    "kbd": 4,
    "cv_sb": 2,
    "var": 6,
    "var_eps": 6,
    "rstd": 6,
    "norm": 6,
    "hT_ps": 6,
    "hT": 6,
    "q_ps": 3,
    "q_sb": 3,
    "qbd0": 1,
    "qbd1": 1,
    "hrep1": 2,
    "kv_ps": 2,
    "k_sb": 1,
    "v_sb": 1,
    "v_out": 16,
    "v_win": 16 * HG,
    "vw_sb": 1,
    "s_ps": 5,
    "s_sb": 5,
    "shift": 5,
    "prob": 5,
    "pT_sb0": 1,
    "pT_ps": 4,
    "pT_sb": 4,
    "o_ps": 6,
    "o_sb": 4 + 2,
    "oT_ps": 4,
    "oT_sb": 4,
    "y_ps": 5,
    "x_bo": 2,
    "x_first": 1,
    "qk_ps": 2,
    "rot_a": 2,
    "rot": 2,
    "neg": 2,
    "expn": 2,
    "phi": 2,
    "phiT_ps": 1,
    "phiqT": 1,
    "phiT_sb": 1,
    "qp": 1,
    "v1_ps": 2,
    "v1_bd": 2,
    "v1_sb": 1,
    "a_ps": 1,
    "a_sb": 4,
    "st_ps": NCK - 1,
    "st_sb": NCK - 1,
    "r_ps": 2,
    "r_shift": 1,
    "r_exp": 1,
    "x_done": 1,
    "pos": 1,
    "sorted": 2 * TB * 16,
    "stored": 16,
    "dve_step": 62,
}


STARTS = {"pos": SIGNALS["pos"], "stored": SIGNALS["stored"]}


def mega_kernel(nc, a, out, upto=99, iters=ITERS, dump=None):
    ctx = ExitStack()
    with ctx:
        sb = lambda name, shape, dt=F32: ctx.enter_context(nc.sbuf_tensor(name, shape, dt))
        sem = lambda name: ctx.enter_context(nc.semaphore(name))
        x5_dram = nc.dram_tensor("x5_scratch", [B, P, TB * D], F32).ap()
        v_dram = nc.dram_tensor("v_scratch", [LANES, SPAD, D], F32).ap()
        hs_dram = nc.dram_tensor("sorted_rows", [E * CAP, D], F32).ap()
        tab = sb("tab", [P, TAB_W])
        table = lambda n: tab[:, TAB_AT[n]:TAB_AT[n] + TABLES[n]]
        gates = sb("gates", [P, NT, 2])
        pos = sb("pos", [P, NT, 2])
        next_row = sb("next_row", [P, E])
        build_layers(nc, ctx, a, x5_dram, v_dram, hs_dram, tab, table, gates, pos, next_row, iters, upto, dump)
        if dump is None:
            build_experts(nc, a, x5_dram, hs_dram, tab, table, gates, pos, next_row, out)


def build_layers(nc, held, a, x5_dram, v_dram, hs_dram, tab, table, gates, pos, next_row, iters, upto, dump):
    with ExitStack() as ctx:
        sb = lambda name, shape, dt=F32: ctx.enter_context(nc.sbuf_tensor(name, shape, dt))
        sem = lambda name: held.enter_context(nc.semaphore(name))
        w = sb("w", [P, NM, KD, D])
        wr = sb("wr", [P, KD, E])
        ternT = sb("ternT", [P, KD, D], BF16)
        bo = sb("bo", [P, 2, D])
        cols = sb("cols", [P, 6, KD])
        fbias = sb("fbias", [P, D])
        wscale = sb("wscale", [P, 1])
        wscale127 = sb("wscale127", [P, 1])
        bound0 = sb("bound0", [P, TB, SC])
        identb = sb("identb", [P, P], BF16)
        packed = sb("packed", [64, D], I32)
        maski = sb("maski", [P, TB, SC], I32)

        L = []
        for n in range(LANES):
            t = {}
            for name, shape in (("xin", [P, TB, D]), ("x", [P, TB, D]), ("h", [P, TB, D]), ("h6", [P, TB, D]),
                                ("hT", [P, KD, SPAD]), ("kT", [P, KD, SPAD]), ("kg", [P, KD, 2, SPAD]),
                                ("qT", [P, KD, SPAD]), ("spread", [P, 3072]),
                                ("crep", [P, KD, CREP]), ("ck", [P, 2, KD, SC]), ("kbd", [P, 2, KD, 8, SC]),
                                ("vbd", [P, 2, NC_CH, VH, DV]), ("o", [P, TB, D]), ("oT", [P, KD, S]),
                                ("v1bd", [P, NCK, NPAIR, 2, DV]), ("v1", [P, TB, H, DV]), ("work", [P, 5632]),
                                ("small", [P, 512])):
                t[name] = sb(f"{name}{n}", shape)
            t["posi"] = sb(f"posi{n}", [P, 2, TB], I32)
            wk = t["work"]
            cut = lambda lo, n_, pat, wk=wk, **k: wk[:, lo:lo + n_].rearrange(pat, **k)
            t["vw"] = cut(0, NW * D, "p (j c) -> p j c", j=NW)
            t["qbd"] = t["spread"][:, 0:KD * NW * P].rearrange("p (k j h q) -> p k j h q", k=KD, j=NW, h=HG)
            t["hrep1"] = t["spread"][:, 0:KD * NCK * P].rearrange("p (k c m) -> p k c m", k=KD, c=NCK)
            t["qp"] = t["spread"][:, KD * NCK * P:KD * NCK * P + KD * NCK * 4 * CK] \
                .rearrange("p (k c r q) -> p k c r q", k=KD, c=NCK, r=4)
            t["hq"] = wk[:, 5120:5376].bitcast(BF16).rearrange("p (t c) -> p t c", t=TB)
            t["hTb"] = wk[:, 5376:5632].bitcast(BF16).rearrange("p (k c) -> p k c", k=KD)
            t["s0"] = cut(2816, NU * WIN, "p (u k) -> p u k", u=NU)
            t["pT0"] = cut(2816 + 1408, NU * WIN, "p (u k) -> p u k", u=NU)
            t["s"] = cut(0, TB * HS, "p (t h s) -> p t h s", t=TB, h=H)
            t["sflat"] = cut(0, TB * HS, "p (t n) -> p t n", t=TB)
            t["pT"] = cut(2464, TB * NC_CH * P, "p (t c q) -> p t c q", t=TB, c=NC_CH)
            t["rotA"] = cut(0, 1024, "p (t c) -> p t c", t=TB)
            t["rotB"] = cut(1024, 1024, "p (t c) -> p t c", t=TB)
            t["at"] = cut(0, 2048, "p (u q) -> p u q", q=CK)
            t["phi"] = cut(2048, 1024, "p (t c) -> p t c", t=TB)
            t["k2"] = cut(3072, 1024, "p (k c h q) -> p k c h q", k=KD, c=NCK, h=2)
            t["st"] = cut(4096, 816, "p (c n) -> p c n", c=NCK - 1)
            t["ps"] = ctx.enter_context(nc.psum_tensor(f"ps{n}", [P, 4, 512], F32))
            t["sem"] = {k: held.enter_context(nc.semaphore(f"{k}_{n}")) for k in SIGNALS}
            L.append(t)

        pads_out = sem("pads_out")
        consts_in = sem("consts_in")
        init_pool = sem("init_pool")
        init_dve = sem("init_dve")
        init_pe = sem("init_pe")
        N_CONST = 12

        def after(eng, t, name, it, k):
            eng.wait_ge(t["sem"][name], it * SIGNALS[name] + k + STARTS.get(name, 0))

        def windows(x, half):
            return bass.AP(x[:, :, :].tensor, x[:, half, 0:1].offset, [x[:, :, :].ap[0], [WQ, NW], [0, HG], [1, WIN]])

        def carry(eng, t, col):
            eng.tensor_tensor(t["small"][:, col:col + 1], table("row"), table("row"), ALU.add)

        def lane_psum(t, bank, lo, hi):
            return t["ps"][:, bank, lo:hi]

        def interleave(programs):
            live = list(programs)
            n = 0
            while live:
                live = [g for g in live if next(g, "end") != "end"]
                n += 1
                if n >= upto:
                    break

        programs = ctx.enter_context(ExitStack())
        block = programs.enter_context(nc.Block())

        @block.sync
        def _(sp):
            for dst, src in (
                (tab[:, :], a["tables"]), (w[:, :, :, :], a["proj"]), (wr[:, :, :], a["router"]),
                (bo[:, :, :], a["bo"].partition_broadcast(P)), (cols[:, :, :], a["cols"]),
                (fbias[:, :], a["fbias"].partition_broadcast(P)),
                (wscale[:, :], a["wscale"].partition_broadcast(P)), (packed[:, :], a["packed"]),
                (maski[:, 0, :], a["mask"][0:P, :]), (maski[:, 1, :], a["mask"][P:2 * P, :]),
            ):
                sp.dma_start(dst, src).then_inc(consts_in, 16)

            def load(n, batch, it, first):
                t = L[n]
                if not first:
                    after(sp, t, "x_first", it, 1)
                    after(sp, t, "cv_sb", it, 2)
                    after(sp, t, "ctx_ps", it, 1)
                for r, (lo, n_c) in enumerate(((0, SC), (SC, SC), (2 * SC, CREP - 2 * SC))):
                    sp.dma_start(t["crep"][:, :, lo:lo + n_c], a["ctxT"][bass.ds(batch, 1), :, :, 0:n_c]
                                 .rearrange("o p k s -> (o p) k s")).then_inc(t["sem"]["ctx_in"], 16)
                sp.dma_start(t["xin"][:, :, :], a["x"][bass.ds(batch, 1)].rearrange("o (t p) c -> p (o t) c", p=P)) \
                  .then_inc(t["sem"]["x_in"], 16)

            sp.wait_ge(init_pool, N_POOL)
            for n in range(LANES):
                for lo, hi in ((0, RADIUS), (RADIUS + S, SPAD)):
                    sp.dma_start(v_dram[n, lo:hi, :], L[n]["hT"][0:hi - lo, 0, 0:D]).then_inc(pads_out, 16)
            sp.wait_ge(pads_out, 16 * 2 * LANES)

            def value_windows(n, it):
                t = L[n]
                after(sp, t, "v_sb", it, 1)
                sp.dma_start(v_dram[n, RADIUS:RADIUS + S, :].rearrange("(t p) c -> p t c", p=P), t["o"][:, :, :]) \
                  .then_inc(t["sem"]["v_out"], 16)
                after(sp, t, "v_out", it, 16)
                rows = v_dram[n, 0:WIN, :]
                for h in range(HG):
                    sp.dma_start(t["vw"][h * WIN:(h + 1) * WIN], bass.AP(rows.tensor, rows.offset, [[D, WIN], [WQ * D, NW], [1, D]])) \
                      .then_inc(t["sem"]["v_win"], 16)

            def store(n, batch, it):
                t = L[n]
                after(sp, t, "x_done", it, 1)
                sp.dma_start(x5_dram[bass.ds(batch, 1)].rearrange("o p c -> (o p) c"),
                             t["x"][:, :, :].rearrange("p t c -> p (t c)")).then_inc(t["sem"]["stored"], 16)

            for n in range(LANES):
                load(n, n, 0, True)
            if iters > 1:
                with sp.Fori(0, iters - 1) as it:
                    for n in range(LANES):
                        value_windows(n, it)
                    for n in range(LANES):
                        load(n, it * LANES + LANES + n, it, False)
                    for n in range(LANES):
                        store(n, it * LANES + n, it)
            for n in range(LANES):
                value_windows(n, iters - 1)
            if upto > 90:
                for n in range(LANES):
                    store(n, (iters - 1) * LANES + n, iters - 1)
                for n in range(LANES):
                    sp.wait_ge(L[n]["sem"]["stored"], SIGNALS["stored"] * iters + STARTS["stored"])

        @block.gpsimd
        def _(pool):
            for t in L:
                for k, (name, start) in enumerate(STARTS.items()):
                    pool.memset(t["small"][:, 505 + k:506 + k], 0.0).then_inc(t["sem"][name], start)
                pool.memset(t["qT"][:, :, :], 0.0).then_inc(init_pool, 1)
                pool.memset(t["kg"][:, :, :, :], 0.0).then_inc(init_pool, 1)
                pool.memset(t["hT"][:, :, :], 0.0).then_inc(init_pool, 1)
                pool.memset(t["v1"][:, :, :, :], 1.0).then_inc(init_pool, 1)
            pool.wait_ge(consts_in, 16 * 10)
            for t in L:
                for layer in range(2):
                    pool.tensor_copy(t["vbd"][:, layer, :, :, DH:DV],
                                     table("vmask").rearrange("p (c h) -> p c h", h=VH).unsqueeze(3)).then_inc(init_pool, 1)
                for c in range(NCK):
                    pool.tensor_copy(t["v1bd"][:, c, :, :, DH:DV],
                                     table("rm2").unsqueeze(1).broadcast_to([P, NPAIR, 2]).unsqueeze(3)).then_inc(init_pool, 1)

            def lane(n, it):
                t = L[n]
                after(pool, t, "ck_sb", it, 1)
                for layer in range(2):
                    for half in range(KD):
                        pool.tensor_tensor(
                            t["kbd"][:, layer, half], t["ck"][:, layer, half].unsqueeze(1).broadcast_to([P, 8, SC]),
                            table("hm8").unsqueeze(2).broadcast_to([P, 8, SC]), ALU.mult) \
                            .then_inc(t["sem"]["kbd"], 1)
                for phase in range(N_PHASES):
                    if phase in NORM_PHASES:
                        k = NORM_PHASES.index(phase) + 1
                        after(pool, t, "var", it, k)
                        carry(pool, t, 450 + phase)
                        rstd = t["small"][:, 20:22]
                        pool.tensor_scalar(rstd.unsqueeze(2),
                                           t["small"][:, 16:20].rearrange("p (t m) -> p t m", m=2)[:, :, 1:2],
                                           EPS_LN, None, ALU.add).then_inc(t["sem"]["var_eps"], 1)
                        after(pool, t, "var_eps", it, k)
                        pool.tensor_tensor(rstd, rstd, table("power"), ALU.pow).then_inc(t["sem"]["rstd"], 1)
                    if phase in BIAS_PHASES:
                        i = BIAS_PHASES.index(phase)
                        after(pool, t, "norm", it, (2, 5)[i])
                        pool.tensor_tensor(t["x"][:, :, :], t["x"][:, :, :], bo[:, i].unsqueeze(1).broadcast_to([P, TB, D]),
                                           ALU.add).then_inc(t["sem"]["x_bo"], 1)
                    if phase == QKV_PHASE:
                        after(pool, t, "q_sb", it, 1)
                        pool.tensor_tensor(t["qbd"][:, 0], windows(t["qT"], 0),
                                           table("hm4").unsqueeze(1).unsqueeze(3).broadcast_to([P, NW, HG, WIN]), ALU.mult) \
                            .then_inc(t["sem"]["qbd0"], 1)
                    if phase == ROT_PHASE:
                        after(pool, t, "hT", it, 4)
                        carry(pool, t, 450 + phase)
                        for half in range(KD):
                            pool.tensor_copy(t["hrep1"][:, half].rearrange("p c (h q) -> p c h q", h=2),
                                             t["hT"][:, half, RADIUS:RADIUS + S].rearrange("p (c q) -> p c q", c=NCK)
                                             .unsqueeze(2).broadcast_to([P, NCK, 2, CK])).then_inc(t["sem"]["hrep1"], 1)
                        for tile in range(TB):
                            after(pool, t, "rot_a", it, tile + 1)
                            pool.tensor_tensor(t["rotA"][:, tile], t["rotA"][:, tile], t["rotB"][:, tile], ALU.add) \
                                .then_inc(t["sem"]["rot"], 1)
                    if phase == N_PHASES - 1:
                        after(pool, t, "pos", it, 1)
                        carry(pool, t, 450 + phase)
                        for i in range(2):
                            for tile in range(TB):
                                pool.indirect_dma_start(
                                    hs_dram[:, :], bass.IndirectOffsetOnAxis(ap=t["posi"][:, i, tile:tile + 1], axis=0),
                                    t["h6"][:, tile, :], None).then_inc(t["sem"]["sorted"], 16)
                    yield

            with pool.Fori(0, iters) as it:
                interleave([lane(n, it) for n in range(LANES)])
                if upto > 90:
                    for t in L:
                        after(pool, t, "sorted", it, SIGNALS["sorted"])

        @block.scalar
        def _(act):
            act.wait_ge(consts_in, 16 * 10)
            act.wait_ge(init_pool, N_POOL)

            def norm_T(t, it, k, dst, lo):
                yield
                after(act, t, "hT_ps", it, k)
                act.activation(dst[:, :, lo:lo + S], t["ps"][:, 0, :].rearrange("p (k c) -> p k c", k=KD), ACT.Copy) \
                    .then_inc(t["sem"]["hT"], 1)

            def out_T(t, it, k, bias):
                after(act, t, "oT_ps", it, k)
                src = t["ps"][:, 0, :].rearrange("p (k c) -> p k c", k=KD)
                if bias is None:
                    last = act.activation(t["oT"][:, :, :], src, ACT.Copy)
                else:
                    for half in range(KD):
                        last = act.activation(t["oT"][:, half], src[:, half], ACT.Identity, bias=cols[:, bias, half:half + 1])
                last.then_inc(t["sem"]["oT_sb"], 1)

            def lane(n, it):
                t = L[n]
                s = t["sem"]
                after(act, t, "ctx_ps", it, 1)
                for layer in range(2):
                    for half in range(KD):
                        i = (layer * KD + half) * SC
                        last = act.activation(t["ck"][:, layer, half], lane_psum(t, 2, i, i + SC), ACT.Identity,
                                              bias=cols[:, 2 * layer + 1, half:half + 1])
                last.then_inc(s["ck_sb"], 1)
                yield
                yield from norm_T(t, it, 1, t["hT"], RADIUS)
                yield
                after(act, t, "q_ps", it, 1)
                act.activation(t["qT"][:, :, RADIUS:RADIUS + S], lane_psum(t, 1, 0, 512).rearrange("p (k c) -> p k c", k=KD),
                               ACT.Copy).then_inc(s["q_sb"], 1)
                after(act, t, "kv_ps", it, 1)
                for g in range(2):
                    last = act.activation(t["kg"][:, :, g, RADIUS:RADIUS + S],
                                          lane_psum(t, 2, 0, 512).rearrange("p (k c) -> p k c", k=KD), ACT.Copy,
                                          scale=table("hg2")[:, g:g + 1])
                last.then_inc(s["k_sb"], 1)
                after(act, t, "kv_ps", it, 2)
                act.activation(t["o"][:, :, :], lane_psum(t, 3, 0, 512).rearrange("p (t c) -> p t c", t=TB), ACT.Copy) \
                    .then_inc(s["v_sb"], 1)
                yield
                after(act, t, "shift", it, 1)
                act.activation(t["s0"], t["s0"], ACT.Exp, scale=L0_SCALE).then_inc(s["prob"], 1)
                yield
                after(act, t, "oT_ps", it, 1)
                act.activation(t["oT"][:, :, :], t["ps"][:, 0:2, 0:S], ACT.Copy).then_inc(s["oT_sb"], 1)
                yield

                def cross(i, sub):
                    yield from norm_T(t, it, sub + 1, t["hT"], RADIUS)
                    yield
                    after(act, t, "q_ps", it, 2 + i)
                    for half in range(KD):
                        last = act.activation(t["kT"][:, half, RADIUS:RADIUS + S], lane_psum(t, 1, half * S, half * S + S),
                                              ACT.Identity, bias=cols[:, 2 * i, half:half + 1])
                    last.then_inc(s["q_sb"], 1)
                    yield
                    yield
                    for tile in range(TB):
                        after(act, t, "shift", it, 2 + TB * i + tile)
                        act.activation(t["sflat"][:, tile], t["sflat"][:, tile], ACT.Exp, scale=DH ** -0.5) \
                            .then_inc(s["prob"], 1)
                    yield
                    for tile in range(TB):
                        after(act, t, "pT_ps", it, TB * i + tile + 1)
                        rest = HS - (NC_CH - 1) * P
                        flat = t["pT"][:, tile].rearrange("p c q -> p (c q)")
                        act.activation(flat[:, 0:4 * P], lane_psum(t, 0, 0, 512), ACT.Copy)
                        act.activation(flat[:, 4 * P:8 * P], lane_psum(t, 1, 0, 512), ACT.Copy)
                        act.activation(flat[:, 8 * P:9 * P], lane_psum(t, 2, 0, P), ACT.Copy)
                        act.activation(flat[0:rest, 9 * P:10 * P], t["ps"][0:rest, 2, P:2 * P], ACT.Copy) \
                            .then_inc(s["pT_sb"], 1)
                        yield
                        yield
                    out_T(t, it, 2 if i == 0 else 4, 4 + i)
                    yield

                yield from cross(0, 1)
                yield
                yield
                yield
                yield from norm_T(t, it, 4, t["hT"], RADIUS)
                yield
                for tile in range(TB):
                    after(act, t, "neg", it, tile + 1)
                    act.activation(t["rotB"][:, tile], t["rotB"][:, tile], ACT.Exp).then_inc(s["expn"], 1)
                yield
                for j in range(TB):
                    after(act, t, "v1_bd", it, j + 1)
                    for r in range(2):
                        src = t["ps"][r * CK:(r + 1) * CK, 1 + j, r * D:(r + 1) * D]
                        last = act.activation(t["v1"][r * CK:(r + 1) * CK, j, :, 0:DH],
                                              src.rearrange("p (h d) -> p h d", h=H), ACT.Copy)
                last.then_inc(s["v1_sb"], 1)
                after(act, t, "phiT_ps", it, 1)
                act.activation(t["kT"][:, :, RADIUS:RADIUS + S], lane_psum(t, 0, 0, 512).rearrange("p (k c) -> p k c", k=KD),
                               ACT.Copy).then_inc(s["phiqT"], 1)
                for h in range(2):
                    last = act.activation(t["k2"][:, :, :, h, :],
                                          lane_psum(t, 3, 0, 512).rearrange("p (k c q) -> p k c q", k=KD, c=NCK), ACT.Copy, scale=table("hm2")[:, h:h + 1])
                last.then_inc(s["phiT_sb"], 1)
                yield
                yield
                yield
                yield
                out_T(t, it, 3, None)
                yield
                yield from cross(1, 4)
                yield from norm_T(t, it, 6, t["hT"], RADIUS)
                yield
                after(act, t, "r_shift", it, 1)
                act.activation(t["small"][:, 320:336], t["small"][:, 320:336], ACT.Exp).then_inc(s["r_exp"], 1)
                yield
                yield

            with act.Fori(0, iters) as it:
                interleave([lane(n, it) for n in range(LANES)])

        @block.tensor
        def _(pe):
            pe.wait_ge(consts_in, 16 * 10)
            pe.wait_ge(init_pool, N_POOL)
            pe.wait_ge(init_dve, N_DVE_INIT)
            ident = table("ident")

            t0 = L[0]
            tern = t0["work"][0:64, 0:512].bitcast(BF16)
            psb = t0["ps"][:, 0, :].bitcast(BF16)
            for shift in range(4):
                for k in range(KD):
                    last = pe.transpose(psb[:, k * D + shift * 64:k * D + shift * 64 + 64],
                                        tern[:, shift * D + k * P:shift * D + k * P + P], identb[0:64, 0:64])
            last.then_inc(init_pe, 1)
            pe.wait_ge(init_dve, N_DVE_INIT + 1)

            def norm_T(t, it, k, src):
                yield
                after(pe, t, "norm", it, k)
                for kk in range(KD):
                    for tile in range(TB):
                        last = pe.transpose(lane_psum(t, 0, kk * S + tile * P, kk * S + tile * P + P),
                                            src[:, tile, kk * P:(kk + 1) * P], ident)
                last.then_inc(t["sem"]["hT_ps"], 1)

            def out_T(t, it, k):
                for kk in range(KD):
                    for tile in range(TB):
                        last = pe.transpose(lane_psum(t, 0, kk * S + tile * P, kk * S + tile * P + P),
                                            t["o"][:, tile, kk * P:(kk + 1) * P], ident)
                last.then_inc(t["sem"]["oT_ps"], 1)

            def out_proj(t, it, k, bank, mat):
                after(pe, t, "oT_sb", it, k)
                for tile in range(TB):
                    for half in range(KD):
                        last = pe.matmul(lane_psum(t, bank, tile * D, tile * D + D), t["oT"][:, half, tile * P:(tile + 1) * P],
                                         w[:, mat, half, :], start=(half == 0), stop=(half == KD - 1))
                last.then_inc(t["sem"]["y_ps"], 1)

            def feature_proj(t, bank, mat, hT):
                for half in range(KD):
                    for k in range(KD):
                        last = pe.matmul(lane_psum(t, bank, half * S, half * S + S), w[:, mat, k, half * P:(half + 1) * P],
                                         hT[:, k, RADIUS:RADIUS + S], start=(k == 0), stop=(k == KD - 1))
                return last

            def lane(n, it):
                t = L[n]
                s = t["sem"]
                hT = t["hT"]
                after(pe, t, "pos", it, 0)
                after(pe, t, "ctx_in", it, 48)
                for layer in range(2):
                    for half in range(KD):
                        i = (layer * KD + half) * SC
                        for k in range(KD):
                            last = pe.matmul(lane_psum(t, 2, i, i + SC), w[:, (X0K, X1K)[layer], k, half * P:(half + 1) * P],
                                             t["crep"][:, k, 0:SC], start=(k == 0), stop=(k == KD - 1))
                last.then_inc(s["ctx_ps"], 1)
                for c in range(NC_CH):
                    h0, n_rows = chunk_heads(c)
                    nh = min(VH, H - h0)
                    off = P * c % SC
                    at = c % CB * 2 * VH * DH
                    dst = t["ps"][0:n_rows, (3, 1)[c // CB], at:at + 2 * VH * DH].rearrange("p (l n) -> p l n", l=2)
                    for k in range(KD):
                        last = pe.matmul(dst[:, :, 0:nh * DH], t["crep"][:, k, off:off + n_rows],
                                         w[:, X0V:X1V + 1:X1V - X0V, k, h0 * DH:(h0 + nh) * DH],
                                         start=(k == 0), stop=(k == KD - 1))
                    if c % CB == CB - 1:
                        last.then_inc(s["ctx_ps"], 1)
                yield
                yield from norm_T(t, it, 1, t["h"])
                yield
                after(pe, t, "hT", it, 1)
                after(pe, t, "cv_sb", it, 2)
                feature_proj(t, 1, W0Q, hT).then_inc(s["q_ps"], 1)
                after(pe, t, "ck_sb", it, 1)
                feature_proj(t, 2, W0K, hT).then_inc(s["kv_ps"], 1)
                for tile in range(TB):
                    for k in range(KD):
                        last = pe.matmul(lane_psum(t, 3, tile * D, tile * D + D), hT[:, k, RADIUS + tile * P:RADIUS + (tile + 1) * P],
                                         w[:, W0V, k, :], start=(k == 0), stop=(k == KD - 1))
                last.then_inc(s["kv_ps"], 1)
                yield
                after(pe, t, "qbd0", it, 1)
                after(pe, t, "qbd1", it, 1)
                after(pe, t, "k_sb", it, 1)
                for u in range(NW * KD):
                    j, half = u // KD, u % KD
                    last = pe.matmul(lane_psum(t, u // 8, u % 8 * 2 * WIN, (u % 8 + 1) * 2 * WIN),
                                     t["qbd"][:, half, j].rearrange("p h q -> p (h q)"), t["kg"][:, half, :, j * WQ:j * WQ + WIN],
                                     start=True, stop=True)
                last.then_inc(s["s_ps"], 1)
                yield
                after(pe, t, "pT_sb0", it, 1)
                after(pe, t, "vw_sb", it, 1)
                for j in range(NW):
                    for g in range(NG):
                        r = 64 * (g % 2)
                        last = pe.matmul(t["ps"][r:r + 64, g // 2, j * WQ:(j + 1) * WQ], t["vw"][:, j, g * 64:(g + 1) * 64],
                                         t["pT0"][:, j * NG + g, RADIUS:WIN], start=True, stop=True)
                last.then_inc(s["oT_ps"], 1)
                out_proj(t, it, 1, 2, W0O)
                yield

                def cross(i, sub):
                    yield from norm_T(t, it, sub + 1, t["h"])
                    yield
                    after(pe, t, "hT", it, sub + 1)
                    feature_proj(t, 1, (X0Q, X1Q)[i], hT).then_inc(s["q_ps"], 1)
                    yield
                    after(pe, t, "q_sb", it, 2 + i)
                    after(pe, t, "kbd", it, 4)
                    for tile in range(TB):
                        if tile:
                            after(pe, t, "s_sb", it, 1 + TB * i + tile)
                        for g in range(4):
                            last = pe.matmul(lane_psum(t, g, 0, 4 * SC),
                                             t["kT"][:, g // 2, RADIUS + tile * P:RADIUS + (tile + 1) * P],
                                             t["kbd"][:, i, g // 2, g % 2 * 4:g % 2 * 4 + 4, :], start=True, stop=True)
                        last.then_inc(s["s_ps"], 1)
                        yield
                    for tile in range(TB):
                        after(pe, t, "prob", it, 2 + TB * i + tile)
                        if tile == 0:
                            after(pe, t, "s_sb", it, 1 + TB * (i + 1))
                        else:
                            after(pe, t, "pT_sb", it, TB * i + tile)
                        for c in range(NC_CH):
                            n_rows = chunk_heads(c)[1]
                            last = pe.transpose(t["ps"][0:n_rows, c // 4, c % 4 * P:c % 4 * P + P],
                                                t["sflat"][:, tile, c * P:c * P + n_rows], ident)
                        last.then_inc(s["pT_ps"], 1)
                        yield
                        after(pe, t, "pT_sb", it, TB * i + tile + 1)
                        if tile:
                            after(pe, t, "o_sb", it, (0 if i == 0 else 4) + tile)
                        for c in range(NC_CH):
                            h0, n_rows = chunk_heads(c)
                            nh = min(VH, H - h0)
                            last = pe.matmul(lane_psum(t, 3, h0 * DV, (h0 + nh) * DV), t["pT"][0:n_rows, tile, c, :],
                                             t["vbd"][0:n_rows, i, c, 0:nh, :], start=(c == 0), stop=(c == NC_CH - 1),
                                             skip_group_check=True)
                        last.then_inc(s["o_ps"], 1)
                        yield
                    after(pe, t, "o_sb", it, (2 if i == 0 else 6))
                    out_T(t, it, 0)
                    out_proj(t, it, (2 if i == 0 else 4), 1, (X0O, X1O)[i])
                    yield

                after(pe, t, "cv_sb", it, 2)
                yield from cross(0, 1)
                yield
                after(pe, t, "norm", it, 3)
                psb = t["ps"][:, 0, :].bitcast(BF16)
                for kk in range(KD):
                    for tile in range(TB):
                        last = pe.transpose(psb[:, kk * S + tile * P:kk * S + tile * P + P],
                                            t["hq"][:, tile, kk * P:(kk + 1) * P], identb[:, :])
                last.then_inc(s["hT_ps"], 1)
                yield
                after(pe, t, "hT", it, 3)
                for tile in range(TB):
                    for k in range(KD):
                        last = pe.matmul(lane_psum(t, 1, tile * D, tile * D + D), t["hTb"][:, k, tile * P:(tile + 1) * P],
                                         ternT[:, k, :], start=(k == 0), stop=(k == KD - 1))
                last.then_inc(s["y_ps"], 1)
                yield
                yield from norm_T(t, it, 4, t["h"])
                yield
                after(pe, t, "hT", it, 4)
                for tile in range(TB):
                    for k in range(KD):
                        last = pe.matmul(lane_psum(t, 1 + tile, 0, 512), hT[:, k, RADIUS + tile * P:RADIUS + (tile + 1) * P],
                                         w[:, W1Q:W1K + 1, k, :], start=(k == 0), stop=(k == KD - 1))
                    last.then_inc(s["qk_ps"], 1)
                yield
                after(pe, t, "rot_a", it, 2)
                after(pe, t, "hrep1", it, 2)
                for c in range(NCK):
                    for k in range(KD):
                        last = pe.matmul(lane_psum(t, 1 + c // 2, c % 2 * D, c % 2 * D + D), t["hrep1"][:, k, c], w[:, W1V, k, :],
                                         start=(k == 0), stop=(k == KD - 1))
                    if c % 2:
                        last.then_inc(s["v1_ps"], 1)
                after(pe, t, "phi", it, 2)
                for part, bank in ((0, 0), (1, 3)):
                    for kk in range(KD):
                        for tile in range(TB):
                            last = pe.transpose(lane_psum(t, bank, kk * S + tile * P, kk * S + tile * P + P),
                                                t["phi"][:, tile, part * D + kk * P:part * D + (kk + 1) * P], ident)
                last.then_inc(s["phiT_ps"], 1)
                yield
                after(pe, t, "phiT_sb", it, 1)
                after(pe, t, "v1_sb", it, 1)
                after(pe, t, "v1_bd", it, 2)
                after(pe, t, "qp", it, 1)
                for c in range(NCK):
                    for half in range(KD):
                        last = pe.matmul(lane_psum(t, c, half * 4 * CK, (half + 1) * 4 * CK),
                                         t["k2"][:, half, c].rearrange("p h q -> p (h q)"),
                                         t["qp"][:, half, c].rearrange("p r q -> p (r q)"), start=True, stop=True)
                last.then_inc(s["a_ps"], 1)
                yield
                for c in range(1, NCK):
                    after(pe, t, "a_sb", it, c)
                    for half in range(KD):
                        dst = lane_psum(t, c - 1, half * 8 * DV, (half + 1) * 8 * DV)
                        col = slice(D + half * P, D + (half + 1) * P)
                        hh = slice(half * 8, half * 8 + 8)
                        full = c // 2
                        if full:
                            last = pe.matmul(dst, t["phi"][:, 0, col], t["v1"][:, 0, hh, :], start=True, stop=(c % 2 == 0))
                        if c % 2:
                            last = pe.matmul(dst, t["phi"][0:CK, full, col], t["v1"][0:CK, full, hh, :],
                                             start=(full == 0), stop=True)
                    last.then_inc(s["st_ps"], 1)
                yield
                after(pe, t, "a_sb", it, 4)
                for c in range(NCK):
                    bank, r = (3, 0)[c // 2], CK * (c % 2)
                    if c:
                        after(pe, t, "st_sb", it, c)
                    for pr in range(NPAIR):
                        last = pe.matmul(t["ps"][r:r + CK, bank, pr * 2 * DV:(pr + 1) * 2 * DV],
                                         t["at"][:, c * NPAIR + pr, :], t["v1bd"][:, c, pr], start=(pr == 0),
                                         stop=(pr == NPAIR - 1 and c == 0), skip_group_check=True)
                    if c:
                        for half in range(KD):
                            last = pe.matmul(t["ps"][r:r + CK, bank, half * 8 * DV:(half + 1) * 8 * DV],
                                             t["kT"][:, half, RADIUS + c * CK:RADIUS + (c + 1) * CK],
                                             t["st"][:, c - 1, half * 8 * DV:(half + 1) * 8 * DV], start=False,
                                             stop=(half == KD - 1), skip_group_check=True)
                    if c % 2:
                        last.then_inc(s["o_ps"], 1)
                yield
                after(pe, t, "o_sb", it, 4)
                out_T(t, it, 0)
                out_proj(t, it, 3, 1, W1O)
                yield
                yield from cross(1, 4)
                yield from norm_T(t, it, 6, t["h6"])
                yield
                after(pe, t, "hT", it, 6)
                for tile in range(TB):
                    for k in range(KD):
                        last = pe.matmul(lane_psum(t, 1, tile * E, (tile + 1) * E),
                                         hT[:, k, RADIUS + tile * P:RADIUS + (tile + 1) * P], wr[:, k, :],
                                         start=(k == 0), stop=(k == KD - 1))
                last.then_inc(s["r_ps"], 1)
                yield
                after(pe, t, "x_done", it, 1)
                pe.matmul(lane_psum(t, 2, 0, TB * E), table("before"), t["small"][:, 402:402 + TB * E], start=True, stop=True)
                pe.matmul(lane_psum(t, 2, TB * E, 2 * TB * E), table("ones"), t["small"][:, 402:402 + TB * E],
                          start=True, stop=True).then_inc(s["r_ps"], 1)
                yield

            with pe.Fori(0, iters) as it:
                interleave([lane(n, it) for n in range(LANES)])

        @block.vector
        def _(dve):
            dve.wait_ge(consts_in, 16 * 10)
            steps = [0]

            def init(ins):
                steps[0] += 1
                ins.then_inc(init_dve, 1)
                dve.wait_ge(init_dve, steps[0])

            init(dve.tensor_copy(identb[:, :], table("ident")))
            init(dve.tensor_copy(next_row[:, :], table("first_row")))
            maskf = L[0]["work"][:, 1024:1024 + TB * SC].rearrange("p (t s) -> p t s", t=TB)
            init(dve.tensor_copy(maskf, maski[:, :, :]))
            init(dve.tensor_scalar(maskf, maskf, 0.0, None, ALU.is_equal))
            init(dve.tensor_scalar(bound0[:, :, :], maskf, -BIG, BIG, ALU.mult, ALU.add))
            init(dve.tensor_scalar(maskf, maskf, -1e10 * DH ** 0.5, None, ALU.mult))
            init(dve.tensor_tensor(bound0[:, :, :], bound0[:, :, :], maskf, ALU.add))
            init(dve.tensor_scalar(wscale127[:, :], wscale[:, :], 1.0 / 127.0, None, ALU.mult))
            codes = L[0]["work"][0:64, 2048:3072].bitcast(I32)
            for shift in range(4):
                init(dve.tensor_scalar(codes[:, shift * D:(shift + 1) * D], packed[:, :], 2 * shift, 3,
                                       ALU.logical_shift_right, ALU.bitwise_and))
            tern = L[0]["work"][0:64, 0:512].bitcast(BF16)
            init(dve.tensor_scalar(tern, codes, -1.0, None, ALU.add))
            assert steps[0] == N_DVE_INIT, steps
            dve.wait_ge(init_pe, 1)
            init(dve.tensor_copy(ternT[:, :, :], L[0]["ps"][:, 0, :].bitcast(BF16)[:, 0:KD * D]
                                 .rearrange("p (k c) -> p k c", k=KD)))
            counts = [[0] for _ in L]
            norms = [0] * LANES

            def lane(n, it):
                t = L[n]
                s = t["sem"]
                count = counts[n]
                small = t["small"]

                def link(ins):
                    count[0] += 1
                    ins.then_inc(s["dve_step"], 1)
                    after(dve, t, "dve_step", it, count[0])

                def layernorm(x, dst, signal):
                    for tile in range(TB):
                        dve.bn_stats(small[:, tile * 6:tile * 6 + 6], x[:, tile]) if tile < TB - 1 else \
                            link(dve.bn_stats(small[:, tile * 6:tile * 6 + 6], x[:, tile]))
                    carry(dve, t, 440 + norms[n])
                    for tile in range(TB):
                        ins = dve.bn_aggr(small[:, 16 + tile * 2:18 + tile * 2], small[:, tile * 6:tile * 6 + 6])
                    ins.then_inc(s["var"], 1)
                    yield
                    norms[n] += 1
                    after(dve, t, "rstd", it, norms[n])
                    for tile in range(TB):
                        ins = dve.tensor_scalar(dst[:, tile], x[:, tile], small[:, 16 + 2 * tile:17 + 2 * tile],
                                                small[:, 20 + tile:21 + tile], ALU.subtract, ALU.mult)
                    if signal:
                        ins.then_inc(s["norm"], 1)
                    else:
                        link(ins)

                def residual(it_k, bank, x_old):
                    after(dve, t, "y_ps", it, it_k)
                    count[0] += 1
                    dve.tensor_tensor(t["x"][:, :, :].rearrange("p t c -> p (t c)"), lane_psum(t, bank, 0, 512),
                                      x_old[:, :, :].rearrange("p t c -> p (t c)"), ALU.add) \
                       .then_inc(s["dve_step"], 1)
                    after(dve, t, "dve_step", it, count[0])

                vm = table("vmask").rearrange("p (c h) -> p c h", h=VH)
                for part in range(2):
                    after(dve, t, "ctx_ps", it, part + 2)
                    ps = t["ps"][:, (3, 1)[part], 0:CB * 2 * VH * DH].rearrange("p (c l h d) -> p c l h d", c=CB, l=2, d=DH)
                    for layer in range(2):
                        full = CB - part
                        c0 = part * CB
                        last = dve.tensor_tensor(t["vbd"][:, layer, c0:c0 + full, :, 0:DH], ps[:, 0:full, layer],
                                                 vm[:, c0:c0 + full].unsqueeze(3).broadcast_to([P, full, VH, DH]), ALU.mult)
                        if part:
                            h0, nr = chunk_heads(NC_CH - 1)
                            nh = H - h0
                            last = dve.tensor_tensor(t["vbd"][0:nr, layer, NC_CH - 1, 0:nh, 0:DH], ps[0:nr, CB - 1, layer, 0:nh],
                                                     vm[0:nr, NC_CH - 1, 0:nh].unsqueeze(2).broadcast_to([nr, nh, DH]), ALU.mult)
                    last.then_inc(s["cv_sb"], 1)
                yield
                after(dve, t, "x_in", it, 16)
                yield from layernorm(t["xin"], t["h"], True)
                yield
                after(dve, t, "q_sb", it, 1)
                dve.tensor_tensor(t["qbd"][:, 1], windows(t["qT"], 1),
                                  table("hm4").unsqueeze(1).unsqueeze(3).broadcast_to([P, NW, HG, WIN]), ALU.mult) \
                    .then_inc(s["qbd1"], 1)
                yield
                after(dve, t, "s_ps", it, 1)
                ps = t["ps"][:, 0:3, :].rearrange("p b (u k) -> p (b u) k", k=WIN)
                dve.tensor_tensor(t["s0"][:, 0:NG], ps[:, 0:NG], table("band0").unsqueeze(1).broadcast_to([P, NG, WIN]), ALU.min)
                dve.tensor_tensor(t["s0"][:, NG:NU], ps[:, NG:NU], table("band").unsqueeze(1).broadcast_to([P, NU - NG, WIN]),
                                  ALU.min).then_inc(s["s_sb"], 1)
                after(dve, t, "s_sb", it, 1)
                link(dve.tensor_reduce(small[:, 64:64 + NU], t["s0"], AX_X, ALU.max))
                dve.tensor_tensor(t["s0"], t["s0"], small[:, 64:64 + NU].unsqueeze(2).broadcast_to([P, NU, WIN]),
                                  ALU.subtract).then_inc(s["shift"], 1)
                after(dve, t, "v_win", it, 16 * HG)
                vw = t["vw"].rearrange("p j (g h d) -> p (j g) h d", h=HG, d=DH)
                dve.tensor_tensor(vw, vw, table("rm4").unsqueeze(1).unsqueeze(3).broadcast_to([P, NU, HG, DH]), ALU.mult) \
                    .then_inc(s["vw_sb"], 1)
                after(dve, t, "prob", it, 1)
                link(dve.tensor_reduce(small[:, 64:64 + NU], t["s0"], AX_X, ALU.add))
                link(dve.reciprocal(small[:, 64:64 + NU], small[:, 64:64 + NU]))
                link(dve.tensor_tensor(t["s0"], t["s0"], small[:, 64:64 + NU].unsqueeze(2).broadcast_to([P, NU, WIN]),
                                       ALU.mult))
                dve.transpose(t["pT0"].rearrange("p u k -> p (u k)"), t["s0"].rearrange("p u k -> p (u k)")) \
                   .then_inc(s["pT_sb0"], 1)
                yield
                after(dve, t, "y_ps", it, 1)
                after(dve, t, "stored", it, 0)
                dve.tensor_tensor(t["x"][:, :, :].rearrange("p t c -> p (t c)"), lane_psum(t, 2, 0, 512),
                                  t["xin"][:, :, :].rearrange("p t c -> p (t c)"), ALU.add).then_inc(s["x_first"], 1)
                after(dve, t, "x_first", it, 1)
                yield

                def normalise(it_k, o_k, bank, tile, floor):
                    after(dve, t, "o_ps", it, o_k)
                    o = lane_psum(t, bank, 0, H * DV).rearrange("p (h d) -> p h d", d=DV)
                    rec = small[:, 160 + 16 * tile:176 + 16 * tile].unsqueeze(2)
                    if floor is None:
                        link(dve.reciprocal(rec, o[:, :, DH:DV]))
                    else:
                        link(dve.tensor_scalar(rec, o[:, :, DH:DV], floor, None, ALU.max))
                        link(dve.reciprocal(rec, rec))
                    dve.tensor_tensor(t["o"][:, tile].rearrange("p (h d) -> p h d", d=DH), o[:, :, 0:DH],
                                      rec.broadcast_to([P, H, DH]), ALU.mult).then_inc(s["o_sb"], 1)

                def cross(i, sub):
                    yield from layernorm(t["x"], t["h"], True)
                    yield
                    yield
                    bounds = bound0[:, :, :] if i == 0 else table("caus").rearrange("p (t s) -> p t s", t=TB)
                    for tile in range(TB):
                        after(dve, t, "s_ps", it, 2 + TB * i + tile)
                        ps = t["ps"][:, :, 0:4 * SC].rearrange("p g (h s) -> p g h s", s=SC)
                        bd = bounds[:, tile].unsqueeze(1).unsqueeze(1).broadcast_to([P, 4, 4, SC])
                        dst = t["s"][:, tile].rearrange("p (g h) s -> p g h s", g=4)
                        dve.tensor_tensor(dst, ps, bd, ALU.min).then_inc(s["s_sb"], 1)
                        if tile == 0:
                            yield
                    for tile in range(TB):
                        after(dve, t, "s_sb", it, 2 + TB * i + tile)
                        mx = small[:, 128 + 16 * tile:144 + 16 * tile]
                        link(dve.tensor_reduce(mx, t["s"][:, tile], AX_X, ALU.max))
                        dve.tensor_tensor(t["s"][:, tile], t["s"][:, tile], mx.unsqueeze(2).broadcast_to([P, H, SC]),
                                          ALU.subtract).then_inc(s["shift"], 1)
                    yield
                    for tile in range(TB):
                        yield
                        normalise(it, (1 if i == 0 else 5) + tile, 3, tile, None)
                        yield
                    after(dve, t, "x_bo", it, i + 1)
                    residual(2 if i == 0 else 5, 1, t["x"])
                    yield

                yield from cross(0, 1)
                yield from layernorm(t["x"], t["h"], False)
                amax = small[:, 200:202]
                link(dve.tensor_reduce(amax, t["h"][:, :, :], AX_X, ALU.max, apply_absolute_value=True))
                link(dve.tensor_scalar(amax, amax, 1e-5, None, ALU.max))
                dve.tensor_scalar(small[:, 204:206], amax, wscale127[:, 0:1], None, ALU.mult)
                link(dve.reciprocal(small[:, 202:204], amax))
                link(dve.tensor_scalar(small[:, 202:204], small[:, 202:204], 127.0, None, ALU.mult))
                for tile in range(TB):
                    ins = dve.tensor_scalar(t["h"][:, tile], t["h"][:, tile], small[:, 202 + tile:203 + tile], MAGIC,
                                            ALU.mult, ALU.add)
                link(ins)
                dve.tensor_scalar(t["hq"], t["h"][:, :, :], -MAGIC, 127.0, ALU.add, ALU.min) \
                   .then_inc(s["norm"], 1)
                yield
                after(dve, t, "hT_ps", it, 3)
                dve.tensor_scalar(t["hTb"], t["ps"][:, 0, :].bitcast(BF16)[:, 0:KD * S]
                                  .rearrange("p (k c) -> p k c", k=KD), -128.0, None, ALU.max).then_inc(s["hT"], 1)
                after(dve, t, "y_ps", it, 3)
                for tile in range(TB):
                    ins = dve.scalar_tensor_tensor(t["h"][:, tile], lane_psum(t, 1, tile * D, tile * D + D),
                                                   small[:, 204 + tile:205 + tile], fbias[:, :], ALU.mult, ALU.add)
                link(ins)
                link(dve.tensor_tensor(t["x"][:, :, :], t["x"][:, :, :], t["h"][:, :, :], ALU.add))
                yield
                yield from layernorm(t["x"], t["h"], True)
                yield
                rope = table("rope").rearrange("p (t c) -> p t c", t=TB)
                for tile in range(TB):
                    after(dve, t, "qk_ps", it, tile + 1)
                    qk = lane_psum(t, 1 + tile, 0, 512).rearrange("p (h d) -> p h d", d=DH)
                    rb = t["rotB"][:, tile].rearrange("p (h d) -> p h d", d=DH)
                    ra = t["rotA"][:, tile].rearrange("p (h r d) -> p h r d", r=2, d=8)
                    dve.tensor_tensor(rb[:, :, 0:8], qk[:, :, 8:16],
                                      rope[:, tile, 8:16].unsqueeze(1).broadcast_to([P, 32, 8]), ALU.mult)
                    dve.tensor_tensor(rb[:, :, 8:16], qk[:, :, 0:8],
                                      rope[:, tile, 16:24].unsqueeze(1).broadcast_to([P, 32, 8]), ALU.mult)
                    dve.tensor_tensor(ra, qk.rearrange("p h (r d) -> p h r d", r=2),
                                      rope[:, tile, 0:8].unsqueeze(1).unsqueeze(1).broadcast_to([P, 32, 2, 8]), ALU.mult) \
                       .then_inc(s["rot_a"], 1)
                for tile in range(TB):
                    after(dve, t, "rot", it, tile + 1)
                    dve.tensor_scalar(t["rotB"][:, tile], t["rotA"][:, tile], 0.0, None, ALU.min).then_inc(s["neg"], 1)
                for tile in range(TB):
                    after(dve, t, "expn", it, tile + 1)
                    dve.scalar_tensor_tensor(t["phi"][:, tile], t["rotA"][:, tile], 0.0, t["rotB"][:, tile],
                                             ALU.max, ALU.add).then_inc(s["phi"], 1)
                yield
                for j in range(2):
                    after(dve, t, "v1_ps", it, j + 1)
                    dve.tensor_tensor(t["v1bd"][:, 2 * j:2 * j + 2, :, :, 0:DH].rearrange("p c q h d -> p (c q) h d"),
                                      lane_psum(t, 1 + j, 0, 512).rearrange("p (q h d) -> p q h d", h=2, d=DH),
                                      table("rm2").unsqueeze(1).unsqueeze(3).broadcast_to([P, 2 * NPAIR, 2, DH]), ALU.mult) \
                       .then_inc(s["v1_bd"], 1)
                after(dve, t, "phiqT", it, 1)
                for half in range(KD):
                    last = dve.tensor_tensor(t["qp"][:, half],
                                             t["kT"][:, half, RADIUS:RADIUS + S].rearrange("p (c q) -> p c q", c=NCK)
                                             .unsqueeze(2).broadcast_to([P, NCK, 4, CK]),
                                             table("hp4").unsqueeze(1).unsqueeze(3).broadcast_to([P, NCK, 4, CK]), ALU.mult)
                last.then_inc(s["qp"], 1)
                yield
                after(dve, t, "a_ps", it, 1)
                for c in range(NCK):
                    dve.tensor_tensor(t["at"][:, c * NPAIR:(c + 1) * NPAIR],
                                      lane_psum(t, c, 0, 512).rearrange("p (u q) -> p u q", q=CK),
                                      table("tri").unsqueeze(1).broadcast_to([P, NPAIR, CK]), ALU.mult) \
                       .then_inc(s["a_sb"], 1)
                yield
                for c in range(1, NCK):
                    after(dve, t, "st_ps", it, c)
                    dve.tensor_tensor(t["st"][:, c - 1].rearrange("p (k h d) -> p k h d", k=KD, h=8),
                                      lane_psum(t, c - 1, 0, H * DV).rearrange("p (k h d) -> p k h d", k=KD, h=8),
                                      table("hm8").unsqueeze(1).unsqueeze(3).broadcast_to([P, KD, 8, DV]), ALU.mult) \
                       .then_inc(s["st_sb"], 1)
                yield
                for tile in range(TB):
                    normalise(it, 3 + tile, (3, 0)[tile], tile, 1e-6)
                yield
                residual(4, 1, t["x"])
                yield
                yield from cross(1, 4)
                yield from layernorm(t["x"], t["h6"], True)
                yield
                after(dve, t, "r_ps", it, 1)
                lg = small[:, 300:316].rearrange("p (t e) -> p t e", e=E)
                m1, m2 = small[:, 340:342], small[:, 342:344]
                r1 = small[:, 344:346]
                pr = small[:, 320:336].rearrange("p (t e) -> p t e", e=E)
                rk = small[:, 350:366].rearrange("p (t e) -> p t e", e=E)
                desc = table("desc").unsqueeze(1).broadcast_to([P, TB, E])
                wide = lambda v: v.unsqueeze(2).broadcast_to([P, TB, E])
                link(dve.tensor_copy(lg, lane_psum(t, 1, 0, TB * E).rearrange("p (t e) -> p t e", e=E)))
                link(dve.tensor_reduce(m1, lg, AX_X, ALU.max))
                dve.tensor_tensor(pr, lg, wide(m1), ALU.subtract).then_inc(s["r_shift"], 1)
                after(dve, t, "r_exp", it, 1)
                link(dve.tensor_reduce(m1, pr, AX_X, ALU.add))
                link(dve.reciprocal(m1, m1))
                link(dve.tensor_tensor(pr, pr, wide(m1), ALU.mult))
                hot = [small[:, 370 + 16 * i:386 + 16 * i].rearrange("p (t e) -> p t e", e=E) for i in range(2)]
                for i, m in enumerate((m1, m2)):
                    link(dve.tensor_reduce(m, pr, AX_X, ALU.max))
                    link(dve.tensor_tensor(rk, pr, wide(m), ALU.is_equal))
                    link(dve.tensor_tensor(rk, rk, desc, ALU.mult))
                    link(dve.tensor_reduce(r1, rk, AX_X, ALU.max))
                    link(dve.tensor_tensor(hot[i], rk, wide(r1), ALU.is_equal))
                    if i == 0:
                        link(dve.tensor_scalar(rk, hot[i], 4.0, None, ALU.mult))
                        link(dve.tensor_tensor(pr, pr, rk, ALU.subtract))
                link(dve.tensor_tensor(r1, m1, m2, ALU.add))
                link(dve.tensor_scalar(r1, r1, 1e-6, None, ALU.add))
                link(dve.reciprocal(r1, r1))
                first = it * LANES * TB + n * TB
                chosen = small[:, 402:418].rearrange("p (t e) -> p t e", e=E)
                dve.tensor_tensor(chosen, hot[0], hot[1], ALU.add)
                for i, m in enumerate((m1, m2)):
                    ins = dve.tensor_tensor(gates[:, bass.ds(first, TB), i], m, r1, ALU.mult)
                ins.then_inc(s["x_done"], 1)
                yield
                after(dve, t, "r_ps", it, 2)
                place = small[:, 420:436].rearrange("p (t e) -> p t e", e=E)
                ranks = lane_psum(t, 2, 0, TB * E).rearrange("p (t e) -> p t e", e=E)
                totals = lane_psum(t, 2, TB * E, 2 * TB * E).rearrange("p (t e) -> p t e", e=E)
                for tile in range(TB):
                    link(dve.tensor_tensor(place[:, tile], ranks[:, tile], next_row[:, :], ALU.add))
                    link(dve.tensor_tensor(next_row[:, :], totals[:, tile], next_row[:, :], ALU.add))
                for i in range(2):
                    link(dve.tensor_tensor(rk, hot[i], place, ALU.mult))
                    link(dve.tensor_reduce(r1, rk, AX_X, ALU.add))
                    dve.tensor_copy(pos[:, bass.ds(first, TB), i], r1)
                    ins = dve.tensor_copy(t["posi"][:, i], r1) if i else link(dve.tensor_copy(t["posi"][:, i], r1))
                ins.then_inc(s["pos"], 1)
                yield
                assert count[0] == SIGNALS["dve_step"], count

            with dve.Fori(0, iters) as it:
                interleave([lane(n, it) for n in range(LANES)])

        programs.close()
        if dump is not None:
            dump(nc, L, dict(ternT=ternT, bound0=bound0, pos=pos, next_row=next_row, gates=gates))


def build_experts(nc, a, x5_dram, hs_dram, tab, table, gates, pos, next_row, out):
    with ExitStack() as ctx:
        sb = lambda name, shape, dt=F32: ctx.enter_context(nc.sbuf_tensor(name, shape, dt))
        sem = lambda name: ctx.enter_context(nc.semaphore(name))
        ys_dram = nc.dram_tensor("sorted_outputs", [NJ * P, D], F32).ap()
        NC = FF // P
        w13 = sb("w13", [P, E, KD, 2 * FF])
        w2 = sb("w2", [P, E, NC, D])
        hin = sb("hin", [P, 2, D])
        hT = sb("hT", [P, 2, KD, P])
        th = sb("th", [P, 2, FF])
        gated = sb("gated", [P, 2, FF])
        inner = sb("inner", [P, 2, FF])
        innerT = sb("innerT", [P, 2, NC, P])
        y = sb("y", [P, 2, D])
        zeros = sb("zeros", [P, D])
        pad_at = sb("pad_at", [P, E], I32)
        plan = sb("plan", [1, 2, NJ], I32)
        f = sb("plan_f", [1, 2, NJ])
        out_at = sb("out_at", [P, NT, 2])
        past = sb("past", [P, NT * 2, E])
        now, upto_e, inside, val = (sb(n, [1, NJ, E]) for n in ("now", "upto_e", "inside", "val"))
        e8 = sb("e8", [P, 7, E])
        padf = sb("padf", [P, E])
        back = sb("back", [P, 2, TB, D])
        yback = sb("yback", [P, 2, 2, TB, D])
        at = sb("at", [P, 2, 2, TB], I32)
        gate = sb("gate", [P, 2, 2, TB])
        gu = ctx.enter_context(nc.psum_tensor("gu", [P, 2, 2, FF], F32))
        psT = ctx.enter_context(nc.psum_tensor("psT", [P, FF], F32))
        psH = ctx.enter_context(nc.psum_tensor("psH", [P, 512], F32))
        psY = ctx.enter_context(nc.psum_tensor("psY", [P, 2, 512], F32))

        weights_in = sem("weights_in")
        plan_step = sem("plan_step")
        zeroed = sem("zeroed")
        padded = sem("padded")
        h_in = [sem(f"h_in{q}") for q in range(2)]
        hT_ps, hT_sb = sem("e_hT_ps"), sem("e_hT_sb")
        gu_ps = sem("gu_ps")
        tanh = sem("tanh")
        gated_done = sem("gated_done")
        inner_sb = sem("inner_sb")
        innerT_ps, innerT_sb = sem("innerT_ps"), sem("innerT_sb")
        e_y_ps, e_y_sb = sem("e_y_ps"), sem("e_y_sb")
        y_stored = [sem(f"y_stored{q}") for q in range(2)]
        at_ready = sem("at_ready")
        gathered = [sem(f"gathered{q}") for q in range(2)]
        carried = sem("carried")
        x_back = [sem(f"x_back{q}") for q in range(2)]
        sum1 = sem("sum1")
        summed = sem("summed")
        out_stored = [sem(f"out_stored{q}") for q in range(2)]
        N_PLAN = 20

        def landed(eng, sems, j, q, amount=16):
            eng.wait_ge(sems[q], (j - q) * (amount // 2) + amount)

        block = ctx.enter_context(nc.Block())

        @block.sync
        def _(sp):
            for e in range(E):
                sp.dma_start(w13[:, e], a["w13"][e]).then_inc(weights_in, 16)
                sp.dma_start(w2[:, e], a["w2"][e]).then_inc(weights_in, 16)
            sp.wait_ge(plan_step, N_PLAN)
            sp.wait_ge(padded, 16 * E)

            def load(j, q):
                row = sp.value_load(plan[0:1, 1, bass.ds(j, 1)], min_val=0, max_val=E * CAP - P)
                sp.dma_start(hin[:, q], hs_dram[bass.ds(row, P), :]).then_inc(h_in[q], 16)

            def store(j, q):
                sp.wait_ge(e_y_sb, j + 1)
                sp.dma_start(ys_dram[bass.ds(j * P, P), :], y[:, q]).then_inc(y_stored[q], 16)

            def step(j, q):
                sp.wait_ge(hT_ps, j)
                load(j + 1, 1 - q)
                store(j - 2, q)

            load(0, 0)
            load(1, 1)
            sp.wait_ge(hT_ps, 1)
            load(2, 0)
            step(2, 0)
            with sp.Fori(0, (NJ - 4) // 2) as i:
                step(2 * i + 3, 1)
                step(2 * i + 4, 0)
            store(NJ - 3, 1)
            store(NJ - 2, 0)
            store(NJ - 1, 1)

            def load_x(b, q):
                sp.dma_start(back[:, q].rearrange("p t c -> p (t c)"), x5_dram[bass.ds(b, 1)].rearrange("o p c -> (o p) c")) \
                  .then_inc(x_back[q], 16)

            def store_out(b, q):
                sp.wait_ge(summed, b + 1)
                sp.dma_start(out[bass.ds(b, 1)].rearrange("o (t p) c -> p (o t) c", p=P), back[:, q]) \
                  .then_inc(out_stored[q], 16)

            load_x(0, 0)
            load_x(1, 1)
            with sp.Fori(0, (B - 2) // 2) as i:
                for q in range(2):
                    store_out(2 * i + q, q)
                    landed(sp, out_stored, 2 * i + q, q)
                    load_x(2 * i + q + 2, q)
            for q in range(2):
                store_out(B - 2 + q, q)
            for q in range(2):
                landed(sp, out_stored, B - 2 + q, q)
                landed(sp, y_stored, NJ - 2 + q, q)

        @block.gpsimd
        def _(pool):
            pool.memset(zeros[:, :], 0.0).then_inc(zeroed, 1)
            pool.wait_ge(zeroed, 1)
            pool.wait_ge(plan_step, N_PLAN)
            for e in range(E):
                pool.indirect_dma_start(hs_dram[:, :], bass.IndirectOffsetOnAxis(ap=pad_at[:, e:e + 1], axis=0),
                                        zeros[:, :], None).then_inc(padded, 16)

            pool.wait_ge(padded, 16 * E)
            for q in range(2):
                landed(pool, y_stored, NJ - 2 + q, q)

            def gather(b, q):
                pool.wait_ge(at_ready, b + 1)
                if not isinstance(b, int) or b:
                    pool.wait_ge(carried, b)
                pool.tensor_tensor(zeros[:, 0:1], table("row"), table("row"), ALU.add).then_inc(carried, 1)
                for i in range(2):
                    for tile in range(TB):
                        pool.indirect_dma_start(yback[:, q, i, tile], None, ys_dram[:, :],
                                                bass.IndirectOffsetOnAxis(ap=at[:, q, i, tile:tile + 1], axis=0)) \
                            .then_inc(gathered[q], 16)

            gather(0, 0)
            gather(1, 1)
            with pool.Fori(0, (B - 2) // 2) as i:
                for q in range(2):
                    gather(2 * i + q + 2, q)
            for q in range(2):
                landed(pool, gathered, B - 2 + q, q, 2 * TB * 16)

        @block.tensor
        def _(pe):
            ident = table("ident")

            def step(j, q, tile_here=True, tile_before=True):
                m, r = j - 1, 1 - q
                if tile_here:
                    landed(pe, h_in, j, q)
                    for k in range(KD):
                        last = pe.transpose(psH[:, k * P:(k + 1) * P], hin[:, q, k * P:(k + 1) * P], ident)
                    last.then_inc(hT_ps, 1)
                if tile_before:
                    pe.wait_ge(inner_sb, m + 1)
                    for c in range(NC):
                        last = pe.transpose(psT[:, c * P:(c + 1) * P], inner[:, r, c * P:(c + 1) * P], ident)
                    last.then_inc(innerT_ps, 1)
                if tile_here:
                    e = pe.value_load(plan[0:1, 0, bass.ds(j, 1)], min_val=0, max_val=E - 1)
                    pe.wait_ge(hT_sb, j + 1)
                    for g in range(2):
                        for k in range(KD):
                            last = pe.matmul(gu[:, q, g], hT[:, q, k],
                                             w13[:, bass.ds(e, 1), k, g * FF:(g + 1) * FF].rearrange("p o n -> p (o n)"),
                                             start=(k == 0), stop=(k == KD - 1))
                    last.then_inc(gu_ps, 1)
                if tile_before:
                    e = pe.value_load(plan[0:1, 0, bass.ds(m, 1)], min_val=0, max_val=E - 1)
                    pe.wait_ge(innerT_sb, m + 1)
                    if not isinstance(m, int) or m >= 2:
                        pe.wait_ge(e_y_sb, m - 1)
                    for c in range(NC):
                        last = pe.matmul(psY[:, r, 0:D], innerT[:, r, c],
                                         w2[:, bass.ds(e, 1), c, :].rearrange("p o n -> p (o n)"), start=(c == 0), stop=(c == NC - 1))
                    last.then_inc(e_y_ps, 1)

            pe.wait_ge(weights_in, 16 * 2 * E)
            pe.wait_ge(plan_step, N_PLAN)
            step(0, 0, tile_before=False)
            step(1, 1)
            step(2, 0)
            with pe.Fori(0, (NJ - 4) // 2) as i:
                step(2 * i + 3, 1)
                step(2 * i + 4, 0)
            step(NJ - 1, 1)
            step(NJ, 0, tile_here=False)

        @block.scalar
        def _(act):
            def step(j, q, tile_here=True, tile_before=True):
                m, r = j - 1, 1 - q
                if tile_here:
                    act.wait_ge(hT_ps, j + 1)
                    act.activation(hT[:, q], psH[:, 0:D].rearrange("p (k c) -> p k c", k=KD), ACT.Copy).then_inc(hT_sb, 1)
                if tile_before:
                    act.wait_ge(innerT_ps, m + 1)
                    act.activation(innerT[:, r], psT[:, :].rearrange("p (k c) -> p k c", k=NC), ACT.Copy).then_inc(innerT_sb, 1)
                if tile_here:
                    act.wait_ge(gu_ps, j + 1)
                    act.activation(th[:, q], gu[:, q, 0], ACT.Tanh, scale=0.5).then_inc(tanh, 1)
                if tile_before:
                    act.wait_ge(e_y_ps, m + 1)
                    if not isinstance(m, int) or m >= 2:
                        landed(act, y_stored, m - 2, r)
                    act.activation(y[:, r], psY[:, r, 0:D], ACT.Copy).then_inc(e_y_sb, 1)

            step(0, 0, tile_before=False)
            step(1, 1)
            step(2, 0)
            with act.Fori(0, (NJ - 4) // 2) as i:
                step(2 * i + 3, 1)
                step(2 * i + 4, 0)
            step(NJ - 1, 1)
            step(NJ, 0, tile_here=False)

        @block.vector
        def _(dve):
            done = [0]

            def plan_link(ins):
                done[0] += 1
                ins.then_inc(plan_step, 1)
                dve.wait_ge(plan_step, done[0])

            plan_link(dve.tensor_scalar(padf[:, :], next_row[:, :], table("row"), None, ALU.add))
            plan_link(dve.tensor_copy(pad_at[:, :], padf[:, :]))
            cnt, tiles, end, start, base, shift, jump = (e8[:, i] for i in range(7))
            first_row = table("first_row")
            plan_link(dve.tensor_tensor(cnt, next_row[:, :], first_row, ALU.subtract))
            plan_link(dve.tensor_scalar(tiles, cnt, 1.0 / P, (P - 1.0) / P - 0.5 + 0.5 / P, ALU.mult, ALU.add))
            plan_link(dve.tensor_scalar(tiles, tiles, MAGIC, None, ALU.add))
            plan_link(dve.tensor_scalar(tiles, tiles, -MAGIC, None, ALU.add))
            src = tiles
            for i, dst in ((1, end), (2, start), (4, end)):
                dve.tensor_copy(dst[:, 0:i], src[:, 0:i])
                plan_link(dve.tensor_tensor(dst[:, i:E], src[:, i:E], src[:, 0:E - i], ALU.add))
                src = dst
            plan_link(dve.tensor_tensor(start, end, tiles, ALU.subtract))
            plan_link(dve.scalar_tensor_tensor(shift, start, float(P), first_row, ALU.mult, ALU.subtract))
            dve.tensor_copy(jump[:, 0:1], shift[:, 0:1])
            dve.tensor_tensor(jump[:, 1:E], shift[:, 1:E], shift[:, 0:E - 1], ALU.subtract)
            tiles_j = table("tiles")[0:1].unsqueeze(2).broadcast_to([1, NJ, E])
            wide = lambda v: v[0:1].unsqueeze(1).broadcast_to([1, NJ, E])
            dve.tensor_tensor(now[:, :, :], tiles_j, wide(start), ALU.is_ge)
            dve.tensor_tensor(upto_e[:, :, :], tiles_j, wide(end), ALU.is_ge)
            plan_link(dve.scalar_tensor_tensor(val[:, :, :], tiles_j, float(P), wide(shift), ALU.mult, ALU.subtract))
            plan_link(dve.tensor_tensor(inside[:, :, :], now[:, :, :], upto_e[:, :, :], ALU.subtract))
            dve.tensor_tensor(val[:, :, :], val[:, :, :], inside[:, :, :], ALU.mult)
            plan_link(dve.tensor_tensor(now[:, :, :], inside[:, :, :], wide(table("expert")), ALU.mult))
            dve.tensor_reduce(f[:, 0], now[:, :, :], AX_X, ALU.add)
            plan_link(dve.tensor_reduce(f[:, 1], val[:, :, :], AX_X, ALU.add))
            plan_link(dve.tensor_copy(plan[:, :, :], f[:, :, :]))
            flat = pos[:, :, :].rearrange("p t i -> p (t i)")
            pairs = lambda v: v.unsqueeze(1).broadcast_to([P, NT * 2, E])
            plan_link(dve.tensor_tensor(past[:, :, :], flat.unsqueeze(2).broadcast_to([P, NT * 2, E]), pairs(first_row),
                                        ALU.is_ge))
            plan_link(dve.tensor_tensor(past[:, :, :], past[:, :, :], pairs(jump), ALU.mult))
            out_flat = out_at[:, :, :].rearrange("p t i -> p (t i)")
            plan_link(dve.tensor_reduce(out_flat, past[:, :, :], AX_X, ALU.add))
            plan_link(dve.tensor_tensor(out_flat, out_flat, flat, ALU.add))
            assert done[0] == N_PLAN, done

            def tile(j, q):
                dve.wait_ge(tanh, j + 1)
                dve.scalar_tensor_tensor(gated[:, q], th[:, q], 1.0, gu[:, q, 0], ALU.add, ALU.mult).then_inc(gated_done, 1)
                dve.wait_ge(gated_done, j + 1)
                if not isinstance(j, int) or j >= 2:
                    dve.wait_ge(innerT_ps, j - 1)
                dve.scalar_tensor_tensor(inner[:, q], gated[:, q], 0.5, gu[:, q, 1], ALU.mult, ALU.mult).then_inc(inner_sb, 1)

            tile(0, 0)
            tile(1, 1)
            with dve.Fori(0, (NJ - 2) // 2) as i:
                tile(2 * i + 2, 0)
                tile(2 * i + 3, 1)

            def copy_at(b, q):
                if not isinstance(b, int):
                    landed(dve, gathered, b - 2, q, 2 * TB * 16)
                dve.tensor_copy(gate[:, q].rearrange("p i t -> p t i"), gates[:, bass.ds(b * TB, TB), :])
                dve.tensor_copy(at[:, q].rearrange("p i t -> p t i"), out_at[:, bass.ds(b * TB, TB), :]).then_inc(at_ready, 1)

            def combine(b, q):
                landed(dve, gathered, b, q, 2 * TB * 16)
                landed(dve, x_back, b, q)
                dve.wait_ge(at_ready, b + 1)
                for i in range(2):
                    for t in range(TB):
                        ins = dve.scalar_tensor_tensor(back[:, q, t], yback[:, q, i, t], gate[:, q, i, t:t + 1], back[:, q, t],
                                                       ALU.mult, ALU.add)
                    ins.then_inc((sum1, summed)[i], 1)
                    dve.wait_ge((sum1, summed)[i], b + 1)

            copy_at(0, 0)
            copy_at(1, 1)
            with dve.Fori(0, (B - 2) // 2) as i:
                for q in range(2):
                    combine(2 * i + q, q)
                    copy_at(2 * i + q + 2, q)
            for q in range(2):
                combine(B - 2 + q, q)


N_PHASES = 41
NORM_PHASES = (1, 6, 16, 19, 27, 37)
QKV_PHASE = 3
BIAS_PHASES = (8, 29)
ROT_PHASE = 21
N_POOL = 8 + LANES * (2 + NCK)
N_DVE_INIT = 13


def arrays_of(i):
    i = {k: np.asarray(v) for k, v in i.items()}
    mats = [i["L0_attn_Wq"], i["L0_attn_Wk"], i["L0_attn_Wv"], i["L0_attn_Wo"],
            i["L0_xattn_Wq"], i["L0_xattn_Wk"], i["L0_xattn_Wv"], i["L0_xattn_Wo"],
            i["L1_attn_Wq"].T, i["L1_attn_Wk"].T, i["L1_attn_Wv"].T, i["L1_attn_Wo"].T,
            i["L1_xattn_Wq"].T, i["L1_xattn_Wk"].T, i["L1_xattn_Wv"].T, i["L1_xattn_Wo"].T]
    rows_first = lambda m: m.reshape(-1, P, m.shape[-1]).transpose(1, 0, 2)
    o = {
        "x": i["x"],
        "ctxT": i["ctx_1024"].reshape(B, SC, KD, P).transpose(0, 3, 2, 1),
        "mask": i["mask_1x1xSxS2_if1"].reshape(S, SC),
        "proj": np.stack([rows_first(m) for m in mats], axis=1),
        "router": rows_first(i["L1_ffn_router_w"].T),
        "bo": np.stack([i["L0_xattn_bo"], i["L1_xattn_bo"]]),
        "cols": np.stack([i[n].reshape(KD, P).T for n in ("L0_xattn_bq", "L0_xattn_bk", "L1_xattn_bq", "L1_xattn_bk",
                                                                          "L0_xattn_bv", "L1_xattn_bv")], axis=1),
        "fbias": i["L0_ffn_bias"],
        "wscale": i["L0_ffn_weight_scale"],
        "packed": i["L0_ffn_packed_weight"].reshape(64, D),
        "w13": i["L1_ffn_w13"].reshape(E, KD, P, 2 * FF).transpose(0, 2, 1, 3),
        "w2": i["L1_ffn_w2"].reshape(E, FF // P, P, D).transpose(0, 2, 1, 3),
        "tables": np.concatenate(list(shape_tables().values()), axis=1),
    }
    return {k: np.ascontiguousarray(v) for k, v in o.items()}


def kernel(**inputs):
    import concourse.bacc as _bacc
    from concourse.bass_utils import run_bass_kernel_spmd as _run

    arrays = {f"in_{k}": v for k, v in arrays_of(inputs).items()}
    nc = _bacc.Bacc("TRN2", target_bir_lowering=False, num_devices=1)
    aps = {k[3:]: nc.dram_tensor(k, v.shape, mybir.dt.from_np(v.dtype), kind="ExternalInput").ap() for k, v in arrays.items()}
    out = nc.dram_tensor("out", (B, S, D), F32, kind="ExternalOutput").ap()
    mega_kernel(nc, aps, out)
    r = _run(nc, [arrays], core_ids=[0])
    return r.results[0]["out"]
```

```python
from contextlib import ExitStack

import numpy as np

import concourse.bass as bass
from concourse import mybir

F32 = mybir.dt.float32
BF16 = mybir.dt.bfloat16
I32 = mybir.dt.int32
ALU = mybir.AluOpType
ACT = mybir.ActivationFunctionType
AX_X = mybir.AxisListType.X

P = 128
B, S, D = 16, 256, 256
SC = 77
H, DH = 16, 16
KD = D // P
TB = S // P
NT = B * TB
HS = H * SC
LANES = 2
ITERS = B // LANES
EPS_LN = 1e-5

RADIUS = 8
WIN = 32
WQ = WIN - RADIUS
NW = -(-S // WQ)
QLAST = S - (NW - 1) * WQ
SPAD = RADIUS + NW * WQ
L0_SCALE = 1.0 / (2.0 * 0.28)
HG = 4
NG = H // HG
NU = NW * NG

NC_CH = -(-HS // P)
CREP = SC + P
CB = NC_CH // 2
VH = 3
DV = DH + 1

CK = 64
NCK = S // CK
NPAIR = H // 2

E, FF = 8, 512
NJ = (2 * B * S) // P + E
CAP = B * S + P
STATS_FIRST = 208
NEG = -1.0e38
BIG = 3.0e38
MAGIC = 12582912.0

(W0Q, W0K, W0V, W0O, X0Q, X0K, X0V, X0O, W1Q, W1K, W1V, W1O, X1Q, X1K, X1V, X1O) = range(16)
NM = 16


def chunk_heads(c):
    return P * c // SC, min(P, HS - P * c)


def shape_tables():
    p = np.arange(P)
    t = {}
    t["ident"] = np.eye(P, dtype=np.float32)
    t["hm4"] = (p[:, None] // DH % HG == np.arange(HG)).astype(np.float32)
    t["hm8"] = (p[:, None] // DH == np.arange(8)).astype(np.float32)
    t["hp4"] = (p[:, None] // (2 * DH) == np.arange(4)).astype(np.float32)
    t["hg2"] = (p[:, None] // (HG * DH) == np.arange(2)).astype(np.float32)
    t["hm2"] = (p[:, None] // DH % 2 == np.arange(2)).astype(np.float32)
    t["rm4"] = (p[:, None] // WIN == np.arange(HG)).astype(np.float32)
    t["rm2"] = (p[:, None] // CK == np.arange(2)).astype(np.float32)
    q, k = (p % WIN)[:, None], np.arange(WIN)[None, :]
    seen = (k <= q) & (k >= q - RADIUS)
    t["band"] = np.where(seen, BIG, NEG).astype(np.float32)
    t["band0"] = np.where(seen & (k >= RADIUS), BIG, NEG).astype(np.float32)
    tok = p[:, None] + P * np.arange(TB)[None, :]
    t["caus"] = np.where(np.arange(SC) <= tok[:, :, None], BIG, NEG).astype(np.float32).reshape(P, -1)
    t["tri"] = ((p % CK)[:, None] <= np.arange(CK)).astype(np.float32)
    vm = np.zeros((P, NC_CH, VH), np.float32)
    for c in range(NC_CH):
        h0, rows = chunk_heads(c)
        head = (P * c + p) // SC
        vm[:, c] = (head[:, None] == h0 + np.arange(VH)) & (p < rows)[:, None]
    t["vmask"] = vm.reshape(P, -1)
    half = DH // 2
    inv = (np.float32(10000.0) ** (-np.arange(half, dtype=np.float32) / np.float32(half))).astype(np.float32)
    ang = (tok.astype(np.float32)[:, :, None] * inv).astype(np.float32)
    c, s = np.cos(ang).astype(np.float32), np.sin(ang).astype(np.float32)
    t["rope"] = np.concatenate([c, -s, s], axis=-1).reshape(P, -1)
    t["power"] = np.full((P, TB), -0.5, np.float32)
    t["ones"] = np.ones((P, P), np.float32)
    t["before"] = (p[:, None] < p[None, :]).astype(np.float32)
    t["desc"] = np.tile(np.arange(E, 0, -1, dtype=np.float32), (P, 1))
    t["row"] = p[:, None].astype(np.float32)
    t["expert"] = np.tile(np.arange(E, dtype=np.float32), (P, 1))
    t["first_row"] = np.tile(CAP * np.arange(E, dtype=np.float32), (P, 1))
    t["tiles"] = np.tile(np.arange(NJ, dtype=np.float32), (P, 1))
    return t


TABLES = {n: a.shape[1] for n, a in shape_tables().items()}
TAB_AT, _n = {}, 0
for _k, _w in TABLES.items():
    TAB_AT[_k] = _n
    _n += _w
TAB_W = _n

SIGNALS = {
    "x_in": 16,
    "ctx_in": 48,
    "ctx_ps": 3,
    "ck_sb": 1,
    "kbd": 4,
    "cv_sb": 2,
    "stats": 1,
    "var": 6,
    "rstd": 12,
    "norm": 6,
    "hT_ps": 6,
    "hT": 6,
    "q_ps": 3,
    "q_sb": 3,
    "qbd0": 1,
    "qbd1": 1,
    "hrep1": 2,
    "kv_ps": 2,
    "k_sb": 1,
    "v_sb": 1,
    "v_out": 16,
    "v_win": 16 * HG,
    "vw_sb": 1,
    "s_ps": 5,
    "s_sb": 5,
    "shift": 3,
    "max1": 2,
    "shift1": 2,
    "prob": 5,
    "pT_sb0": 1,
    "pT_ps": 4,
    "pT_sb": 4,
    "o_ps": 6,
    "o_sb": 4 + 2,
    "oT_ps": 4,
    "oT_sb": 4,
    "y_ps": 5,
    "x_bo": 2,
    "x_first": 1,
    "qk_ps": 2,
    "rot_a": 2,
    "rot": 2,
    "expn": 2,
    "phi": 4,
    "phiT_ps": 1,
    "phiqT": 1,
    "phiT_sb": 1,
    "qp": 2,
    "v1_ps": 2,
    "v1_bd": 2,
    "v1_sb": 1,
    "a_ps": 1,
    "a_sb": 4,
    "st_ps": NCK - 1,
    "st_sb": NCK - 1,
    "r_ps": 2,
    "r_shift": 1,
    "r_exp": 1,
    "x_done": 1,
    "pos": 1,
    "sorted": 2 * TB * 16,
    "stored": 16,
    "dve_step": 59,
}


STARTS = {"pos": SIGNALS["pos"], "stored": SIGNALS["stored"]}


def mega_kernel(nc, a, out):
    ctx = ExitStack()
    with ctx:
        sb = lambda name, shape, dt=F32: ctx.enter_context(nc.sbuf_tensor(name, shape, dt))
        sem = lambda name: ctx.enter_context(nc.semaphore(name))
        x5_dram = nc.dram_tensor("x5_scratch", [B, P, TB * D], F32).ap()
        v_dram = nc.dram_tensor("v_scratch", [LANES, SPAD, D], F32).ap()
        hs_dram = nc.dram_tensor("sorted_rows", [E * CAP, D], F32).ap()
        tab = sb("tab", [P, TAB_W])
        table = lambda n: tab[:, TAB_AT[n]:TAB_AT[n] + TABLES[n]]
        gates = sb("gates", [P, NT, 2])
        pos = sb("pos", [P, NT, 2])
        next_row = sb("next_row", [P, E])
        build_layers(nc, ctx, a, x5_dram, v_dram, hs_dram, tab, table, gates, pos, next_row)
        build_experts(nc, a, x5_dram, hs_dram, tab, table, gates, pos, next_row, out)


def build_layers(nc, held, a, x5_dram, v_dram, hs_dram, tab, table, gates, pos, next_row):
    with ExitStack() as ctx:
        sb = lambda name, shape, dt=F32: ctx.enter_context(nc.sbuf_tensor(name, shape, dt))
        sem = lambda name: held.enter_context(nc.semaphore(name))
        w = sb("w", [P, NM, KD, D])
        wr = sb("wr", [P, KD, E])
        ternT = sb("ternT", [P, KD, D], BF16)
        bo = sb("bo", [P, 2, D])
        cols = sb("cols", [P, 6, KD])
        fbias = sb("fbias", [P, D])
        wscale = sb("wscale", [P, 1])
        wscale127 = sb("wscale127", [P, 1])
        bound0 = sb("bound0", [P, TB, SC])
        identb = sb("identb", [P, P], BF16)
        packed = sb("packed", [64, D], I32)
        maski = sb("maski", [P, TB, SC], I32)

        L = []
        for n in range(LANES):
            t = {}
            for name, shape in (("xin", [P, TB, D]), ("x", [P, TB, D]), ("h", [P, TB, D]), ("h6", [P, TB, D]),
                                ("hT", [P, KD, SPAD]), ("kT", [P, KD, SPAD]), ("kg", [P, KD, 2, SPAD]),
                                ("qT", [P, KD, SPAD]), ("spread", [P, 3072]),
                                ("crep", [P, KD, CREP]), ("ck", [P, 2, KD, SC]), ("kbd", [P, 2, KD, 8, SC]),
                                ("vbd", [P, 2, NC_CH, VH, DV]), ("o", [P, TB, D]), ("oT", [P, KD, S]),
                                ("v1bd", [P, NCK, NPAIR, 2, DV]), ("v1", [P, TB, H, DV]), ("work", [P, 5632]),
                                ("small", [P, 512])):
                t[name] = sb(f"{name}{n}", shape)
            t["posi"] = sb(f"posi{n}", [P, 2, TB], I32)
            wk = t["work"]
            cut = lambda lo, n_, pat, wk=wk, **k: wk[:, lo:lo + n_].rearrange(pat, **k)
            t["vw"] = cut(0, NW * D, "p (j c) -> p j c", j=NW)
            t["qbd"] = t["spread"][:, 0:KD * NW * P].rearrange("p (k j h q) -> p k j h q", k=KD, j=NW, h=HG)
            t["hrep1"] = t["spread"][:, 0:KD * NCK * P].rearrange("p (k c m) -> p k c m", k=KD, c=NCK)
            t["qp"] = t["spread"][:, KD * NCK * P:KD * NCK * P + KD * NCK * 4 * CK] \
                .rearrange("p (k c r q) -> p k c r q", k=KD, c=NCK, r=4)
            t["hq"] = wk[:, 5120:5376].bitcast(BF16).rearrange("p (t c) -> p t c", t=TB)
            t["hTb"] = wk[:, 5376:5632].bitcast(BF16).rearrange("p (k c) -> p k c", k=KD)
            t["s0"] = cut(2816, NU * WIN, "p (u k) -> p u k", u=NU)
            t["pT0"] = cut(2816 + 1408, NU * WIN, "p (u k) -> p u k", u=NU)
            t["s"] = cut(0, TB * HS, "p (t h s) -> p t h s", t=TB, h=H)
            t["sflat"] = cut(0, TB * HS, "p (t n) -> p t n", t=TB)
            t["pT"] = cut(2464, TB * NC_CH * P, "p (t c q) -> p t c q", t=TB, c=NC_CH)
            t["rotA"] = cut(0, 1024, "p (t c) -> p t c", t=TB)
            t["rotB"] = cut(1024, 1024, "p (t c) -> p t c", t=TB)
            t["at"] = cut(0, 2048, "p (u q) -> p u q", q=CK)
            t["phi"] = cut(2048, 1024, "p (t c) -> p t c", t=TB)
            t["k2"] = cut(3072, 1024, "p (k c h q) -> p k c h q", k=KD, c=NCK, h=2)
            t["st"] = cut(4096, 816, "p (c n) -> p c n", c=NCK - 1)
            t["ps"] = ctx.enter_context(nc.psum_tensor(f"ps{n}", [P, 4, 512], F32))
            t["sem"] = {k: held.enter_context(nc.semaphore(f"{k}_{n}")) for k in SIGNALS}
            L.append(t)

        pads_out = sem("pads_out")
        consts_in = sem("consts_in")
        init_pool = sem("init_pool")
        init_dve = sem("init_dve")
        init_pe = sem("init_pe")
        N_CONST = 12

        def after(eng, t, name, it, k):
            eng.wait_ge(t["sem"][name], it * SIGNALS[name] + k + STARTS.get(name, 0))

        def windows(x, half):
            return bass.AP(x[:, :, :].tensor, x[:, half, 0:1].offset, [x[:, :, :].ap[0], [WQ, NW], [0, HG], [1, WIN]])

        def carry(eng, t, col):
            eng.tensor_tensor(t["small"][:, col:col + 1], table("row"), table("row"), ALU.add)

        def lane_psum(t, bank, lo, hi):
            return t["ps"][:, bank, lo:hi]

        def spread_queries(eng, t, half):
            return eng.tensor_tensor(t["qp"][:, half],
                                     t["kT"][:, half, RADIUS:RADIUS + S].rearrange("p (c q) -> p c q", c=NCK)
                                     .unsqueeze(2).broadcast_to([P, NCK, 4, CK]),
                                     table("hp4").unsqueeze(1).unsqueeze(3).broadcast_to([P, NCK, 4, CK]), ALU.mult)

        def turns(programs):
            while programs:
                programs = [program for program in programs if next(program) == STEP]

        def interleave(engine, batch, next_batch):
            joined, ahead = JOINED[engine], AHEAD[engine]
            for phase in range(N_FIRST, N_PHASES):
                if phase - 1 not in joined:
                    last = phase
                    while last in joined:
                        last += 1
                    if last == phase:
                        turns(batch)
                    else:
                        for program in batch:
                            for _ in range(phase, last + 1):
                                turns([program])
                for _ in range(ahead.get(phase, 0)):
                    turns(next_batch)
            for program in batch + next_batch:
                assert next(program, "end") == "end"

        def begin(programs):
            for _ in range(N_FIRST):
                turns(programs)

        programs = ctx.enter_context(ExitStack())
        block = programs.enter_context(nc.Block())

        @block.sync
        def _(sp):
            for dst, src in (
                (tab[:, :], a["tables"]), (w[:, :, :, :], a["proj"]), (wr[:, :, :], a["router"]),
                (bo[:, :, :], a["bo"].partition_broadcast(P)), (cols[:, :, :], a["cols"]),
                (fbias[:, :], a["fbias"].partition_broadcast(P)),
                (wscale[:, :], a["wscale"].partition_broadcast(P)), (packed[:, :], a["packed"]),
                (maski[:, 0, :], a["mask"][0:P, :]), (maski[:, 1, :], a["mask"][P:2 * P, :]),
            ):
                sp.dma_start(dst, src).then_inc(consts_in, 16)

            def load_x(n, batch):
                sp.dma_start(L[n]["xin"][:, :, :], a["x"][bass.ds(batch, 1)].rearrange("o (t p) c -> p (o t) c", p=P)) \
                  .then_inc(L[n]["sem"]["x_in"], 16)

            def load(n, batch, it, first):
                t = L[n]
                if not first:
                    after(sp, t, "x_first", it, 1)
                    after(sp, t, "cv_sb", it, 2)
                    after(sp, t, "ctx_ps", it, 1)
                for r, (lo, n_c) in enumerate(((0, SC), (SC, SC), (2 * SC, CREP - 2 * SC))):
                    sp.dma_start(t["crep"][:, :, lo:lo + n_c], a["ctxT"][bass.ds(batch, 1), :, :, 0:n_c]
                                 .rearrange("o p k s -> (o p) k s")).then_inc(t["sem"]["ctx_in"], 16)
                load_x(n, batch)

            sp.wait_ge(init_pool, N_POOL)
            for n in range(LANES):
                for lo, hi in ((0, RADIUS), (RADIUS + S, SPAD)):
                    sp.dma_start(v_dram[n, lo:hi, :], L[n]["hT"][0:hi - lo, 0, 0:D]).then_inc(pads_out, 16)
            sp.wait_ge(pads_out, 16 * 2 * LANES)

            def value_windows(n, it):
                t = L[n]
                after(sp, t, "v_sb", it, 1)
                sp.dma_start(v_dram[n, RADIUS:RADIUS + S, :].rearrange("(t p) c -> p t c", p=P), t["o"][:, :, :]) \
                  .then_inc(t["sem"]["v_out"], 16)
                after(sp, t, "v_out", it, 16)
                rows = v_dram[n, 0:WIN, :]
                for h in range(HG):
                    sp.dma_start(t["vw"][h * WIN:(h + 1) * WIN], bass.AP(rows.tensor, rows.offset, [[D, WIN], [WQ * D, NW], [1, D]])) \
                      .then_inc(t["sem"]["v_win"], 16)

            def store(n, batch, it):
                t = L[n]
                after(sp, t, "x_done", it, 1)
                sp.dma_start(x5_dram[bass.ds(batch, 1)].rearrange("o p c -> (o p) c"),
                             t["x"][:, :, :].rearrange("p t c -> p (t c)")).then_inc(t["sem"]["stored"], 16)

            for n in range(LANES):
                load(n, n, 0, True)
            with sp.Fori(0, ITERS - 1) as it:
                for n in range(LANES):
                    value_windows(n, it)
                for n in range(LANES):
                    load(n, it * LANES + LANES + n, it, False)
                for n in range(LANES):
                    store(n, it * LANES + n, it)
            for n in range(LANES):
                value_windows(n, ITERS - 1)
            for n in range(LANES):
                after(sp, L[n], "x_first", ITERS - 1, 1)
                load_x(n, n)
            for n in range(LANES):
                store(n, (ITERS - 1) * LANES + n, ITERS - 1)
            for n in range(LANES):
                sp.wait_ge(L[n]["sem"]["stored"], SIGNALS["stored"] * ITERS + STARTS["stored"])

        @block.gpsimd
        def _(pool):
            for t in L:
                for k, (name, start) in enumerate(STARTS.items()):
                    pool.memset(t["small"][:, 505 + k:506 + k], 0.0).then_inc(t["sem"][name], start)
                pool.memset(t["qT"][:, :, :], 0.0).then_inc(init_pool, 1)
                pool.memset(t["kg"][:, :, :, :], 0.0).then_inc(init_pool, 1)
                pool.memset(t["hT"][:, :, :], 0.0).then_inc(init_pool, 1)
                pool.memset(t["v1"][:, :, :, :], 1.0).then_inc(init_pool, 1)
            pool.wait_ge(consts_in, 16 * 10)
            for t in L:
                for layer in range(2):
                    pool.tensor_copy(t["vbd"][:, layer, :, :, DH:DV],
                                     table("vmask").rearrange("p (c h) -> p c h", h=VH).unsqueeze(3)).then_inc(init_pool, 1)
                for c in range(NCK):
                    pool.tensor_copy(t["v1bd"][:, c, :, :, DH:DV],
                                     table("rm2").unsqueeze(1).broadcast_to([P, NPAIR, 2]).unsqueeze(3)).then_inc(init_pool, 1)

            def lane(n, it, first):
                t = L[n]
                for phase in range(N_FIRST) if first else range(N_FIRST, N_PHASES):
                    if phase == CTX_PHASE:
                        after(pool, t, "ck_sb", it, 1)
                        for layer in range(2):
                            for half in range(KD):
                                pool.tensor_tensor(
                                    t["kbd"][:, layer, half], t["ck"][:, layer, half].unsqueeze(1).broadcast_to([P, 8, SC]),
                                    table("hm8").unsqueeze(2).broadcast_to([P, 8, SC]), ALU.mult) \
                                    .then_inc(t["sem"]["kbd"], 1)
                    if phase in NORM_PHASES:
                        k = NORM_PHASES.index(phase) + 1
                        after(pool, t, "var", it, k)
                        carry(pool, t, 450 + phase)
                        base = STATS_FIRST if first else 0
                        rstd = t["small"][:, base + 20:base + 22]
                        pool.tensor_scalar(rstd.unsqueeze(2),
                                           t["small"][:, base + 16:base + 20].rearrange("p (t m) -> p t m", m=2)[:, :, 1:2],
                                           EPS_LN, None, ALU.add).then_inc(t["sem"]["rstd"], 1)
                        after(pool, t, "rstd", it, 2 * k - 1)
                        pool.tensor_tensor(rstd, rstd, table("power"), ALU.pow).then_inc(t["sem"]["rstd"], 1)
                    if phase in BIAS_PHASES:
                        i = BIAS_PHASES.index(phase)
                        after(pool, t, "norm", it, (2, 5)[i])
                        pool.tensor_tensor(t["x"][:, :, :], t["x"][:, :, :], bo[:, i].unsqueeze(1).broadcast_to([P, TB, D]),
                                           ALU.add).then_inc(t["sem"]["x_bo"], 1)
                    if phase == QKV_PHASE:
                        after(pool, t, "q_sb", it, 1)
                        pool.tensor_tensor(t["qbd"][:, 0], windows(t["qT"], 0),
                                           table("hm4").unsqueeze(1).unsqueeze(3).broadcast_to([P, NW, HG, WIN]), ALU.mult) \
                            .then_inc(t["sem"]["qbd0"], 1)
                    if phase == QKV_PHASE + 1:
                        after(pool, t, "v_win", it, 16 * HG)
                        vw = t["vw"].rearrange("p j (g h d) -> p (j g) h d", h=HG, d=DH)
                        pool.tensor_tensor(vw, vw, table("rm4").unsqueeze(1).unsqueeze(3).broadcast_to([P, NU, HG, DH]), ALU.mult) \
                            .then_inc(t["sem"]["vw_sb"], 1)
                    if phase in SOFTMAX_PHASES:
                        i = SOFTMAX_PHASES.index(phase)
                        after(pool, t, "max1", it, i + 1)
                        mx = t["small"][:, 144:160]
                        pool.tensor_tensor(t["s"][:, 1], t["s"][:, 1], mx.unsqueeze(2).broadcast_to([P, H, SC]), ALU.subtract) \
                            .then_inc(t["sem"]["shift1"], 1)
                    if phase == ROT_PHASE:
                        for tile in range(TB):
                            after(pool, t, "rot_a", it, tile + 1)
                            pool.tensor_tensor(t["rotA"][:, tile], t["rotA"][:, tile], t["rotB"][:, tile], ALU.add) \
                                .then_inc(t["sem"]["rot"], 1)
                    if phase == QP_PHASE:
                        after(pool, t, "phiqT", it, 1)
                        spread_queries(pool, t, 1).then_inc(t["sem"]["qp"], 1)
                    if phase == N_PHASES - 1:
                        after(pool, t, "pos", it, 1)
                        carry(pool, t, 450 + phase)
                        for i in range(2):
                            for tile in range(TB):
                                pool.indirect_dma_start(
                                    hs_dram[:, :], bass.IndirectOffsetOnAxis(ap=t["posi"][:, i, tile:tile + 1], axis=0),
                                    t["h6"][:, tile, :], None).then_inc(t["sem"]["sorted"], 16)
                    yield

            begin([lane(n, 0, True) for n in range(LANES)])
            with pool.Fori(0, ITERS) as it:
                interleave("Pool", [lane(n, it, False) for n in range(LANES)], [lane(n, it + 1, True) for n in range(LANES)])
                for t in L:
                    after(pool, t, "sorted", it, SIGNALS["sorted"])

        @block.scalar
        def _(act):
            act.wait_ge(consts_in, 16 * 10)
            act.wait_ge(init_pool, N_POOL)

            def norm_T(t, it, k, dst, lo, bank=0):
                yield
                after(act, t, "hT_ps", it, k)
                act.activation(dst[:, :, lo:lo + S], t["ps"][:, bank, :].rearrange("p (k c) -> p k c", k=KD), ACT.Copy) \
                    .then_inc(t["sem"]["hT"], 1)

            def out_T(t, it, k, bias):
                after(act, t, "oT_ps", it, k)
                src = t["ps"][:, 0, :].rearrange("p (k c) -> p k c", k=KD)
                if bias is None:
                    last = act.activation(t["oT"][:, :, :], src, ACT.Copy)
                else:
                    for half in range(KD):
                        last = act.activation(t["oT"][:, half], src[:, half], ACT.Identity, bias=cols[:, bias, half:half + 1])
                last.then_inc(t["sem"]["oT_sb"], 1)

            def lane(n, it, first):
                t = L[n]
                s = t["sem"]
                if first:
                    yield
                    yield from norm_T(t, it, 1, t["hT"], RADIUS, bank=2)
                    yield
                    after(act, t, "q_ps", it, 1)
                    act.activation(t["qT"][:, :, RADIUS:RADIUS + S], lane_psum(t, 1, 0, 512).rearrange("p (k c) -> p k c", k=KD),
                                   ACT.Copy).then_inc(s["q_sb"], 1)
                    after(act, t, "kv_ps", it, 1)
                    for g in range(2):
                        last = act.activation(t["kg"][:, :, g, RADIUS:RADIUS + S],
                                              lane_psum(t, 2, 0, 512).rearrange("p (k c) -> p k c", k=KD), ACT.Copy,
                                              scale=table("hg2")[:, g:g + 1])
                    last.then_inc(s["k_sb"], 1)
                    after(act, t, "kv_ps", it, 2)
                    act.activation(t["o"][:, :, :], lane_psum(t, 3, 0, 512).rearrange("p (t c) -> p t c", t=TB), ACT.Copy) \
                        .then_inc(s["v_sb"], 1)
                    yield
                    return
                after(act, t, "shift", it, 1)
                act.activation(t["s0"], t["s0"], ACT.Exp, scale=L0_SCALE).then_inc(s["prob"], 1)
                yield
                after(act, t, "ctx_ps", it, 1)
                for layer in range(2):
                    for half in range(KD):
                        i = (layer * KD + half) * SC
                        last = act.activation(t["ck"][:, layer, half], lane_psum(t, 1, i, i + SC), ACT.Identity,
                                              bias=cols[:, 2 * layer + 1, half:half + 1])
                last.then_inc(s["ck_sb"], 1)
                yield
                after(act, t, "oT_ps", it, 1)
                full = (NW - 1) * WQ
                for g in range(2):
                    r = slice(g * 64, (g + 1) * 64)
                    act.activation(t["oT"][r, :, 0:full].rearrange("p f (j q) -> p f j q", q=WQ),
                                   t["ps"][r, 0:2, 0:2 * full].rearrange("p f (j g q) -> p f j g q", g=2, q=WQ)[:, :, :, g], ACT.Copy)
                    last = act.activation(t["oT"][r, :, full:S], t["ps"][r, 0:2, 2 * full + g * QLAST:2 * full + (g + 1) * QLAST],
                                          ACT.Copy)
                last.then_inc(s["oT_sb"], 1)
                yield

                def cross(i, sub):
                    yield from norm_T(t, it, sub + 1, t["hT"], RADIUS)
                    yield
                    after(act, t, "q_ps", it, 2 + i)
                    for half in range(KD):
                        last = act.activation(t["kT"][:, half, RADIUS:RADIUS + S], lane_psum(t, 1, half * S, half * S + S),
                                              ACT.Identity, bias=cols[:, 2 * i, half:half + 1])
                    last.then_inc(s["q_sb"], 1)
                    yield
                    yield
                    for tile in range(TB):
                        after(act, t, ("shift", "shift1")[tile], it, (2, 1)[tile] + i)
                        act.activation(t["sflat"][:, tile], t["sflat"][:, tile], ACT.Exp, scale=DH ** -0.5) \
                            .then_inc(s["prob"], 1)
                    yield
                    for tile in range(TB):
                        after(act, t, "pT_ps", it, TB * i + tile + 1)
                        rest = HS - (NC_CH - 1) * P
                        flat = t["pT"][:, tile].rearrange("p c q -> p (c q)")
                        act.activation(flat[:, 0:4 * P], lane_psum(t, 0, 0, 512), ACT.Copy)
                        act.activation(flat[:, 4 * P:8 * P], lane_psum(t, 1, 0, 512), ACT.Copy)
                        act.activation(flat[:, 8 * P:9 * P], lane_psum(t, 2, 0, P), ACT.Copy)
                        act.activation(flat[0:rest, 9 * P:10 * P], t["ps"][0:rest, 2, P:2 * P], ACT.Copy) \
                            .then_inc(s["pT_sb"], 1)
                        yield
                        yield
                    out_T(t, it, 2 if i == 0 else 4, 4 + i)
                    yield

                yield from cross(0, 1)
                yield
                yield
                yield
                yield from norm_T(t, it, 4, t["hT"], RADIUS)
                yield
                after(act, t, "hT", it, 4)
                for half in range(KD):
                    act.activation(t["hrep1"][:, half].rearrange("p c (h q) -> p c h q", h=2),
                                   t["hT"][:, half, RADIUS:RADIUS + S].rearrange("p (c q) -> p c q", c=NCK)
                                   .unsqueeze(2).broadcast_to([P, NCK, 2, CK]), ACT.Copy).then_inc(s["hrep1"], 1)
                for tile in range(TB):
                    after(act, t, "phi", it, tile + 1)
                    act.activation(t["rotB"][:, tile], t["rotB"][:, tile], ACT.Exp).then_inc(s["expn"], 1)
                yield
                for j in range(TB):
                    after(act, t, "v1_bd", it, j + 1)
                    for r in range(2):
                        src = t["ps"][r * CK:(r + 1) * CK, 1 + j, r * D:(r + 1) * D]
                        last = act.activation(t["v1"][r * CK:(r + 1) * CK, j, :, 0:DH],
                                              src.rearrange("p (h d) -> p h d", h=H), ACT.Copy)
                last.then_inc(s["v1_sb"], 1)
                after(act, t, "phiT_ps", it, 1)
                act.activation(t["kT"][:, :, RADIUS:RADIUS + S], lane_psum(t, 0, 0, 512).rearrange("p (k c) -> p k c", k=KD),
                               ACT.Copy).then_inc(s["phiqT"], 1)
                for h in range(2):
                    last = act.activation(t["k2"][:, :, :, h, :],
                                          lane_psum(t, 3, 0, 512).rearrange("p (k c q) -> p k c q", k=KD, c=NCK), ACT.Copy, scale=table("hm2")[:, h:h + 1])
                last.then_inc(s["phiT_sb"], 1)
                yield
                yield
                yield
                yield
                out_T(t, it, 3, None)
                yield
                yield from cross(1, 4)
                yield from norm_T(t, it, 6, t["oT"], 0)
                yield
                after(act, t, "r_shift", it, 1)
                act.activation(t["small"][:, 320:336], t["small"][:, 320:336], ACT.Exp).then_inc(s["r_exp"], 1)
                yield
                yield

            begin([lane(n, 0, True) for n in range(LANES)])
            with act.Fori(0, ITERS) as it:
                interleave("ScalarE", [lane(n, it, False) for n in range(LANES)], [lane(n, it + 1, True) for n in range(LANES)])

        @block.tensor
        def _(pe):
            pe.wait_ge(consts_in, 16 * 10)
            pe.wait_ge(init_pool, N_POOL)
            pe.wait_ge(init_dve, N_DVE_INIT)
            ident = table("ident")

            t0 = L[0]
            tern = t0["work"][0:64, 0:512].bitcast(BF16)
            psb = t0["ps"][:, 0, :].bitcast(BF16)
            for shift in range(4):
                for k in range(KD):
                    last = pe.transpose(psb[:, k * D + shift * 64:k * D + shift * 64 + 64],
                                        tern[:, shift * D + k * P:shift * D + k * P + P], identb[0:64, 0:64])
            last.then_inc(init_pe, 1)
            pe.wait_ge(init_dve, N_DVE_INIT + 1)

            def norm_T(t, it, k, src, bank=0):
                yield
                after(pe, t, "norm", it, k)
                for kk in range(KD):
                    for tile in range(TB):
                        last = pe.transpose(lane_psum(t, bank, kk * S + tile * P, kk * S + tile * P + P),
                                            src[:, tile, kk * P:(kk + 1) * P], ident)
                last.then_inc(t["sem"]["hT_ps"], 1)

            def out_T(t, it, k):
                for kk in range(KD):
                    for tile in range(TB):
                        last = pe.transpose(lane_psum(t, 0, kk * S + tile * P, kk * S + tile * P + P),
                                            t["o"][:, tile, kk * P:(kk + 1) * P], ident)
                last.then_inc(t["sem"]["oT_ps"], 1)

            def out_proj(t, it, k, bank, mat):
                after(pe, t, "oT_sb", it, k)
                for tile in range(TB):
                    for half in range(KD):
                        last = pe.matmul(lane_psum(t, bank, tile * D, tile * D + D), t["oT"][:, half, tile * P:(tile + 1) * P],
                                         w[:, mat, half, :], start=(half == 0), stop=(half == KD - 1))
                last.then_inc(t["sem"]["y_ps"], 1)

            def feature_proj(t, bank, mat, hT):
                for half in range(KD):
                    for k in range(KD):
                        last = pe.matmul(lane_psum(t, bank, half * S, half * S + S), w[:, mat, k, half * P:(half + 1) * P],
                                         hT[:, k, RADIUS:RADIUS + S], start=(k == 0), stop=(k == KD - 1))
                return last

            def lane(n, it, first):
                t = L[n]
                s = t["sem"]
                hT = t["hT"]
                if first:
                    yield
                    yield from norm_T(t, it, 1, t["h"], bank=2)
                    yield
                    after(pe, t, "hT", it, 1)
                    feature_proj(t, 1, W0Q, hT).then_inc(s["q_ps"], 1)
                    feature_proj(t, 2, W0K, hT).then_inc(s["kv_ps"], 1)
                    for tile in range(TB):
                        for k in range(KD):
                            last = pe.matmul(lane_psum(t, 3, tile * D, tile * D + D), hT[:, k, RADIUS + tile * P:RADIUS + (tile + 1) * P],
                                             w[:, W0V, k, :], start=(k == 0), stop=(k == KD - 1))
                    last.then_inc(s["kv_ps"], 1)
                    yield
                    return
                after(pe, t, "pos", it, 0)
                after(pe, t, "qbd0", it, 1)
                after(pe, t, "qbd1", it, 1)
                after(pe, t, "k_sb", it, 1)
                for u in range(NW * KD):
                    j, half = u // KD, u % KD
                    last = pe.matmul(lane_psum(t, u // 8, u % 8 * 2 * WIN, (u % 8 + 1) * 2 * WIN),
                                     t["qbd"][:, half, j].rearrange("p h q -> p (h q)"), t["kg"][:, half, :, j * WQ:j * WQ + WIN],
                                     start=True, stop=True)
                last.then_inc(s["s_ps"], 1)
                yield
                after(pe, t, "s_sb", it, 1)
                after(pe, t, "v_sb", it, 1)
                after(pe, t, "ctx_in", it, 48)
                for layer in range(2):
                    for half in range(KD):
                        i = (layer * KD + half) * SC
                        for k in range(KD):
                            last = pe.matmul(lane_psum(t, 1, i, i + SC), w[:, (X0K, X1K)[layer], k, half * P:(half + 1) * P],
                                             t["crep"][:, k, 0:SC], start=(k == 0), stop=(k == KD - 1))
                last.then_inc(s["ctx_ps"], 1)
                for c in range(NC_CH):
                    h0, n_rows = chunk_heads(c)
                    nh = min(VH, H - h0)
                    off = P * c % SC
                    at = c % CB * 2 * VH * DH
                    dst = t["ps"][0:n_rows, (2, 3)[c // CB], at:at + 2 * VH * DH].rearrange("p (l n) -> p l n", l=2)
                    for k in range(KD):
                        last = pe.matmul(dst[:, :, 0:nh * DH], t["crep"][:, k, off:off + n_rows],
                                         w[:, X0V:X1V + 1:X1V - X0V, k, h0 * DH:(h0 + nh) * DH],
                                         start=(k == 0), stop=(k == KD - 1))
                    if c % CB == CB - 1:
                        last.then_inc(s["ctx_ps"], 1)
                yield
                after(pe, t, "ck_sb", it, 1)
                after(pe, t, "pT_sb0", it, 1)
                after(pe, t, "vw_sb", it, 1)
                pT = t["pT0"].rearrange("p (j f g) k -> p j f g k", f=KD, g=2)

                def window_out(half, j, n_j, n_q):
                    lo = (j + 1 - n_j) * 2 * WQ
                    dst = lane_psum(t, half, lo, lo + n_j * 2 * n_q).rearrange("p (j g q) -> p j g q", j=n_j, g=2)
                    return pe.matmul(dst, t["vw"][:, j, half * P:(half + 1) * P],
                                     pT[:, j + 1 - n_j:j + 1, half, :, RADIUS:RADIUS + n_q], start=True, stop=True)

                for half in range(KD):
                    window_out(half, NW - 1, 1, QLAST)
                    for j in range(NW - 2, 0, -1):
                        window_out(half, j, 2, WQ)
                    last = window_out(half, 0, 1, WQ)
                last.then_inc(s["oT_ps"], 1)
                after(pe, t, "cv_sb", it, 2)
                out_proj(t, it, 1, 2, W0O)
                yield

                def cross(i, sub):
                    yield from norm_T(t, it, sub + 1, t["h"])
                    yield
                    after(pe, t, "hT", it, sub + 1)
                    feature_proj(t, 1, (X0Q, X1Q)[i], hT).then_inc(s["q_ps"], 1)
                    yield
                    after(pe, t, "q_sb", it, 2 + i)
                    after(pe, t, "kbd", it, 4)
                    for tile in range(TB):
                        if tile:
                            after(pe, t, "s_sb", it, 1 + TB * i + tile)
                        for g in range(4):
                            last = pe.matmul(lane_psum(t, g, 0, 4 * SC),
                                             t["kT"][:, g // 2, RADIUS + tile * P:RADIUS + (tile + 1) * P],
                                             t["kbd"][:, i, g // 2, g % 2 * 4:g % 2 * 4 + 4, :], start=True, stop=True)
                        last.then_inc(s["s_ps"], 1)
                        yield
                    for tile in range(TB):
                        after(pe, t, "prob", it, 2 + TB * i + tile)
                        if tile == 0:
                            after(pe, t, "s_sb", it, 1 + TB * (i + 1))
                        else:
                            after(pe, t, "pT_sb", it, TB * i + tile)
                        for c in range(NC_CH):
                            n_rows = chunk_heads(c)[1]
                            last = pe.transpose(t["ps"][0:n_rows, c // 4, c % 4 * P:c % 4 * P + P],
                                                t["sflat"][:, tile, c * P:c * P + n_rows], ident)
                        last.then_inc(s["pT_ps"], 1)
                        yield
                        after(pe, t, "pT_sb", it, TB * i + tile + 1)
                        if tile:
                            after(pe, t, "o_sb", it, (0 if i == 0 else 4) + tile)
                        for c in range(NC_CH):
                            h0, n_rows = chunk_heads(c)
                            nh = min(VH, H - h0)
                            last = pe.matmul(lane_psum(t, 3, h0 * DV, (h0 + nh) * DV), t["pT"][0:n_rows, tile, c, :],
                                             t["vbd"][0:n_rows, i, c, 0:nh, :], start=(c == 0), stop=(c == NC_CH - 1),
                                             skip_group_check=True)
                        last.then_inc(s["o_ps"], 1)
                        yield
                    after(pe, t, "o_sb", it, (2 if i == 0 else 6))
                    out_T(t, it, 0)
                    out_proj(t, it, (2 if i == 0 else 4), 1, (X0O, X1O)[i])
                    yield

                yield from cross(0, 1)
                yield
                after(pe, t, "norm", it, 3)
                psb = t["ps"][:, 0, :].bitcast(BF16)
                for kk in range(KD):
                    for tile in range(TB):
                        last = pe.transpose(psb[:, kk * S + tile * P:kk * S + tile * P + P],
                                            t["hq"][:, tile, kk * P:(kk + 1) * P], identb[:, :])
                last.then_inc(s["hT_ps"], 1)
                yield
                after(pe, t, "hT", it, 3)
                for tile in range(TB):
                    for k in range(KD):
                        last = pe.matmul(lane_psum(t, 1, tile * D, tile * D + D), t["hTb"][:, k, tile * P:(tile + 1) * P],
                                         ternT[:, k, :], start=(k == 0), stop=(k == KD - 1))
                last.then_inc(s["y_ps"], 1)
                yield
                yield from norm_T(t, it, 4, t["h"])
                yield
                after(pe, t, "hT", it, 4)
                for tile in range(TB):
                    for k in range(KD):
                        last = pe.matmul(lane_psum(t, 1 + tile, 0, 512), hT[:, k, RADIUS + tile * P:RADIUS + (tile + 1) * P],
                                         w[:, W1Q:W1K + 1, k, :], start=(k == 0), stop=(k == KD - 1))
                    last.then_inc(s["qk_ps"], 1)
                yield
                after(pe, t, "rot_a", it, 2)
                after(pe, t, "hrep1", it, 2)
                for c in range(NCK):
                    for k in range(KD):
                        last = pe.matmul(lane_psum(t, 1 + c // 2, c % 2 * D, c % 2 * D + D), t["hrep1"][:, k, c], w[:, W1V, k, :],
                                         start=(k == 0), stop=(k == KD - 1))
                    if c % 2:
                        last.then_inc(s["v1_ps"], 1)
                after(pe, t, "phi", it, 4)
                for part, bank in ((0, 0), (1, 3)):
                    for kk in range(KD):
                        for tile in range(TB):
                            last = pe.transpose(lane_psum(t, bank, kk * S + tile * P, kk * S + tile * P + P),
                                                t["phi"][:, tile, part * D + kk * P:part * D + (kk + 1) * P], ident)
                last.then_inc(s["phiT_ps"], 1)
                yield
                after(pe, t, "phiT_sb", it, 1)
                after(pe, t, "v1_sb", it, 1)
                after(pe, t, "v1_bd", it, 2)
                after(pe, t, "qp", it, 2)
                for c in range(NCK):
                    for half in range(KD):
                        last = pe.matmul(lane_psum(t, c, half * 4 * CK, (half + 1) * 4 * CK),
                                         t["k2"][:, half, c].rearrange("p h q -> p (h q)"),
                                         t["qp"][:, half, c].rearrange("p r q -> p (r q)"), start=True, stop=True)
                last.then_inc(s["a_ps"], 1)
                yield
                for c in range(1, NCK):
                    after(pe, t, "a_sb", it, c)
                    for half in range(KD):
                        dst = lane_psum(t, c - 1, half * 8 * DV, (half + 1) * 8 * DV)
                        col = slice(D + half * P, D + (half + 1) * P)
                        hh = slice(half * 8, half * 8 + 8)
                        full = c // 2
                        if full:
                            last = pe.matmul(dst, t["phi"][:, 0, col], t["v1"][:, 0, hh, :], start=True, stop=(c % 2 == 0))
                        if c % 2:
                            last = pe.matmul(dst, t["phi"][0:CK, full, col], t["v1"][0:CK, full, hh, :],
                                             start=(full == 0), stop=True)
                    last.then_inc(s["st_ps"], 1)
                yield
                after(pe, t, "a_sb", it, 4)
                for c in range(NCK):
                    bank, r = (3, 0)[c // 2], CK * (c % 2)
                    if c:
                        after(pe, t, "st_sb", it, c)
                    for pr in range(NPAIR):
                        last = pe.matmul(t["ps"][r:r + CK, bank, pr * 2 * DV:(pr + 1) * 2 * DV],
                                         t["at"][:, c * NPAIR + pr, :], t["v1bd"][:, c, pr], start=(pr == 0),
                                         stop=(pr == NPAIR - 1 and c == 0), skip_group_check=True)
                    if c:
                        for half in range(KD):
                            last = pe.matmul(t["ps"][r:r + CK, bank, half * 8 * DV:(half + 1) * 8 * DV],
                                             t["kT"][:, half, RADIUS + c * CK:RADIUS + (c + 1) * CK],
                                             t["st"][:, c - 1, half * 8 * DV:(half + 1) * 8 * DV], start=False,
                                             stop=(half == KD - 1), skip_group_check=True)
                    if c % 2:
                        last.then_inc(s["o_ps"], 1)
                yield
                after(pe, t, "o_sb", it, 4)
                out_T(t, it, 0)
                out_proj(t, it, 3, 1, W1O)
                yield
                yield from cross(1, 4)
                yield from norm_T(t, it, 6, t["h6"])
                yield
                after(pe, t, "hT", it, 6)
                for tile in range(TB):
                    for k in range(KD):
                        last = pe.matmul(lane_psum(t, 0, tile * E, (tile + 1) * E),
                                         t["oT"][:, k, tile * P:(tile + 1) * P], wr[:, k, :],
                                         start=(k == 0), stop=(k == KD - 1))
                last.then_inc(s["r_ps"], 1)
                yield
                after(pe, t, "x_done", it, 1)
                pe.matmul(lane_psum(t, 0, 0, TB * E), table("before"), t["small"][:, 402:402 + TB * E], start=True, stop=True)
                pe.matmul(lane_psum(t, 0, TB * E, 2 * TB * E), table("ones"), t["small"][:, 402:402 + TB * E],
                          start=True, stop=True).then_inc(s["r_ps"], 1)
                yield

            begin([lane(n, 0, True) for n in range(LANES)])
            with pe.Fori(0, ITERS) as it:
                interleave("TensorE", [lane(n, it, False) for n in range(LANES)], [lane(n, it + 1, True) for n in range(LANES)])

        @block.vector
        def _(dve):
            dve.wait_ge(consts_in, 16 * 10)
            steps = [0]

            def init(ins):
                steps[0] += 1
                ins.then_inc(init_dve, 1)
                dve.wait_ge(init_dve, steps[0])

            init(dve.tensor_copy(identb[:, :], table("ident")))
            init(dve.tensor_copy(next_row[:, :], table("first_row")))
            maskf = L[0]["work"][:, 1024:1024 + TB * SC].rearrange("p (t s) -> p t s", t=TB)
            init(dve.tensor_copy(maskf, maski[:, :, :]))
            init(dve.tensor_scalar(maskf, maskf, 0.0, None, ALU.is_equal))
            init(dve.tensor_scalar(bound0[:, :, :], maskf, -BIG, BIG, ALU.mult, ALU.add))
            init(dve.tensor_scalar(maskf, maskf, -1e10 * DH ** 0.5, None, ALU.mult))
            init(dve.tensor_tensor(bound0[:, :, :], bound0[:, :, :], maskf, ALU.add))
            init(dve.tensor_scalar(wscale127[:, :], wscale[:, :], 1.0 / 127.0, None, ALU.mult))
            codes = L[0]["work"][0:64, 2048:3072].bitcast(I32)
            for shift in range(4):
                init(dve.tensor_scalar(codes[:, shift * D:(shift + 1) * D], packed[:, :], 2 * shift, 3,
                                       ALU.logical_shift_right, ALU.bitwise_and))
            tern = L[0]["work"][0:64, 0:512].bitcast(BF16)
            init(dve.tensor_scalar(tern, codes, -1.0, None, ALU.add))
            assert steps[0] == N_DVE_INIT, steps
            dve.wait_ge(init_pe, 1)
            init(dve.tensor_copy(ternT[:, :, :], L[0]["ps"][:, 0, :].bitcast(BF16)[:, 0:KD * D]
                                 .rearrange("p (k c) -> p k c", k=KD)))

            def lane(n, it, first):
                t = L[n]
                s = t["sem"]
                count, norms = [0], {n: 0 if first else 1}
                small = t["small"]

                def link(ins):
                    count[0] += 1
                    ins.then_inc(s["dve_step"], 1)
                    after(dve, t, "dve_step", it, count[0])

                def chain(ins):
                    count[0] += 1
                    k = count[0]
                    ins.then_inc(s["dve_step"], 1)
                    yield STEP
                    after(dve, t, "dve_step", it, k)

                def layernorm(x, dst, signal):
                    base = STATS_FIRST if first else 0
                    for tile in range(TB):
                        ins = dve.bn_stats(small[:, base + tile * 6:base + tile * 6 + 6], x[:, tile])
                    if first:
                        ins.then_inc(s["stats"], 1)
                        after(dve, t, "stats", it, 1)
                    else:
                        link(ins)
                    carry(dve, t, 440 + norms[n])
                    for tile in range(TB):
                        ins = dve.bn_aggr(small[:, base + 16 + tile * 2:base + 18 + tile * 2],
                                          small[:, base + tile * 6:base + tile * 6 + 6])
                    ins.then_inc(s["var"], 1)
                    norms[n] += 1
                    k = norms[n]
                    yield
                    after(dve, t, "rstd", it, 2 * k)
                    for tile in range(TB):
                        ins = dve.tensor_scalar(dst[:, tile], x[:, tile], small[:, base + 16 + 2 * tile:base + 17 + 2 * tile],
                                                small[:, base + 20 + tile:base + 21 + tile], ALU.subtract, ALU.mult)
                    if signal:
                        ins.then_inc(s["norm"], 1)
                    else:
                        link(ins)

                def residual(it_k, bank, x_old):
                    after(dve, t, "y_ps", it, it_k)
                    count[0] += 1
                    dve.tensor_tensor(t["x"][:, :, :].rearrange("p t c -> p (t c)"), lane_psum(t, bank, 0, 512),
                                      x_old[:, :, :].rearrange("p t c -> p (t c)"), ALU.add) \
                       .then_inc(s["dve_step"], 1)
                    after(dve, t, "dve_step", it, count[0])

                if first:
                    after(dve, t, "x_in", it, 16)
                    yield from layernorm(t["xin"], t["h"], True)
                    yield
                    yield
                    after(dve, t, "q_sb", it, 1)
                    dve.tensor_tensor(t["qbd"][:, 1], windows(t["qT"], 1),
                                      table("hm4").unsqueeze(1).unsqueeze(3).broadcast_to([P, NW, HG, WIN]), ALU.mult) \
                        .then_inc(s["qbd1"], 1)
                    yield
                    return
                after(dve, t, "s_ps", it, 1)
                ps = t["ps"][:, 0:3, :].rearrange("p b (u k) -> p (b u) k", k=WIN)
                dve.tensor_tensor(t["s0"][:, 0:NG], ps[:, 0:NG], table("band0").unsqueeze(1).broadcast_to([P, NG, WIN]), ALU.min)
                dve.tensor_tensor(t["s0"][:, NG:NU], ps[:, NG:NU], table("band").unsqueeze(1).broadcast_to([P, NU - NG, WIN]),
                                  ALU.min).then_inc(s["s_sb"], 1)
                after(dve, t, "s_sb", it, 1)
                link(dve.tensor_reduce(small[:, 64:64 + NU], t["s0"], AX_X, ALU.max))
                dve.tensor_tensor(t["s0"], t["s0"], small[:, 64:64 + NU].unsqueeze(2).broadcast_to([P, NU, WIN]),
                                  ALU.subtract).then_inc(s["shift"], 1)
                yield STEP
                after(dve, t, "prob", it, 1)
                link(dve.tensor_reduce(small[:, 64:64 + NU], t["s0"], AX_X, ALU.add))
                link(dve.reciprocal(small[:, 64:64 + NU], small[:, 64:64 + NU]))
                link(dve.tensor_tensor(t["s0"], t["s0"], small[:, 64:64 + NU].unsqueeze(2).broadcast_to([P, NU, WIN]),
                                       ALU.mult))
                dve.transpose(t["pT0"].rearrange("p u k -> p (u k)"), t["s0"].rearrange("p u k -> p (u k)")) \
                   .then_inc(s["pT_sb0"], 1)
                yield
                vm = table("vmask").rearrange("p (c h) -> p c h", h=VH)
                for part in range(2):
                    after(dve, t, "ctx_ps", it, part + 2)
                    ps = t["ps"][:, (2, 3)[part], 0:CB * 2 * VH * DH].rearrange("p (c l h d) -> p c l h d", c=CB, l=2, d=DH)
                    for layer in range(2):
                        full = CB - part
                        c0 = part * CB
                        last = dve.tensor_tensor(t["vbd"][:, layer, c0:c0 + full, :, 0:DH], ps[:, 0:full, layer],
                                                 vm[:, c0:c0 + full].unsqueeze(3).broadcast_to([P, full, VH, DH]), ALU.mult)
                        if part:
                            h0, nr = chunk_heads(NC_CH - 1)
                            nh = H - h0
                            last = dve.tensor_tensor(t["vbd"][0:nr, layer, NC_CH - 1, 0:nh, 0:DH], ps[0:nr, CB - 1, layer, 0:nh],
                                                     vm[0:nr, NC_CH - 1, 0:nh].unsqueeze(2).broadcast_to([nr, nh, DH]), ALU.mult)
                    last.then_inc(s["cv_sb"], 1)
                yield
                after(dve, t, "y_ps", it, 1)
                after(dve, t, "stored", it, 0)
                dve.tensor_tensor(t["x"][:, :, :].rearrange("p t c -> p (t c)"), lane_psum(t, 2, 0, 512),
                                  t["xin"][:, :, :].rearrange("p t c -> p (t c)"), ALU.add).then_inc(s["x_first"], 1)
                after(dve, t, "x_first", it, 1)
                yield

                def normalise(it_k, o_k, bank, tile, floor):
                    after(dve, t, "o_ps", it, o_k)
                    o = lane_psum(t, bank, 0, H * DV).rearrange("p (h d) -> p h d", d=DV)
                    rec = small[:, 160 + 16 * tile:176 + 16 * tile].unsqueeze(2)
                    if floor is None:
                        link(dve.reciprocal(rec, o[:, :, DH:DV]))
                    else:
                        link(dve.tensor_scalar(rec, o[:, :, DH:DV], floor, None, ALU.max))
                        link(dve.reciprocal(rec, rec))
                    dve.tensor_tensor(t["o"][:, tile].rearrange("p (h d) -> p h d", d=DH), o[:, :, 0:DH],
                                      rec.broadcast_to([P, H, DH]), ALU.mult).then_inc(s["o_sb"], 1)

                def cross(i, sub):
                    yield from layernorm(t["x"], t["h"], True)
                    yield
                    yield
                    bounds = bound0[:, :, :] if i == 0 else table("caus").rearrange("p (t s) -> p t s", t=TB)
                    for tile in range(TB):
                        after(dve, t, "s_ps", it, 2 + TB * i + tile)
                        ps = t["ps"][:, :, 0:4 * SC].rearrange("p g (h s) -> p g h s", s=SC)
                        bd = bounds[:, tile].unsqueeze(1).unsqueeze(1).broadcast_to([P, 4, 4, SC])
                        dst = t["s"][:, tile].rearrange("p (g h) s -> p g h s", g=4)
                        dve.tensor_tensor(dst, ps, bd, ALU.min).then_inc(s["s_sb"], 1)
                        if tile == 0:
                            yield
                    for tile in range(TB):
                        after(dve, t, "s_sb", it, 2 + TB * i + tile)
                        mx = small[:, 128 + 16 * tile:144 + 16 * tile]
                        if tile:
                            dve.tensor_reduce(mx, t["s"][:, tile], AX_X, ALU.max).then_inc(s["max1"], 1)
                            break
                        link(dve.tensor_reduce(mx, t["s"][:, tile], AX_X, ALU.max))
                        dve.tensor_tensor(t["s"][:, tile], t["s"][:, tile], mx.unsqueeze(2).broadcast_to([P, H, SC]),
                                          ALU.subtract).then_inc(s["shift"], 1)
                    yield
                    for tile in range(TB):
                        yield
                        normalise(it, (1 if i == 0 else 5) + tile, 3, tile, None)
                        yield
                    after(dve, t, "x_bo", it, i + 1)
                    residual(2 if i == 0 else 5, 1, t["x"])
                    yield

                yield from cross(0, 1)
                yield from layernorm(t["x"], t["h"], False)
                amax = small[:, 200:202]
                yield from chain(dve.tensor_reduce(amax, t["h"][:, :, :], AX_X, ALU.max, apply_absolute_value=True))
                yield from chain(dve.tensor_scalar(amax, amax, 1e-5, None, ALU.max))
                dve.tensor_scalar(small[:, 204:206], amax, wscale127[:, 0:1], None, ALU.mult)
                yield from chain(dve.reciprocal(small[:, 202:204], amax))
                yield from chain(dve.tensor_scalar(small[:, 202:204], small[:, 202:204], 127.0, None, ALU.mult))
                for tile in range(TB):
                    ins = dve.tensor_scalar(t["h"][:, tile], t["h"][:, tile], small[:, 202 + tile:203 + tile], MAGIC,
                                            ALU.mult, ALU.add)
                yield from chain(ins)
                dve.tensor_scalar(t["hq"], t["h"][:, :, :], -MAGIC, 127.0, ALU.add, ALU.min) \
                   .then_inc(s["norm"], 1)
                yield
                after(dve, t, "hT_ps", it, 3)
                dve.tensor_scalar(t["hTb"], t["ps"][:, 0, :].bitcast(BF16)[:, 0:KD * S]
                                  .rearrange("p (k c) -> p k c", k=KD), -128.0, None, ALU.max).then_inc(s["hT"], 1)
                yield STEP
                after(dve, t, "y_ps", it, 3)
                for tile in range(TB):
                    ins = dve.scalar_tensor_tensor(t["h"][:, tile], lane_psum(t, 1, tile * D, tile * D + D),
                                                   small[:, 204 + tile:205 + tile], fbias[:, :], ALU.mult, ALU.add)
                yield from chain(ins)
                yield from chain(dve.tensor_tensor(t["x"][:, :, :], t["x"][:, :, :], t["h"][:, :, :], ALU.add))
                yield
                yield from layernorm(t["x"], t["h"], True)
                yield
                rope = table("rope").rearrange("p (t c) -> p t c", t=TB)
                for tile in range(TB):
                    after(dve, t, "qk_ps", it, tile + 1)
                    qk = lane_psum(t, 1 + tile, 0, 512).rearrange("p (h d) -> p h d", d=DH)
                    rb = t["rotB"][:, tile].rearrange("p (h d) -> p h d", d=DH)
                    ra = t["rotA"][:, tile].rearrange("p (h r d) -> p h r d", r=2, d=8)
                    dve.tensor_tensor(rb[:, :, 0:8], qk[:, :, 8:16],
                                      rope[:, tile, 8:16].unsqueeze(1).broadcast_to([P, 32, 8]), ALU.mult)
                    dve.tensor_tensor(rb[:, :, 8:16], qk[:, :, 0:8],
                                      rope[:, tile, 16:24].unsqueeze(1).broadcast_to([P, 32, 8]), ALU.mult)
                    dve.tensor_tensor(ra, qk.rearrange("p h (r d) -> p h r d", r=2),
                                      rope[:, tile, 0:8].unsqueeze(1).unsqueeze(1).broadcast_to([P, 32, 2, 8]), ALU.mult) \
                       .then_inc(s["rot_a"], 1)
                yield STEP
                for tile in range(TB):
                    after(dve, t, "rot", it, tile + 1)
                    dve.tensor_scalar(t["rotB"][:, tile], t["rotA"][:, tile], 0.0, None, ALU.min).then_inc(s["phi"], 1)
                for tile in range(TB):
                    after(dve, t, "expn", it, tile + 1)
                    dve.scalar_tensor_tensor(t["phi"][:, tile], t["rotA"][:, tile], 0.0, t["rotB"][:, tile],
                                             ALU.max, ALU.add).then_inc(s["phi"], 1)
                yield
                for j in range(2):
                    after(dve, t, "v1_ps", it, j + 1)
                    dve.tensor_tensor(t["v1bd"][:, 2 * j:2 * j + 2, :, :, 0:DH].rearrange("p c q h d -> p (c q) h d"),
                                      lane_psum(t, 1 + j, 0, 512).rearrange("p (q h d) -> p q h d", h=2, d=DH),
                                      table("rm2").unsqueeze(1).unsqueeze(3).broadcast_to([P, 2 * NPAIR, 2, DH]), ALU.mult) \
                       .then_inc(s["v1_bd"], 1)
                after(dve, t, "phiqT", it, 1)
                spread_queries(dve, t, 0).then_inc(s["qp"], 1)
                yield
                after(dve, t, "a_ps", it, 1)
                for c in range(NCK):
                    dve.tensor_tensor(t["at"][:, c * NPAIR:(c + 1) * NPAIR],
                                      lane_psum(t, c, 0, 512).rearrange("p (u q) -> p u q", q=CK),
                                      table("tri").unsqueeze(1).broadcast_to([P, NPAIR, CK]), ALU.mult) \
                       .then_inc(s["a_sb"], 1)
                yield
                for c in range(1, NCK):
                    after(dve, t, "st_ps", it, c)
                    dve.tensor_tensor(t["st"][:, c - 1].rearrange("p (k h d) -> p k h d", k=KD, h=8),
                                      lane_psum(t, c - 1, 0, H * DV).rearrange("p (k h d) -> p k h d", k=KD, h=8),
                                      table("hm8").unsqueeze(1).unsqueeze(3).broadcast_to([P, KD, 8, DV]), ALU.mult) \
                       .then_inc(s["st_sb"], 1)
                yield
                for tile in range(TB):
                    normalise(it, 3 + tile, (3, 0)[tile], tile, 1e-6)
                yield
                residual(4, 1, t["x"])
                yield
                yield from cross(1, 4)
                yield from layernorm(t["x"], t["h6"], True)
                yield
                after(dve, t, "r_ps", it, 1)
                lg = small[:, 300:316].rearrange("p (t e) -> p t e", e=E)
                m1, m2 = small[:, 340:342], small[:, 342:344]
                r1 = small[:, 344:346]
                pr = small[:, 320:336].rearrange("p (t e) -> p t e", e=E)
                rk = small[:, 350:366].rearrange("p (t e) -> p t e", e=E)
                desc = table("desc").unsqueeze(1).broadcast_to([P, TB, E])
                wide = lambda v: v.unsqueeze(2).broadcast_to([P, TB, E])
                yield from chain(dve.tensor_copy(lg, lane_psum(t, 0, 0, TB * E).rearrange("p (t e) -> p t e", e=E)))
                yield from chain(dve.tensor_reduce(m1, lg, AX_X, ALU.max))
                dve.tensor_tensor(pr, lg, wide(m1), ALU.subtract).then_inc(s["r_shift"], 1)
                yield STEP
                after(dve, t, "r_exp", it, 1)
                yield from chain(dve.tensor_reduce(m1, pr, AX_X, ALU.add))
                yield from chain(dve.reciprocal(m1, m1))
                yield from chain(dve.tensor_tensor(pr, pr, wide(m1), ALU.mult))
                hot = [small[:, 370 + 16 * i:386 + 16 * i].rearrange("p (t e) -> p t e", e=E) for i in range(2)]
                for i, m in enumerate((m1, m2)):
                    yield from chain(dve.tensor_reduce(m, pr, AX_X, ALU.max))
                    yield from chain(dve.tensor_tensor(rk, pr, wide(m), ALU.is_equal))
                    yield from chain(dve.tensor_tensor(rk, rk, desc, ALU.mult))
                    yield from chain(dve.tensor_reduce(r1, rk, AX_X, ALU.max))
                    yield from chain(dve.tensor_tensor(hot[i], rk, wide(r1), ALU.is_equal))
                    if i == 0:
                        yield from chain(dve.tensor_scalar(rk, hot[i], 4.0, None, ALU.mult))
                        yield from chain(dve.tensor_tensor(pr, pr, rk, ALU.subtract))
                yield from chain(dve.tensor_tensor(r1, m1, m2, ALU.add))
                yield from chain(dve.tensor_scalar(r1, r1, 1e-6, None, ALU.add))
                yield from chain(dve.reciprocal(r1, r1))
                first = it * LANES * TB + n * TB
                chosen = small[:, 402:418].rearrange("p (t e) -> p t e", e=E)
                dve.tensor_tensor(chosen, hot[0], hot[1], ALU.add)
                for i, m in enumerate((m1, m2)):
                    ins = dve.tensor_tensor(gates[:, bass.ds(first, TB), i], m, r1, ALU.mult)
                ins.then_inc(s["x_done"], 1)
                yield
                after(dve, t, "r_ps", it, 2)
                place = small[:, 420:436].rearrange("p (t e) -> p t e", e=E)
                ranks = lane_psum(t, 0, 0, TB * E).rearrange("p (t e) -> p t e", e=E)
                totals = lane_psum(t, 0, TB * E, 2 * TB * E).rearrange("p (t e) -> p t e", e=E)
                for tile in range(TB):
                    link(dve.tensor_tensor(place[:, tile], ranks[:, tile], next_row[:, :], ALU.add))
                    link(dve.tensor_tensor(next_row[:, :], totals[:, tile], next_row[:, :], ALU.add))
                for i in range(2):
                    link(dve.tensor_tensor(rk, hot[i], place, ALU.mult))
                    link(dve.tensor_reduce(r1, rk, AX_X, ALU.add))
                    dve.tensor_copy(pos[:, bass.ds(first, TB), i], r1)
                    ins = dve.tensor_copy(t["posi"][:, i], r1) if i else link(dve.tensor_copy(t["posi"][:, i], r1))
                ins.then_inc(s["pos"], 1)
                yield
                assert count[0] == SIGNALS["dve_step"], count

            begin([lane(n, 0, True) for n in range(LANES)])
            with dve.Fori(0, ITERS) as it:
                interleave("VectorE", [lane(n, it, False) for n in range(LANES)], [lane(n, it + 1, True) for n in range(LANES)])

        programs.close()


def build_experts(nc, a, x5_dram, hs_dram, tab, table, gates, pos, next_row, out):
    with ExitStack() as ctx:
        sb = lambda name, shape, dt=F32: ctx.enter_context(nc.sbuf_tensor(name, shape, dt))
        sem = lambda name: ctx.enter_context(nc.semaphore(name))
        ys_dram = nc.dram_tensor("sorted_outputs", [NJ * P, D], F32).ap()
        NC = FF // P
        w13 = sb("w13", [P, E, KD, 2 * FF])
        w2 = sb("w2", [P, E, NC, D])
        hin = sb("hin", [P, 2, D])
        hT = sb("hT", [P, 2, KD, P])
        th = sb("th", [P, 2, FF])
        gated = sb("gated", [P, 2, FF])
        inner = sb("inner", [P, 2, FF])
        innerT = sb("innerT", [P, 2, NC, P])
        y = sb("y", [P, 2, D])
        zeros = sb("zeros", [P, D])
        ticks = sb("ticks", [P, E])
        pad_at = sb("pad_at", [P, E], I32)
        plan = sb("plan", [1, 2, NJ], I32)
        f = sb("plan_f", [1, 2, NJ])
        out_at = sb("out_at", [P, NT, 2])
        past = sb("past", [P, NT * 2, E])
        now, upto_e, inside, val = (sb(n, [1, NJ, E]) for n in ("now", "upto_e", "inside", "val"))
        e8 = sb("e8", [P, 7, E])
        padf = sb("padf", [P, E])
        back = sb("back", [P, NT, D])
        yback = sb("yback", [P, 2, 2, TB, D])
        at = sb("at", [P, 2, 2, TB], I32)
        gate = sb("gate", [P, 2, 2, TB])
        gu = ctx.enter_context(nc.psum_tensor("gu", [P, 2, 2, FF], F32))
        psT = ctx.enter_context(nc.psum_tensor("psT", [P, FF], F32))
        psH = ctx.enter_context(nc.psum_tensor("psH", [P, 512], F32))
        psY = ctx.enter_context(nc.psum_tensor("psY", [P, 2, 512], F32))

        weights_in = [sem(f"weights_in{q}") for q in range(2)]
        weights_ready = sem("weights_ready")
        plan_step = sem("plan_step")
        padded = sem("padded")
        h_in = [sem(f"h_in{q}") for q in range(2)]
        hT_ps, hT_sb = sem("e_hT_ps"), sem("e_hT_sb")
        gu_ps = sem("gu_ps")
        tanh = sem("tanh")
        gated_done = sem("gated_done")
        inner_sb = sem("inner_sb")
        innerT_ps, innerT_sb = sem("innerT_ps"), sem("innerT_sb")
        e_y_ps, e_y_sb = sem("e_y_ps"), sem("e_y_sb")
        y_stored = [sem(f"y_stored{q}") for q in range(2)]
        at_ready = sem("at_ready")
        gathered = [sem(f"gathered{q}") for q in range(2)]
        carried = sem("carried")
        x_back = sem("x_back")
        summed = sem("summed")
        out_stored = sem("out_stored")
        N_TILES = 16

        def landed(eng, sems, j, q, amount=16):
            eng.wait_ge(sems[q], (j - q) * (amount // 2) + amount)

        block = ctx.enter_context(nc.Block())

        @block.sync
        def _(sp):
            sp.wait_ge(plan_step, N_TILES)
            sp.wait_ge(padded, 16 * E)

            def load(j, q):
                row = sp.value_load(plan[0:1, 1, bass.ds(j, 1)], min_val=0, max_val=E * CAP - P)
                sp.dma_start(hin[:, q], hs_dram[bass.ds(row, P), :]).then_inc(h_in[q], 16)

            def store(j, q):
                sp.wait_ge(e_y_sb, j + 1)
                sp.dma_start(ys_dram[bass.ds(j * P, P), :], y[:, q]).then_inc(y_stored[q], 16)

            def step(j, q):
                sp.wait_ge(hT_ps, j)
                load(j + 1, 1 - q)
                store(j - 2, q)

            load(0, 0)
            load(1, 1)
            sp.wait_ge(hT_ps, 1)
            load(2, 0)
            step(2, 0)
            with sp.Fori(0, B) as b:
                step(2 * b + 3, 1)
                sp.dma_start(back[:, bass.ds(b * TB, TB), :].rearrange("p n c -> p (n c)"),
                             x5_dram[bass.ds(b, 1)].rearrange("o p c -> p (o c)")).then_inc(x_back, 16)
                step(2 * b + 4, 0)
            with sp.Fori(B, (NJ - 4) // 2) as i:
                step(2 * i + 3, 1)
                step(2 * i + 4, 0)
            store(NJ - 3, 1)
            store(NJ - 2, 0)
            store(NJ - 1, 1)

            def store_out(b):
                sp.wait_ge(summed, 2 * b + 2)
                sp.dma_start(out[bass.ds(b, 1)].rearrange("o (t p) c -> p (o t) c", p=P), back[:, bass.ds(b * TB, TB), :]) \
                  .then_inc(out_stored, 16)

            with sp.Fori(0, B) as b:
                store_out(b)
            sp.wait_ge(out_stored, 16 * B)
            for q in range(2):
                landed(sp, y_stored, NJ - 2 + q, q)

        @block.gpsimd
        def _(pool):
            def load_weights(e):
                pool.dma_start(w13[:, e], a["w13"][e]).then_inc(weights_in[e % 2], 16)
                pool.dma_start(w2[:, e], a["w2"][e]).then_inc(weights_in[e % 2], 16)

            load_weights(0)
            load_weights(1)
            pool.memset(zeros[:, :], 0.0).then_inc(carried, 1)
            pool.wait_ge(carried, 1)
            pool.wait_ge(plan_step, 2)
            for e in range(E):
                pool.indirect_dma_start(hs_dram[:, :], bass.IndirectOffsetOnAxis(ap=pad_at[:, e:e + 1], axis=0),
                                        zeros[:, :], None).then_inc(padded, 16)

            for e in range(E):
                pool.wait_ge(weights_in[e % 2], 2 * 16 * (e // 2 + 1))
                pool.memset(ticks[:, e:e + 1], 0.0).then_inc(weights_ready, 1)
                if e + 2 < E:
                    load_weights(e + 2)
            pool.wait_ge(padded, 16 * E)
            for q in range(2):
                landed(pool, y_stored, NJ - 2 + q, q)

            def gather(b, q):
                pool.wait_ge(at_ready, b + 1)
                pool.wait_ge(carried, b + 1)
                pool.tensor_tensor(ticks[:, 0:1], table("row"), table("row"), ALU.add).then_inc(carried, 1)
                for i in range(2):
                    for tile in range(TB):
                        pool.indirect_dma_start(yback[:, q, i, tile], None, ys_dram[:, :],
                                                bass.IndirectOffsetOnAxis(ap=at[:, q, i, tile:tile + 1], axis=0)) \
                            .then_inc(gathered[q], 16)

            gather(0, 0)
            gather(1, 1)
            with pool.Fori(0, (B - 2) // 2) as i:
                for q in range(2):
                    gather(2 * i + q + 2, q)
            for q in range(2):
                landed(pool, gathered, B - 2 + q, q, 2 * TB * 16)

        @block.tensor
        def _(pe):
            ident = table("ident")

            def step(j, q, tile_here=True, tile_before=True):
                m, r = j - 1, 1 - q
                if tile_here:
                    landed(pe, h_in, j, q)
                    for k in range(KD):
                        last = pe.transpose(psH[:, k * P:(k + 1) * P], hin[:, q, k * P:(k + 1) * P], ident)
                    last.then_inc(hT_ps, 1)
                if tile_before:
                    pe.wait_ge(inner_sb, m + 1)
                    for c in range(NC):
                        last = pe.transpose(psT[:, c * P:(c + 1) * P], inner[:, r, c * P:(c + 1) * P], ident)
                    last.then_inc(innerT_ps, 1)
                if tile_here:
                    e = pe.value_load(plan[0:1, 0, bass.ds(j, 1)], min_val=0, max_val=E - 1)
                    pe.wait_ge(weights_ready, e + 1)
                    pe.wait_ge(hT_sb, j + 1)
                    for g in range(2):
                        for k in range(KD):
                            last = pe.matmul(gu[:, q, g], hT[:, q, k],
                                             w13[:, bass.ds(e, 1), k, g * FF:(g + 1) * FF].rearrange("p o n -> p (o n)"),
                                             start=(k == 0), stop=(k == KD - 1))
                        last.then_inc(gu_ps, 1)
                if tile_before:
                    e = pe.value_load(plan[0:1, 0, bass.ds(m, 1)], min_val=0, max_val=E - 1)
                    pe.wait_ge(innerT_sb, m + 1)
                    if not isinstance(m, int) or m >= 2:
                        pe.wait_ge(e_y_sb, m - 1)
                    for c in range(NC):
                        last = pe.matmul(psY[:, r, 0:D], innerT[:, r, c],
                                         w2[:, bass.ds(e, 1), c, :].rearrange("p o n -> p (o n)"), start=(c == 0), stop=(c == NC - 1))
                    last.then_inc(e_y_ps, 1)

            pe.wait_ge(plan_step, N_TILES)
            step(0, 0, tile_before=False)
            step(1, 1)
            step(2, 0)
            with pe.Fori(0, (NJ - 4) // 2) as i:
                step(2 * i + 3, 1)
                step(2 * i + 4, 0)
            step(NJ - 1, 1)
            step(NJ, 0, tile_here=False)

        @block.scalar
        def _(act):
            def step(j, q, tile_here=True, tile_before=True):
                m, r = j - 1, 1 - q
                if tile_here:
                    act.wait_ge(hT_ps, j + 1)
                    act.activation(hT[:, q], psH[:, 0:D].rearrange("p (k c) -> p k c", k=KD), ACT.Copy).then_inc(hT_sb, 1)
                if tile_before:
                    act.wait_ge(innerT_ps, m + 1)
                    act.activation(innerT[:, r], psT[:, :].rearrange("p (k c) -> p k c", k=NC), ACT.Copy).then_inc(innerT_sb, 1)
                if tile_here:
                    act.wait_ge(gu_ps, 2 * j + 1)
                    act.activation(th[:, q], gu[:, q, 0], ACT.Tanh, scale=0.5).then_inc(tanh, 1)
                if tile_before:
                    act.wait_ge(e_y_ps, m + 1)
                    if not isinstance(m, int) or m >= 2:
                        landed(act, y_stored, m - 2, r)
                    act.activation(y[:, r], psY[:, r, 0:D], ACT.Copy).then_inc(e_y_sb, 1)

            step(0, 0, tile_before=False)
            step(1, 1)
            step(2, 0)
            with act.Fori(0, (NJ - 4) // 2) as i:
                step(2 * i + 3, 1)
                step(2 * i + 4, 0)
            step(NJ - 1, 1)
            step(NJ, 0, tile_here=False)

        @block.vector
        def _(dve):
            done = [0]

            def plan_link(ins):
                done[0] += 1
                ins.then_inc(plan_step, 1)
                dve.wait_ge(plan_step, done[0])

            plan_link(dve.tensor_scalar(padf[:, :], next_row[:, :], table("row"), None, ALU.add))
            plan_link(dve.tensor_copy(pad_at[:, :], padf[:, :]))
            cnt, tiles, end, start, base, shift, jump = (e8[:, i] for i in range(7))
            first_row = table("first_row")
            plan_link(dve.tensor_tensor(cnt, next_row[:, :], first_row, ALU.subtract))
            plan_link(dve.tensor_scalar(tiles, cnt, 1.0 / P, (P - 1.0) / P - 0.5 + 0.5 / P, ALU.mult, ALU.add))
            plan_link(dve.tensor_scalar(tiles, tiles, MAGIC, None, ALU.add))
            plan_link(dve.tensor_scalar(tiles, tiles, -MAGIC, None, ALU.add))
            src = tiles
            for i, dst in ((1, end), (2, start), (4, end)):
                dve.tensor_copy(dst[:, 0:i], src[:, 0:i])
                plan_link(dve.tensor_tensor(dst[:, i:E], src[:, i:E], src[:, 0:E - i], ALU.add))
                src = dst
            plan_link(dve.tensor_tensor(start, end, tiles, ALU.subtract))
            plan_link(dve.scalar_tensor_tensor(shift, start, float(P), first_row, ALU.mult, ALU.subtract))
            dve.tensor_copy(jump[:, 0:1], shift[:, 0:1])
            dve.tensor_tensor(jump[:, 1:E], shift[:, 1:E], shift[:, 0:E - 1], ALU.subtract)
            tiles_j = table("tiles")[0:1].unsqueeze(2).broadcast_to([1, NJ, E])
            wide = lambda v: v[0:1].unsqueeze(1).broadcast_to([1, NJ, E])
            dve.tensor_tensor(now[:, :, :], tiles_j, wide(start), ALU.is_ge)
            dve.tensor_tensor(upto_e[:, :, :], tiles_j, wide(end), ALU.is_ge)
            plan_link(dve.scalar_tensor_tensor(val[:, :, :], tiles_j, float(P), wide(shift), ALU.mult, ALU.subtract))
            plan_link(dve.tensor_tensor(inside[:, :, :], now[:, :, :], upto_e[:, :, :], ALU.subtract))
            dve.tensor_tensor(val[:, :, :], val[:, :, :], inside[:, :, :], ALU.mult)
            plan_link(dve.tensor_tensor(now[:, :, :], inside[:, :, :], wide(table("expert")), ALU.mult))
            dve.tensor_reduce(f[:, 0], now[:, :, :], AX_X, ALU.add)
            plan_link(dve.tensor_reduce(f[:, 1], val[:, :, :], AX_X, ALU.add))
            plan_link(dve.tensor_copy(plan[:, :, :], f[:, :, :]))
            assert done[0] == N_TILES, done
            flat = pos[:, :, :].rearrange("p t i -> p (t i)")
            pairs = lambda v: v.unsqueeze(1).broadcast_to([P, NT * 2, E])
            plan_link(dve.tensor_tensor(past[:, :, :], flat.unsqueeze(2).broadcast_to([P, NT * 2, E]), pairs(first_row),
                                        ALU.is_ge))
            plan_link(dve.tensor_tensor(past[:, :, :], past[:, :, :], pairs(jump), ALU.mult))
            out_flat = out_at[:, :, :].rearrange("p t i -> p (t i)")
            plan_link(dve.tensor_reduce(out_flat, past[:, :, :], AX_X, ALU.add))
            plan_link(dve.tensor_tensor(out_flat, out_flat, flat, ALU.add))

            def tile(j, q):
                dve.wait_ge(tanh, j + 1)
                dve.scalar_tensor_tensor(gated[:, q], th[:, q], 1.0, gu[:, q, 0], ALU.add, ALU.mult).then_inc(gated_done, 1)
                dve.wait_ge(gated_done, j + 1)
                dve.wait_ge(gu_ps, 2 * j + 2)
                if not isinstance(j, int) or j >= 2:
                    dve.wait_ge(innerT_ps, j - 1)
                dve.scalar_tensor_tensor(inner[:, q], gated[:, q], 0.5, gu[:, q, 1], ALU.mult, ALU.mult).then_inc(inner_sb, 1)

            tile(0, 0)
            tile(1, 1)
            with dve.Fori(0, (NJ - 2) // 2) as i:
                tile(2 * i + 2, 0)
                tile(2 * i + 3, 1)

            def copy_at(b, q):
                if not isinstance(b, int):
                    landed(dve, gathered, b - 2, q, 2 * TB * 16)
                dve.tensor_copy(gate[:, q].rearrange("p i t -> p t i"), gates[:, bass.ds(b * TB, TB), :])
                dve.tensor_copy(at[:, q].rearrange("p i t -> p t i"), out_at[:, bass.ds(b * TB, TB), :]).then_inc(at_ready, 1)

            def combine(b, q):
                landed(dve, gathered, b, q, 2 * TB * 16)
                dve.wait_ge(at_ready, b + 1)
                for i in range(2):
                    for t in range(TB):
                        row = back[:, bass.ds(b * TB + t, 1), :].rearrange("p o c -> p (o c)")
                        ins = dve.scalar_tensor_tensor(row, yback[:, q, i, t], gate[:, q, i, t:t + 1], row, ALU.mult, ALU.add)
                    ins.then_inc(summed, 1)
                    dve.wait_ge(summed, 2 * b + 1 + i)

            dve.wait_ge(x_back, 16 * B)
            copy_at(0, 0)
            copy_at(1, 1)
            with dve.Fori(0, (B - 2) // 2) as i:
                for q in range(2):
                    combine(2 * i + q, q)
                    copy_at(2 * i + q + 2, q)
            for q in range(2):
                combine(B - 2 + q, q)


N_FIRST = 4
N_PHASES = 42
NORM_PHASES = (0, 7, 17, 20, 28, 38)
QKV_PHASE = 3
CTX_PHASE = 5
BIAS_PHASES = (9, 30)
SOFTMAX_PHASES = (11, 32)
ROT_PHASE = 21
QP_PHASE = 23
AHEAD = {"TensorE": {38: 1, 39: 2, 40: 1}, "VectorE": {38: 1, 39: 1, 40: 2},
         "ScalarE": {38: 1, 39: 2, 40: 1}, "Pool": {38: 1, 39: 1, 40: 2}}
STEP = "step"
JOINED = {"TensorE": (8, 13, 28, 29, 30), "VectorE": (6, 7, 13, 27, 28), "ScalarE": (11, 13, 28, 29, 30, 32), "Pool": (7, 8, 9, 13)}
N_POOL = 8 + LANES * (2 + NCK)
N_DVE_INIT = 13


def arrays_of(i):
    i = {k: np.asarray(v) for k, v in i.items()}
    mats = [i["L0_attn_Wq"], i["L0_attn_Wk"], i["L0_attn_Wv"], i["L0_attn_Wo"],
            i["L0_xattn_Wq"], i["L0_xattn_Wk"], i["L0_xattn_Wv"], i["L0_xattn_Wo"],
            i["L1_attn_Wq"].T, i["L1_attn_Wk"].T, i["L1_attn_Wv"].T, i["L1_attn_Wo"].T,
            i["L1_xattn_Wq"].T, i["L1_xattn_Wk"].T, i["L1_xattn_Wv"].T, i["L1_xattn_Wo"].T]
    rows_first = lambda m: m.reshape(-1, P, m.shape[-1]).transpose(1, 0, 2)
    o = {
        "x": i["x"],
        "ctxT": i["ctx_1024"].reshape(B, SC, KD, P).transpose(0, 3, 2, 1),
        "mask": i["mask_1x1xSxS2_if1"].reshape(S, SC),
        "proj": np.stack([rows_first(m) for m in mats], axis=1),
        "router": rows_first(i["L1_ffn_router_w"].T),
        "bo": np.stack([i["L0_xattn_bo"], i["L1_xattn_bo"]]),
        "cols": np.stack([i[n].reshape(KD, P).T for n in ("L0_xattn_bq", "L0_xattn_bk", "L1_xattn_bq", "L1_xattn_bk",
                                                                          "L0_xattn_bv", "L1_xattn_bv")], axis=1),
        "fbias": i["L0_ffn_bias"],
        "wscale": i["L0_ffn_weight_scale"],
        "packed": i["L0_ffn_packed_weight"].reshape(64, D),
        "w13": i["L1_ffn_w13"].reshape(E, KD, P, 2 * FF).transpose(0, 2, 1, 3),
        "w2": i["L1_ffn_w2"].reshape(E, FF // P, P, D).transpose(0, 2, 1, 3),
        "tables": np.concatenate(list(shape_tables().values()), axis=1),
    }
    return {k: np.ascontiguousarray(v) for k, v in o.items()}


def kernel(**inputs):
    import concourse.bacc as _bacc
    from concourse.bass_utils import run_bass_kernel_spmd as _run

    arrays = {f"in_{k}": v for k, v in arrays_of(inputs).items()}
    nc = _bacc.Bacc("TRN2", target_bir_lowering=False, num_devices=1)
    aps = {k[3:]: nc.dram_tensor(k, v.shape, mybir.dt.from_np(v.dtype), kind="ExternalInput").ap() for k, v in arrays.items()}
    out = nc.dram_tensor("out", (B, S, D), F32, kind="ExternalOutput").ap()
    mega_kernel(nc, aps, out)
    r = _run(nc, [arrays], core_ids=[0])
    return r.results[0]["out"]
```
